# Optimizing a Trainium2 kernel written in Bass

```python
import numpy as np
import jax
import jax.numpy as jnp

def _softmax(x, axis=-1):
    return jax.nn.softmax(x, axis=axis)

def _gelu(x):
    return jax.nn.gelu(x, approximate=True)

def _silu(x):
    return jax.nn.silu(x)

def _sigmoid(x):
    return jax.nn.sigmoid(x)

def _layernorm(x, axis=-1, eps=1e-05):
    m = jnp.mean(x, axis=axis, keepdims=True)
    v = jnp.var(x, axis=axis, keepdims=True)
    return (x - m) / jnp.sqrt(v + eps)

def _scatter_add(tgt, idx, src, axis=0):
    return tgt.at[idx].add(src)

def _segment_sum(src, seg, n):
    return jax.ops.segment_sum(src, seg, n)
kernel_name = 'mk_seq_postln_d2_jaxref_r4_7f2bab'

def setup_inputs(seed: int=0):
    np.random.seed(seed)
    _w = jnp.asarray

    def _L0_attn_setup():
        import jax, jax.numpy as jnp
        import numpy as np
        import math
        DIM = 256
        NUM_HEADS = 16
        HEAD_DIM = DIM // NUM_HEADS
        WINDOW = 64

        def _apply_rotary(x, cos, sin):
            d = x.shape[-1] // 2
            x1, x2 = (x[..., :d], x[..., d:])
            return jnp.concatenate([x1 * cos - x2 * sin, x2 * cos + x1 * sin], axis=-1)
        key = jax.random.key(seed)
        k1, k2, k3 = jax.random.split(key, 3)
        B, T = (2, 512)
        x = jax.random.normal(k1, (B, T, DIM), dtype=jnp.float32)
        w_qkv = jax.random.normal(k2, (3 * DIM, DIM), dtype=jnp.float32) * (1.0 / math.sqrt(DIM))
        w_out = jax.random.normal(k3, (DIM, DIM), dtype=jnp.float32) * (1.0 / math.sqrt(DIM))
        return {'x': x, 'w_qkv': w_qkv, 'w_out': w_out}
    _L0_attn_in = _L0_attn_setup()

    def _L0_ffn_setup():
        import jax, jax.numpy as jnp
        import numpy as np
        DIM = 256

        def _reference_tuple_inner(x, W_r, W_k, W_v, mu_r, mu_k):
            B, T, C = x.shape
            x_prev = jnp.concatenate([jnp.zeros((B, 1, C), x.dtype), x[:, :-1, :]], axis=1)
            xr = mu_r * x + (1.0 - mu_r) * x_prev
            xk = mu_k * x + (1.0 - mu_k) * x_prev
            r = jax.nn.sigmoid(jnp.einsum('btc,dc->btd', xr, W_r))
            k = jnp.einsum('btc,dc->btd', xk, W_k)
            k_act = jnp.square(jax.nn.relu(k))
            out = r * jnp.einsum('btc,dc->btd', k_act, W_v)
            new_state = x[:, -1, :]
            return (out, new_state)
        key = jax.random.key(seed)
        ks = jax.random.split(key, 6)
        B, T, C = (8, 512, DIM)
        x = jax.random.normal(ks[0], (B, T, C), dtype=jnp.float32)
        s = 1.0 / np.sqrt(C)
        W_r = jax.random.uniform(ks[1], (C, C), jnp.float32, -s, s)
        W_k = jax.random.uniform(ks[2], (C, C), jnp.float32, -s, s)
        W_v = jax.random.uniform(ks[3], (C, C), jnp.float32, -s, s)
        mu_r = jax.random.uniform(ks[4], (C,), jnp.float32)
        mu_k = jax.random.uniform(ks[5], (C,), jnp.float32)
        return {'x': x, 'W_r': W_r, 'W_k': W_k, 'W_v': W_v, 'mu_r': mu_r, 'mu_k': mu_k}
    _L0_ffn_in = _L0_ffn_setup()

    def _L1_attn_setup():
        import jax, jax.numpy as jnp
        import numpy as np
        DIM = 256
        HEADS = 16
        HEAD_DIM = DIM // HEADS
        FEAT = 64
        B, N = (4, 1024)
        key = jax.random.key(seed)
        ks = jax.random.split(key, 10)
        s = 1.0 / np.sqrt(DIM)
        return {'x': jax.random.normal(ks[0], (B, N, DIM), jnp.float32), 'Wq': jax.random.normal(ks[1], (DIM, DIM), jnp.float32) * s, 'bq': jnp.zeros((DIM,), jnp.float32), 'Wk': jax.random.normal(ks[2], (DIM, DIM), jnp.float32) * s, 'bk': jnp.zeros((DIM,), jnp.float32), 'Wv': jax.random.normal(ks[3], (DIM, DIM), jnp.float32) * s, 'bv': jnp.zeros((DIM,), jnp.float32), 'Wo': jax.random.normal(ks[4], (DIM, DIM), jnp.float32) * s, 'bo': jnp.zeros((DIM,), jnp.float32), 'random_features': jax.random.normal(ks[5], (HEAD_DIM, FEAT), jnp.float32) / np.sqrt(FEAT)}
    _L1_attn_in = _L1_attn_setup()

    def _L1_ffn_setup():
        import jax, jax.numpy as jnp
        import numpy as np
        import math
        B, T, D, H, E, TOPK, CAPF = (4, 512, 256, 16, 8, 2, 2.0)
        HD = D // H

        def layernorm(x, g, b, eps=1e-05):
            m = jnp.mean(x, -1, keepdims=True)
            v = jnp.mean(jnp.square(x - m), -1, keepdims=True)
            return (x - m) * jax.lax.rsqrt(v + eps) * g + b

        def block_forward(x, ln1_g, ln1_b, Wqkv, Wproj, ln2_g, ln2_b, Wgate, W1, b1, W2, b2):
            Bb, Tt, d = x.shape
            hd = HD
            half = hd // 2
            h = layernorm(x, ln1_g, ln1_b)
            qkv = (h @ Wqkv).reshape(Bb, Tt, H, 3 * hd)
            q, k, v = (qkv[..., :hd], qkv[..., hd:2 * hd], qkv[..., 2 * hd:])
            inv_freq = 1.0 / 10000.0 ** (jnp.arange(0, hd, 2, dtype=jnp.float32) / hd)
            ang = jnp.arange(Tt, dtype=jnp.float32)[:, None] * inv_freq
            sin = jnp.sin(ang)[None, :, None, :].astype(x.dtype)
            cos = jnp.cos(ang)[None, :, None, :].astype(x.dtype)

            def rope(t):
                t1, t2 = (t[..., :half], t[..., half:])
                return jnp.concatenate([t1 * cos - t2 * sin, t1 * sin + t2 * cos], -1)
            q, k = (rope(q), rope(k))
            scores = jnp.einsum('bqhd,bkhd->bhqk', q, k) / math.sqrt(hd)
            causal = jnp.tril(jnp.ones((Tt, Tt), dtype=bool))
            scores = jnp.where(causal, scores, jnp.asarray(-1000000000.0, scores.dtype))
            probs = jax.nn.softmax(scores, axis=-1)
            attn = jnp.einsum('bhqk,bkhd->bqhd', probs, v).reshape(Bb, Tt, d) @ Wproj
            x = x + attn
            h2 = layernorm(x, ln2_g, ln2_b)
            flat = h2.reshape(-1, d)
            N = flat.shape[0]
            capacity = int(math.ceil(CAPF * N / E))
            gates = jax.nn.softmax((flat @ Wgate).astype(jnp.float32), -1).astype(flat.dtype)
            _, top_inds = jax.lax.top_k(gates, TOPK)
            mask = jnp.zeros((N, E), dtype=bool).at[jnp.arange(N)[:, None], top_inds].set(True)
            pos = jnp.cumsum(mask.astype(jnp.int32), axis=0) * mask - 1
            keep = (pos < capacity) & mask
            t_flat = jnp.repeat(jnp.arange(N), TOPK)
            e_flat = top_inds.reshape(-1)
            p = pos[t_flat, e_flat]
            kp = keep[t_flat, e_flat]
            p_eff = jnp.where(kp, p, capacity)
            exp_in = jnp.zeros((E, capacity, d), flat.dtype).at[e_flat, p_eff].set(flat[t_flat], mode='drop')
            hmid = jax.nn.gelu(jnp.einsum('ecd,edf->ecf', exp_in, W1) + b1[:, None, :], approximate=False)
            exp_out = jnp.einsum('ecf,efd->ecd', hmid, W2) + b2[:, None, :]
            gate = gates[t_flat, e_flat] * kp.astype(flat.dtype)
            p_g = jnp.minimum(p_eff, capacity - 1)
            moe = jnp.zeros((N, d), flat.dtype).at[t_flat].add(exp_out[e_flat, p_g] * gate[:, None])
            return x + moe.reshape(Bb, Tt, d)
        key = jax.random.key(seed)
        ks = jax.random.split(key, 8)
        s = 0.02
        return {'x': jax.random.normal(ks[0], (B, T, D), jnp.float32), 'ln1_g': jnp.ones((D,), jnp.float32), 'ln1_b': jnp.zeros((D,), jnp.float32), 'Wqkv': jax.random.normal(ks[1], (D, 3 * D), jnp.float32) * s, 'Wproj': jax.random.normal(ks[2], (D, D), jnp.float32) * s, 'ln2_g': jnp.ones((D,), jnp.float32), 'ln2_b': jnp.zeros((D,), jnp.float32), 'Wgate': jax.random.normal(ks[3], (D, E), jnp.float32) * s, 'W1': jax.random.normal(ks[4], (E, D, 4 * D), jnp.float32) * s, 'b1': jnp.zeros((E, 4 * D), jnp.float32), 'W2': jax.random.normal(ks[5], (E, 4 * D, D), jnp.float32) * s, 'b2': jnp.zeros((E, D), jnp.float32)}
    _L1_ffn_in = _L1_ffn_setup()
    _d = {'L0_attn_x': _L0_attn_in['x'], 'L0_attn_w_qkv': _L0_attn_in['w_qkv'], 'L0_attn_w_out': _L0_attn_in['w_out'], 'L0_ffn_W_r': _L0_ffn_in['W_r'], 'L0_ffn_W_k': _L0_ffn_in['W_k'], 'L0_ffn_W_v': _L0_ffn_in['W_v'], 'L0_ffn_mu_r': _L0_ffn_in['mu_r'], 'L0_ffn_mu_k': _L0_ffn_in['mu_k'], 'L1_attn_Wq': _L1_attn_in['Wq'], 'L1_attn_bq': _L1_attn_in['bq'], 'L1_attn_Wk': _L1_attn_in['Wk'], 'L1_attn_bk': _L1_attn_in['bk'], 'L1_attn_Wv': _L1_attn_in['Wv'], 'L1_attn_bv': _L1_attn_in['bv'], 'L1_attn_Wo': _L1_attn_in['Wo'], 'L1_attn_bo': _L1_attn_in['bo'], 'L1_attn_random_features': _L1_attn_in['random_features'], 'L1_ffn_ln1_g': _L1_ffn_in['ln1_g'], 'L1_ffn_ln1_b': _L1_ffn_in['ln1_b'], 'L1_ffn_Wqkv': _L1_ffn_in['Wqkv'], 'L1_ffn_Wproj': _L1_ffn_in['Wproj'], 'L1_ffn_ln2_g': _L1_ffn_in['ln2_g'], 'L1_ffn_ln2_b': _L1_ffn_in['ln2_b'], 'L1_ffn_Wgate': _L1_ffn_in['Wgate'], 'L1_ffn_W1': _L1_ffn_in['W1'], 'L1_ffn_b1': _L1_ffn_in['b1'], 'L1_ffn_W2': _L1_ffn_in['W2'], 'L1_ffn_b2': _L1_ffn_in['b2']}
    _x0 = _d['L0_attn_x']
    _d['L0_attn_x'] = jax.random.normal(jax.random.fold_in(jax.random.key(seed), 1), (4, 1024, 256), dtype=_x0.dtype)
    del _x0
    return _d

def reference(L0_attn_x, L0_attn_w_qkv, L0_attn_w_out, L0_ffn_W_r, L0_ffn_W_k, L0_ffn_W_v, L0_ffn_mu_r, L0_ffn_mu_k, L1_attn_Wq, L1_attn_bq, L1_attn_Wk, L1_attn_bk, L1_attn_Wv, L1_attn_bv, L1_attn_Wo, L1_attn_bo, L1_attn_random_features, L1_ffn_ln1_g, L1_ffn_ln1_b, L1_ffn_Wqkv, L1_ffn_Wproj, L1_ffn_ln2_g, L1_ffn_ln2_b, L1_ffn_Wgate, L1_ffn_W1, L1_ffn_b1, L1_ffn_W2, L1_ffn_b2):

    def _L0_attn_ref(x, w_qkv, w_out):
        import jax, jax.numpy as jnp
        import numpy as np
        import math
        DIM = 256
        NUM_HEADS = 16
        HEAD_DIM = DIM // NUM_HEADS
        WINDOW = 64

        def _apply_rotary(x, cos, sin):
            d = x.shape[-1] // 2
            x1, x2 = (x[..., :d], x[..., d:])
            return jnp.concatenate([x1 * cos - x2 * sin, x2 * cos + x1 * sin], axis=-1)
        B, T, C = x.shape
        H, Dh = (NUM_HEADS, HEAD_DIM)
        qkv = (x @ w_qkv.T).reshape(B, T, 3, H, Dh)
        q, k, v = (qkv[:, :, 0], qkv[:, :, 1], qkv[:, :, 2])
        q = jnp.transpose(q, (0, 2, 1, 3))
        k = jnp.transpose(k, (0, 2, 1, 3))
        v = jnp.transpose(v, (0, 2, 1, 3))
        inv_freq = 1.0 / 10000.0 ** (jnp.arange(0, Dh, 2, dtype=jnp.float32) / Dh)
        t = jnp.arange(T, dtype=jnp.float32)
        freqs = jnp.einsum('i,j->ij', t, inv_freq)
        cos, sin = (jnp.cos(freqs), jnp.sin(freqs))
        q = _apply_rotary(q, cos, sin)
        k = _apply_rotary(k, cos, sin)
        scale = 1.0 / math.sqrt(Dh)
        attn = jnp.einsum('bhqd,bhkd->bhqk', q, k) * scale
        i = jnp.arange(T)[:, None]
        j = jnp.arange(T)[None, :]
        allowed = (j <= i) & (i - j < WINDOW)
        attn = jnp.where(allowed, attn, -jnp.inf)
        attn = jax.nn.softmax(attn, axis=-1)
        out = jnp.einsum('bhqk,bhkd->bhqd', attn, v)
        out = jnp.transpose(out, (0, 2, 1, 3)).reshape(B, T, C)
        return out @ w_out.T

    def _L0_ffn_ref(x, W_r, W_k, W_v, mu_r, mu_k):
        import jax, jax.numpy as jnp
        import numpy as np
        DIM = 256

        def _reference_tuple_inner(x, W_r, W_k, W_v, mu_r, mu_k):
            B, T, C = x.shape
            x_prev = jnp.concatenate([jnp.zeros((B, 1, C), x.dtype), x[:, :-1, :]], axis=1)
            xr = mu_r * x + (1.0 - mu_r) * x_prev
            xk = mu_k * x + (1.0 - mu_k) * x_prev
            r = jax.nn.sigmoid(jnp.einsum('btc,dc->btd', xr, W_r))
            k = jnp.einsum('btc,dc->btd', xk, W_k)
            k_act = jnp.square(jax.nn.relu(k))
            out = r * jnp.einsum('btc,dc->btd', k_act, W_v)
            new_state = x[:, -1, :]
            return (out, new_state)
        return _reference_tuple_inner(x, W_r, W_k, W_v, mu_r, mu_k)[0]

    def _L1_attn_ref(x, Wq, bq, Wk, bk, Wv, bv, Wo, bo, random_features):
        import jax, jax.numpy as jnp
        import numpy as np
        DIM = 256
        HEADS = 16
        HEAD_DIM = DIM // HEADS
        FEAT = 64
        B, N = (4, 1024)
        Bsz, Nlen, C = x.shape
        q = (x @ Wq + bq).reshape(Bsz, Nlen, HEADS, HEAD_DIM)
        k = (x @ Wk + bk).reshape(Bsz, Nlen, HEADS, HEAD_DIM)
        v = (x @ Wv + bv).reshape(Bsz, Nlen, HEADS, HEAD_DIM)
        q = jax.nn.elu(q) + 1.0
        k = jax.nn.elu(k) + 1.0
        q = jnp.einsum('bnhd,df->bnhf', q, random_features)
        k = jnp.einsum('bnhd,df->bnhf', k, random_features)
        kv = jnp.einsum('bnhf,bnhd->bhfd', k, v)
        out = jnp.einsum('bnhf,bhfd->bnhd', q, kv)
        out = out.reshape(Bsz, Nlen, C)
        return out @ Wo + bo

    def _L1_ffn_ref(x, ln1_g, ln1_b, Wqkv, Wproj, ln2_g, ln2_b, Wgate, W1, b1, W2, b2):
        import jax, jax.numpy as jnp
        import numpy as np
        import math
        B, T, D, H, E, TOPK, CAPF = (4, 512, 256, 16, 8, 2, 2.0)
        HD = D // H

        def layernorm(x, g, b, eps=1e-05):
            m = jnp.mean(x, -1, keepdims=True)
            v = jnp.mean(jnp.square(x - m), -1, keepdims=True)
            return (x - m) * jax.lax.rsqrt(v + eps) * g + b

        def block_forward(x, ln1_g, ln1_b, Wqkv, Wproj, ln2_g, ln2_b, Wgate, W1, b1, W2, b2):
            Bb, Tt, d = x.shape
            hd = HD
            half = hd // 2
            h = layernorm(x, ln1_g, ln1_b)
            qkv = (h @ Wqkv).reshape(Bb, Tt, H, 3 * hd)
            q, k, v = (qkv[..., :hd], qkv[..., hd:2 * hd], qkv[..., 2 * hd:])
            inv_freq = 1.0 / 10000.0 ** (jnp.arange(0, hd, 2, dtype=jnp.float32) / hd)
            ang = jnp.arange(Tt, dtype=jnp.float32)[:, None] * inv_freq
            sin = jnp.sin(ang)[None, :, None, :].astype(x.dtype)
            cos = jnp.cos(ang)[None, :, None, :].astype(x.dtype)

            def rope(t):
                t1, t2 = (t[..., :half], t[..., half:])
                return jnp.concatenate([t1 * cos - t2 * sin, t1 * sin + t2 * cos], -1)
            q, k = (rope(q), rope(k))
            scores = jnp.einsum('bqhd,bkhd->bhqk', q, k) / math.sqrt(hd)
            causal = jnp.tril(jnp.ones((Tt, Tt), dtype=bool))
            scores = jnp.where(causal, scores, jnp.asarray(-1000000000.0, scores.dtype))
            probs = jax.nn.softmax(scores, axis=-1)
            attn = jnp.einsum('bhqk,bkhd->bqhd', probs, v).reshape(Bb, Tt, d) @ Wproj
            x = x + attn
            h2 = layernorm(x, ln2_g, ln2_b)
            flat = h2.reshape(-1, d)
            N = flat.shape[0]
            capacity = int(math.ceil(CAPF * N / E))
            gates = jax.nn.softmax((flat @ Wgate).astype(jnp.float32), -1).astype(flat.dtype)
            _, top_inds = jax.lax.top_k(gates, TOPK)
            mask = jnp.zeros((N, E), dtype=bool).at[jnp.arange(N)[:, None], top_inds].set(True)
            pos = jnp.cumsum(mask.astype(jnp.int32), axis=0) * mask - 1
            keep = (pos < capacity) & mask
            t_flat = jnp.repeat(jnp.arange(N), TOPK)
            e_flat = top_inds.reshape(-1)
            p = pos[t_flat, e_flat]
            kp = keep[t_flat, e_flat]
            p_eff = jnp.where(kp, p, capacity)
            exp_in = jnp.zeros((E, capacity, d), flat.dtype).at[e_flat, p_eff].set(flat[t_flat], mode='drop')
            hmid = jax.nn.gelu(jnp.einsum('ecd,edf->ecf', exp_in, W1) + b1[:, None, :], approximate=False)
            exp_out = jnp.einsum('ecf,efd->ecd', hmid, W2) + b2[:, None, :]
            gate = gates[t_flat, e_flat] * kp.astype(flat.dtype)
            p_g = jnp.minimum(p_eff, capacity - 1)
            moe = jnp.zeros((N, d), flat.dtype).at[t_flat].add(exp_out[e_flat, p_g] * gate[:, None])
            return x + moe.reshape(Bb, Tt, d)
        return block_forward(x, ln1_g, ln1_b, Wqkv, Wproj, ln2_g, ln2_b, Wgate, W1, b1, W2, b2)
    x = L0_attn_x
    x = _layernorm(x + _L0_attn_ref(x, L0_attn_w_qkv, L0_attn_w_out), axis=-1)
    x = _layernorm(x + _L0_ffn_ref(x, L0_ffn_W_r, L0_ffn_W_k, L0_ffn_W_v, L0_ffn_mu_r, L0_ffn_mu_k), axis=-1)
    x = _layernorm(x + _L1_attn_ref(x, L1_attn_Wq, L1_attn_bq, L1_attn_Wk, L1_attn_bk, L1_attn_Wv, L1_attn_bv, L1_attn_Wo, L1_attn_bo, L1_attn_random_features), axis=-1)
    x = _layernorm(x + _L1_ffn_ref(x, L1_ffn_ln1_g, L1_ffn_ln1_b, L1_ffn_Wqkv, L1_ffn_Wproj, L1_ffn_ln2_g, L1_ffn_ln2_b, L1_ffn_Wgate, L1_ffn_W1, L1_ffn_b1, L1_ffn_W2, L1_ffn_b2), axis=-1)
    return x

_drawn_inputs = setup_inputs


def setup_inputs(seed=0):
    import zlib

    import numpy as np

    out = dict(_drawn_inputs(seed))
    spreads = {'L1_attn_bq': (0.0, 0.368),
     'L1_attn_bk': (0.0, 0.374),
     'L1_attn_bv': (0.0, 0.1),
     'L1_attn_bo': (0.0, 0.8),
     'L1_ffn_ln1_g': (1.0, 0.6),
     'L1_ffn_ln1_b': (0.0, 0.8),
     'L1_ffn_ln2_g': (1.0, 0.6),
     'L1_ffn_ln2_b': (0.0, 0.8),
     'L1_ffn_b1': (0.0, 0.8),
     'L1_ffn_b2': (0.0, 0.8)}
    factors = {'L0_ffn_W_r': 6.904,
     'L0_ffn_mu_r': 8.0,
     'L0_ffn_mu_k': 3.642,
     'L1_ffn_Wgate': 4.529,
     'L1_ffn_W1': 5.963,
     'L1_ffn_W2': 5.327}
    for name, (base, spread) in spreads.items():
        noise = np.random.default_rng([zlib.crc32(name.encode()), seed]).standard_normal(out[name].shape)
        drawn = base * np.exp(spread * noise) if base else spread * noise
        out[name] = jnp.asarray(drawn.astype(out[name].dtype))
    for name, factor in factors.items():
        out[name] = (out[name] * factor).astype(out[name].dtype)
    return out
```

```python
from collections import namedtuple
from contextlib import ExitStack

import numpy as np

import concourse.bass as bass
from concourse import mybir

ALU = mybir.AluOpType
ACT = mybir.ActivationFunctionType
AX = mybir.AxisListType
F32 = mybir.dt.float32
BF16 = mybir.dt.bfloat16
U32 = mybir.dt.uint32

P = 128
B, T, D = 4, 1024, 256
NT = T // P
NC = D // P
H, HD = 16, 16
HG = 4
NG = H // HG
WINDOW = 64
HALF = HD // 2
SCALE = HD ** -0.5
SLOTS = 6
KS = SLOTS * HD
KM = KS + 3
WQ = P + WINDOW
E_, F_, TOPK = 8, 1024, 2
N = B * T
CAP = 2 * N // E_
NF = F_ // P
CT = CAP // P
NEG = -2.0 ** 100
EPS = 1e-5
BANK = 512
DROPPED = 65536.0


def named(things):
    return namedtuple("Named", list(things))(*things.values())


def semaphores(nc, ctx, prefix, names):
    made = {n: ctx.enter_context(nc.semaphore(f"{prefix}_{n}")) for n in names.split()}
    return named(dict(made, all=[h for n, h in made.items() if not n.endswith("_gathered")]))


def clear(nc, sems):
    with nc.Block() as block:
        @block.gpsimd
        def _(pool):
            for s in sems.all:
                pool.sem_clear(s)


def dve_chain(dve, sem):
    count = [0]

    def link(ins):
        count[0] += 1
        ins.then_inc(sem, 1)
        dve.wait_ge(sem, count[0])
    return link



class Schedule:

    def __init__(self, windowed):
        self.nm = NT if windowed else NT * HG
        self.ns = NT if windowed else NT * HG
        self.ring = []
        self.ring += [("max", 0, n) for n in range(self.nm)]
        for g in range(NG):
            self.ring += [("exp", g, n) for n in range(self.ns)]
            if g + 1 < NG:
                self.ring += [("max", g + 1, n) for n in range(self.nm)]
            self.ring.append(("out", g, 0))
        self.at = {x: i for i, x in enumerate(self.ring)}
        self.prep = [("proj", 0), ("proj", 1), ("turn", 0), ("turn", 1), ("proj", 2), ("turn", 2),
                     ("turn", 3), ("proj", 3), ("turn", 4), ("turn", 5), ("turn", 6), ("turn", 7)]

    def prep_at(self, n):
        k = len(self.prep)
        return [self.prep[i] for i in range(k) if (i * self.ns) // k == n]

    def slot(self, what):
        return self.at[what] % 2

    def wait_slot(self, eng, what, s):
        i = self.at[what] - 2
        if i < 0:
            return
        kind, g, n = self.ring[i]
        if kind == "max":
            eng.wait_ge(s.max_read, g * self.nm + n + 1)
        elif kind == "exp":
            eng.wait_ge(s.exp_done, g * self.ns + n + 1)
        else:
            eng.wait_ge(s.out_ready, g + 1)


def attention(nc, b, u, s, windowed, x_dram=None):
    plan = Schedule(windowed)
    w_sb = u.wqkv0 if windowed else u.wqkv1

    def spans(first, last):
        cuts = [first] + [c for c in range(BANK, T, BANK) if first < c < last] + [last]
        return list(zip(cuts[:-1], cuts[1:]))

    with nc.Block() as block:
        @block.sync
        def _(sp):
            if x_dram is not None:
                for h in range(2):
                    sp.dma_start(u.src[:, 4 * h:4 * h + 4, :], x_dram[bass.ds(b, 1), BANK * h:BANK * (h + 1), :]
                                 .rearrange("o (t p) d -> p (o t) d", p=P)).then_inc(s.src_in, 16)
            for g in range(NG):
                sp.wait_ge(s.mt_read, g + 1)
                for j in range(3):
                    sp.dma_start(u.qk[g % 2][KS + j:KS + j + 1, 0:HG, :].rearrange("o h (t q) -> o (h t) q", q=P),
                                 u.mrow[32 * j:32 * j + 32, :]).then_inc(s.m_rows, 16)
            sp.wait_ge(s.m_rows, 48 * NG)

        @block.tensor
        def _(pe):
            if x_dram is not None:
                pe.wait_ge(s.src_in, 32)
            for c in range(NC):
                for h in range(2):
                    for t in range(4):
                        i = pe.transpose(u.ring[:, 2 * c + h, P * t:P * t + P],
                                         u.src[:, 4 * h + t, P * c:P * c + P], u.id32[:, :])
                    i.then_inc(s.xt_ready, 1)

            def proj(g, k):
                i = 4 * g + k
                if i:
                    pe.wait_ge(s.pj_read, i)
                else:
                    pe.wait_ge(s.xt_read, 4)
                for t in range(2):
                    for c in range(NC):
                        ins = pe.matmul(u.pj[:, t * 192:t * 192 + 192], u.xt[:, c, P * (2 * k + t):P * (2 * k + t + 1)],
                                        w_sb[:, c, g, :], start=(c == 0), stop=(c == NC - 1))
                ins.then_inc(s.pj_ready, 1)

            def turn(g, t):
                i = 8 * g + t
                if i:
                    pe.wait_ge(s.tr_read, i)
                if g:
                    pe.wait_ge(s.mt_read, g)
                pe.wait_ge(s.stack_ready, 4 * g + t // 2 + 1)
                for h in range(2 * HG):
                    ins = pe.transpose(u.tr[0:KS, h, :], u.stack[(t // 2) % 2][:, t % 2, h, :], u.id16[:, :])
                ins.then_inc(s.tr_ready, 1)

            def step(kind, g, k):
                (proj if kind == "proj" else turn)(g, k)

            def scores_for_max(g, n):
                q = u.qk[g % 2]
                what = ("max", g, n)
                r = u.ring2[plan.slot(what)]
                plan.wait_slot(pe, what, s)
                if n == 0:
                    pe.wait_ge(s.tr_read, 8 * (g + 1))
                if windowed:
                    k0, w = max(0, P * n - WINDOW), min(WQ, P * n + P)
                    for j in range(2):
                        out = r[:, BANK * j:BANK * j + 2 * WQ].rearrange("p (h w) -> p h w", h=2)[:, :, 0:w]
                        pe.matmul(out, u.id16[:, :], u.mask_q[:, :, WQ - w:WQ], start=True, stop=True,
                                  skip_group_check=True)
                        for h in range(2):
                            ins = pe.matmul(out[:, h, :], q[0:KS, 2 * j + h, P * n:P * n + P],
                                            q[0:KS, HG + 2 * j + h, k0:k0 + w], start=False, stop=True,
                                            skip_group_check=True)
                else:
                    t, h = divmod(n, HG)
                    for a, e in spans(0, P * t + P):
                        last = e == P * t + P
                        if last:
                            pe.matmul(r[:, P * t:P * t + P], u.id16[:, :], u.causal_q[:, :], start=True, stop=True,
                                  skip_group_check=True)
                        ins = pe.matmul(r[:, a:e], q[0:KS, h, P * t:P * t + P], q[0:KS, HG + h, a:e],
                                        start=not last, stop=True, skip_group_check=True)
                ins.then_inc(s.max_ready, 1)

            def turn_maxima(g):
                pe.wait_ge(s.tr_read, 8 * (g + 1))
                if g:
                    pe.wait_ge(s.mt_read, g)
                pe.wait_ge(s.m_parts, g + 1)
                pe.transpose(u.tr[0:KS, 0, :], u.mparts[:, :], u.id16[:, :]).then_inc(s.mt_ready, 1)

            def scores_for_exp(g, n):
                q = u.qk[g % 2]
                what = ("exp", g, n)
                r = u.ring2[plan.slot(what)]
                plan.wait_slot(pe, what, s)
                if n == 0:
                    pe.wait_ge(s.m_rows, 48 * (g + 1))
                if windowed:
                    q0, w = P * n, min(WQ, T - P * n)
                    for j in range(2):
                        out = r[:, BANK * j:BANK * j + 2 * WQ].rearrange("p (h w) -> p h w", h=2)[:, :, 0:w]
                        pe.matmul(out, u.id16[:, :], u.mask_k[:, :, 0:w], start=True, stop=True,
                                  skip_group_check=True)
                        for h in range(2):
                            ins = pe.matmul(out[:, h, :], q[0:KM, HG + 2 * j + h, P * n:P * n + P],
                                            q[0:KM, 2 * j + h, q0:q0 + w], start=False, stop=True,
                                            skip_group_check=True)
                else:
                    t, h = divmod(n, HG)
                    for a, e in spans(P * t, T):
                        first = a == P * t
                        if first:
                            pe.matmul(r[:, a:a + P], u.id16[:, :], u.causal_k[:, :], start=True, stop=True,
                                  skip_group_check=True)
                        ins = pe.matmul(r[:, a:e], q[0:KM, HG + h, P * t:P * t + P], q[0:KM, h, a:e],
                                        start=not first, stop=True, skip_group_check=True)
                ins.then_inc(s.exp_ready, 1)

            def values(g, t):
                pe.wait_ge(s.exp_done, g * plan.ns + (t + 1) * plan.ns // NT)
                if t == 0 and g:
                    pe.wait_ge(s.o_read, g)
                last_q = min(T, P * t + WQ) if windowed else T
                for a, e in spans(P * t, last_q):
                    first = (t == 0) if not windowed else a in (0, BANK) and (t == 0 or a > P * t)
                    for h in range(HG):
                        probs = (u.probs[t % 2][:, h, 0:WQ][:, a - P * t:e - P * t] if windowed
                                 else u.probs[t % 2][:, h, a:e])
                        ins = pe.matmul(u.ot[32 * h:32 * h + 32, a:e], u.v[g % 2][:, t, h, :], probs,
                                        start=first, stop=True, tile_position=(0, 32 * h), skip_group_check=True)
                ins.then_inc(s.pv_done, 1)

            def turn_out(g):
                what = ("out", g, 0)
                r = u.ring2[plan.slot(what)]
                plan.wait_slot(pe, what, s)
                pe.wait_ge(s.o_read, g + 1)
                for t in range(NT):
                    ins = pe.transpose(r[:, P * t:P * t + P], u.ot_sb[:, P * t:P * t + P], u.id32[:, :])
                ins.then_inc(s.on_ready, 1)

            for x in plan.prep:
                step(x[0], 0, x[1])
            for n in range(plan.nm):
                scores_for_max(0, n)
            turn_maxima(0)
            per_tile = plan.ns // NT
            for g in range(NG):
                for n in range(plan.ns):
                    scores_for_exp(g, n)
                    if g + 1 < NG:
                        for kind, k in plan.prep_at(n):
                            step(kind, g + 1, k)
                    if n % per_tile == per_tile - 1 and n >= per_tile:
                        values(g, n // per_tile - 1)
                values(g, NT - 1)
                if g + 1 < NG:
                    for n in range(plan.nm):
                        scores_for_max(g + 1, n)
                    turn_maxima(g + 1)
                turn_out(g)

        @block.scalar
        def _(act):
            for c in range(NC):
                for h in range(2):
                    act.wait_ge(s.xt_ready, 2 * c + h + 1)
                    if windowed:
                        act.activation(u.xt[:, c, BANK * h:BANK * h + BANK], u.ring[:, 2 * c + h, :], ACT.Copy
                                       ).then_inc(s.xt_read, 1)
                    else:
                        act.activation(u.xt[:, c, BANK * h:BANK * h + BANK], u.ring[:, 2 * c + h, :], ACT.Identity,
                                       scale=u.ln1g[:, c:c + 1], bias=u.ln1b[:, c:c + 1]).then_inc(s.xt_read, 1)

            for g in range(NG):
                for n in range(plan.ns):
                    t = n * NT // plan.ns
                    act.wait_ge(s.exp_ready, g * plan.ns + n + 1)
                    if g * NT + t >= 2 and n % (plan.ns // NT) == 0:
                        act.wait_ge(s.pv_done, g * NT + t - 1)
                    r = u.ring2[plan.slot(("exp", g, n))]
                    if windowed:
                        w = min(WQ, T - P * n)
                        act.activation(u.probs[t % 2][:, :, 0:w].rearrange("p (j h) w -> p j h w", j=2),
                                       r.rearrange("p (j x) -> p j x", j=2)[:, :, 0:2 * WQ].rearrange(
                                           "p j (h w) -> p j h w", h=2)[:, :, :, 0:w],
                                       ACT.Exp, scale=SCALE).then_inc(s.exp_done, 1)
                    else:
                        act.activation(u.probs[t % 2][:, n % HG, P * t:T], r[:, P * t:T], ACT.Exp, scale=SCALE
                                       ).then_inc(s.exp_done, 1)
                act.wait_ge(s.pv_done, NT * (g + 1))
                if g:
                    act.wait_ge(s.on_ready, g)
                act.activation(u.ot_sb[:, :], u.ot[:, :], ACT.Copy).then_inc(s.o_read, 1)

        @block.vector
        def _(dve):
            link = dve_chain(dve, s.chain)

            def rotate(g, k):
                i = 4 * g + k
                dve.wait_ge(s.pj_ready, i + 1)
                src = u.pj[:, 0:384].rearrange("p (t a) -> p t a", t=2)[:, :, 0:128].rearrange(
                    "p t (h d) -> p t h d", d=HD)
                cos = u.cos[:, 2 * k:2 * k + 2, :].unsqueeze(2).broadcast_to([P, 2, 2 * HG, HD])
                dve.tensor_tensor(u.ra[:, :, :, :], src, cos, ALU.mult)
                for x in range(2):
                    sin = u.sin[:, 2 * k:2 * k + 2, HALF * x:HALF * x + HALF].unsqueeze(2).broadcast_to(
                        [P, 2, 2 * HG, HALF])
                    dve.tensor_tensor(u.rb[:, :, :, HALF * x:HALF * x + HALF],
                                            src[:, :, :, HALF * (1 - x):HALF * (1 - x) + HALF], sin, ALU.mult)
                dve.tensor_copy(u.v[g % 2][:, 2 * k:2 * k + 2, :, 0:HD],
                                u.pj[:, 0:384].rearrange("p (t a h d) -> p t a h d", t=2, a=3, h=HG)[:, :, 2, :, :]
                                ).then_inc(s.pj_read, 1)
                dve.wait_ge(s.pj_read, i + 1)
                if i >= 2:
                    dve.wait_ge(s.stack_ready, i - 1)
                dve.tensor_tensor(u.rot[i % 2][:, :, :, :], u.ra[:, :, :, :], u.rb[:, :, :, :], ALU.add
                                  ).then_inc(s.rotated, 1)
                dve.wait_ge(s.rotated, i + 1)

            def place(g, t):
                dve.wait_ge(s.tr_ready, 8 * g + t + 1)
                dve.tensor_copy(u.qk[g % 2][0:KS, :, P * t:P * t + P], u.tr[0:KS, :, :]).then_inc(s.tr_read, 1)

            def step(kind, g, k):
                (rotate if kind == "proj" else place)(g, k)

            def maxima(g):
                for n in range(plan.nm):
                    dve.wait_ge(s.max_ready, g * plan.nm + n + 1)
                    r = u.ring2[plan.slot(("max", g, n))]
                    if windowed:
                        w = min(WQ, P * n + P)
                        ins = dve.tensor_reduce(
                            u.mneg[:, :, n].rearrange("p (j h) -> p j h", j=2),
                            r.rearrange("p (j x) -> p j x", j=2)[:, :, 0:2 * WQ].rearrange(
                                "p j (h w) -> p j h w", h=2)[:, :, :, 0:w],
                            AX.X, ALU.max, negate=True)
                    else:
                        t, h = divmod(n, HG)
                        ins = dve.tensor_reduce(u.mneg[:, h, t:t + 1], r[:, 0:P * t + P], AX.X, ALU.max, negate=True)
                    ins.then_inc(s.max_read, 1)
                dve.wait_ge(s.max_read, plan.nm * (g + 1))
                m = u.mneg[:, :, :].rearrange("p h t -> p (h t)")
                if g:
                    dve.wait_ge(s.mt_ready, g)
                link(dve.tensor_copy(u.mparts[:, 0:32], m))
                link(dve.tensor_tensor(u.mrest[:, :], m, u.mparts[:, 0:32], ALU.subtract))
                link(dve.tensor_copy(u.mparts[:, 32:64], u.mrest[:, :]))
                dve.tensor_tensor(u.mparts[:, 64:96], u.mrest[:, :], u.mparts[:, 32:64], ALU.subtract
                                  ).then_inc(s.m_parts, 1)
                dve.wait_ge(s.mt_ready, g + 1)
                if g:
                    dve.wait_ge(s.m_rows, 48 * g)
                dve.tensor_copy(u.mrow[0:KS, :], u.tr[0:KS, 0, :]).then_inc(s.mt_read, 1)

            def normalise(g):
                dve.wait_ge(s.on_ready, g + 1)
                r = u.ring2[plan.slot(("out", g, 0))].rearrange("p (t h x) -> p t h x", t=NT, h=HG)
                link(dve.reciprocal(u.rden[:, :, :], r[:, :, :, HD]))
                dve.tensor_tensor(u.o[:, :, HG * HD * g:HG * HD * (g + 1)].rearrange("p t (h d) -> p t h d", h=HG),
                                  r[:, :, :, 0:HD], u.rden[:, :, :].unsqueeze(3).broadcast_to([P, NT, HG, HD]),
                                  ALU.mult).then_inc(s.out_ready, 1)

            for x in plan.prep:
                step(x[0], 0, x[1])
            maxima(0)
            for g in range(NG):
                if g + 1 < NG:
                    for x in plan.prep:
                        step(x[0], g + 1, x[1])
                    maxima(g + 1)
                normalise(g)

        @block.gpsimd
        def _(pool):
            for i in range(4 * NG):
                r, st = u.rot[i % 2], u.stack[i % 2]
                q = st[:, :, 0:HG, :].rearrange("p t h (s d) -> p t h s d", d=HD)
                k = st[:, :, HG:2 * HG, :].rearrange("p t h (s d) -> p t h s d", d=HD)
                both = st[:, :, :, :].rearrange("p t h (s d) -> p t h s d", d=HD)
                rq, rk = u.rest[:, :, 0:HG, :], u.rest[:, :, HG:2 * HG, :]
                pool.wait_ge(s.rotated, i + 1)
                if i >= 2:
                    pool.wait_ge(s.tr_ready, 2 * (i - 1))
                n = 3 * i
                pool.tensor_copy(both[:, :, :, 0, :], r[:, :, :, :]).then_inc(s.split, 1)
                pool.wait_ge(s.split, n + 1)
                pool.tensor_tensor(u.rest[:, :, :, :], r[:, :, :, :], both[:, :, :, 0, :], ALU.subtract).then_inc(s.split, 1)
                for x in (1, 2):
                    pool.tensor_copy(q[:, :, :, x, :], q[:, :, :, 0, :])
                for x in (4, 5):
                    pool.tensor_copy(k[:, :, :, x, :], k[:, :, :, 0, :])
                pool.wait_ge(s.split, n + 2)
                pool.tensor_copy(both[:, :, :, 3, :], u.rest[:, :, :, :]).then_inc(s.split, 1)
                pool.wait_ge(s.split, n + 3)
                pool.tensor_copy(q[:, :, :, 4, :], q[:, :, :, 3, :])
                pool.tensor_copy(k[:, :, :, 1, :], k[:, :, :, 3, :])
                pool.tensor_tensor(q[:, :, :, 5, :], rq, q[:, :, :, 3, :], ALU.subtract)
                pool.tensor_tensor(k[:, :, :, 2, :], rk, k[:, :, :, 3, :], ALU.subtract).then_inc(s.stack_ready, 1)
    clear(nc, s)


ATT_SEMS = ("src_in xt_ready xt_read pj_ready pj_read rotated split stack_ready tr_ready tr_read max_ready "
            "max_read m_parts mt_ready mt_read m_rows exp_ready exp_done pv_done o_read on_ready out_ready chain")



def constants():
    inv = 1.0 / 10000.0 ** (np.arange(0, HD, 2, dtype=np.float32) / HD)
    angle = (np.arange(T, dtype=np.float32)[:, None] * inv.astype(np.float32)).astype(np.float32)
    cos, sin = np.cos(angle), np.sin(angle)

    def by_tile(x):
        return np.ascontiguousarray(x.reshape(NT, P, HD).transpose(1, 0, 2)).astype(np.float32)
    p, w, f = np.arange(P)[:, None], np.arange(WQ)[None], np.arange(P)[None]
    behind = p + WINDOW - w
    mask_q = np.where((behind >= 0) & (behind < WINDOW), 0.0, NEG)
    ahead = w - p
    mask_k = np.where((ahead >= 0) & (ahead < WINDOW), 0.0, NEG)
    return {
        "c_cos": by_tile(np.concatenate([cos, cos], -1)),
        "c_sin": by_tile(np.concatenate([-sin, sin], -1)),
        "c_id32": np.eye(P, dtype=np.float32),
        "c_tables": np.concatenate(
            [np.eye(P), mask_q, mask_q, mask_k, mask_k, np.where(f <= p, 0.0, NEG), np.where(f >= p, 0.0, NEG),
             f >= p], 1).astype(np.float32),
        "c_blocks": (p // HD == f // HD).astype(np.float32),
        "c_iota": np.repeat(np.arange(E_, dtype=np.float32)[None], P, 0),
        "c_token": (P * np.arange(NT)[None] + p).astype(np.uint32),
    }


def sbuf(nc, ctx, made, name, shape, dtype=F32):
    made[name] = ctx.enter_context(nc.sbuf_tensor(f"b_{name}", shape, dtype))


def attention_buffers(nc, ctx, u):
    sbuf(nc, ctx, u, "cos", [P, NT, HD])
    sbuf(nc, ctx, u, "sin", [P, NT, HD])
    sbuf(nc, ctx, u, "id16", [P, P], BF16)
    sbuf(nc, ctx, u, "mask_q", [P, 2, WQ], BF16)
    sbuf(nc, ctx, u, "mask_k", [P, 2, WQ], BF16)
    sbuf(nc, ctx, u, "causal_q", [P, P], BF16)
    sbuf(nc, ctx, u, "causal_k", [P, P], BF16)
    sbuf(nc, ctx, u, "src", [P, NT, D])
    sbuf(nc, ctx, u, "xt", [P, NC, T])
    sbuf(nc, ctx, u, "o", [P, NT, D])
    sbuf(nc, ctx, u, "ra", [P, 2, 2 * HG, HD])
    sbuf(nc, ctx, u, "rb", [P, 2, 2 * HG, HD])
    sbuf(nc, ctx, u, "rest", [P, 2, 2 * HG, HD])
    sbuf(nc, ctx, u, "mneg", [P, HG, NT])
    sbuf(nc, ctx, u, "mrest", [P, HG * NT])
    sbuf(nc, ctx, u, "mparts", [P, KS], BF16)
    sbuf(nc, ctx, u, "mrow", [P, P], BF16)
    sbuf(nc, ctx, u, "ot_sb", [P, T])
    sbuf(nc, ctx, u, "rden", [P, NT, HG])
    for name, shape, dtype in (("rot", [P, 2, 2 * HG, HD], F32), ("stack", [P, 2, 2 * HG, KS], BF16),
                               ("qk", [P, 2 * HG, T], BF16), ("v", [P, NT, HG, 32], F32),
                               ("probs", [P, HG, T], F32)):
        for i in range(2):
            sbuf(nc, ctx, u, f"{name}{i}", shape, dtype)
        u[name] = [u[f"{name}0"], u[f"{name}1"]]
    psum = u["psum"]
    u["ring"] = psum[:, 0:4, :]
    u["ring2"] = [psum[:, 2 * i:2 * i + 2, :].rearrange("p a x -> p (a x)") for i in range(2)]
    u["ot"] = psum[:, 4:6, :].rearrange("p a x -> p (a x)")
    u["pj"] = psum[:, 6, :]
    u["tr"] = psum[:, 7, :].bitcast(BF16).rearrange("p (h x) -> p h x", x=P)



def norm_variance(dve, link, y, u, s):
    for t in range(NT):
        ins = dve.bn_stats(u.bn[:, t, :], y[:, t, :])
    link(ins)
    for t in range(NT):
        ins = dve.bn_aggr(u.mv[:, t, :], u.bn[:, t, :])
    link(ins)
    dve.tensor_scalar(u.var[:, :], u.mv[:, :, 1], EPS, None, ALU.add).then_inc(s.var_ready, 1)


def norm_root(act, u, s, k):
    act.wait_ge(s.var_ready, k + 1)
    act.activation(u.lnv[:, :], u.var[:, :], ACT.Ln).then_inc(s.ln_done, 1)
    act.wait_ge(s.ln_done, k + 1)
    act.activation(u.root[:, :], u.lnv[:, :], ACT.Exp, scale=-0.5).then_inc(s.root_ready, 1)


def norm_apply(dve, link, y, out, u, s, k):
    dve.wait_ge(s.root_ready, k + 1)
    link(dve.tensor_tensor(u.nt[:, :], u.root[:, :], u.root[:, :], ALU.mult))
    link(dve.tensor_tensor(u.nt[:, :], u.nt[:, :], u.var[:, :], ALU.mult))
    link(dve.tensor_scalar(u.nt[:, :], u.nt[:, :], -0.5, 1.5, ALU.mult, ALU.add))
    link(dve.tensor_tensor(u.rstd[:, :], u.root[:, :], u.nt[:, :], ALU.mult))
    for t in range(NT):
        ins = dve.tensor_scalar(out[:, t, :], y[:, t, :], u.mv[:, t, 0:1], u.rstd[:, t:t + 1],
                                ALU.subtract, ALU.mult)
    return ins


NORM_SEMS = " var_ready ln_done root_ready chain "


def turn_tiles(pe, src, u, s):
    for c in range(NC):
        for h in range(2):
            for t in range(4):
                ins = pe.transpose(u.psum[:, 2 * c + h, P * t:P * t + P], src[:, 4 * h + t, P * c:P * c + P], u.id32[:, :])
            ins.then_inc(s.turned, 1)


def take_turned(act, dst, u, s, k, gain=None, offset=None):
    for c in range(NC):
        for h in range(2):
            act.wait_ge(s.turned, 4 * k + 2 * c + h + 1)
            d = dst[:, c, BANK * h:BANK * h + BANK]
            if gain is None:
                act.activation(d, u.psum[:, 2 * c + h, :], ACT.Copy).then_inc(s.taken, 1)
            else:
                act.activation(d, u.psum[:, 2 * c + h, :], ACT.Identity, scale=gain[:, c:c + 1],
                               bias=offset[:, c:c + 1]).then_inc(s.taken, 1)


def pair_product(pe, bank, lhs, rhs, k):
    for t in range(2):
        for c in range(NC):
            ins = pe.matmul(bank[:, D * t:D * t + D], lhs[:, c, P * (2 * k + t):P * (2 * k + t + 1)], rhs[:, c, :],
                            start=(c == 0), stop=(c == NC - 1))
    return ins


def bank_pair(u, bank):
    return u.psum[:, bank, :].rearrange("p (t d) -> p t d", t=2)


def pair(x, k):
    return x[:, 2 * k:2 * k + 2, :].rearrange("p t d -> p (t d)")



POST0_SEMS = "turned taken pj_ready y_done x1_ready mix_r mix_k k_ready k_done r_ready r_low r_done v_ready v_done" + NORM_SEMS


def mixing(nc, u, s):
    with nc.Block() as block:
        @block.tensor
        def _(pe):
            turn_tiles(pe, u.o, u, s)
            pe.wait_ge(s.taken, 4)
            for k in range(4):
                if k >= 2:
                    pe.wait_ge(s.y_done, k - 1)
                pair_product(pe, u.psum[:, 4 + k % 2, :], u.xt, u.wout, k).then_inc(s.pj_ready, 1)
            pe.wait_ge(s.x1_ready, 1)
            turn_tiles(pe, u.src, u, s)
            pe.wait_ge(s.taken, 8)
            pe.wait_ge(s.mix_k, 2)
            for c in range(NC):
                for h in range(2):
                    for a in range(NC):
                        ins = pe.matmul(u.psum[:, 2 * c + h, :], u.wk0[:, a, P * c:P * c + P],
                                        u.xk[:, a, BANK * h:BANK * h + BANK], start=(a == 0), stop=(a == NC - 1))
                    ins.then_inc(s.k_ready, 1)
            pe.wait_ge(s.mix_r, 2)
            for k in range(4):
                if k >= 2:
                    pe.wait_ge(s.r_low, k - 1)
                pair_product(pe, u.psum[:, 4 + k % 2, :], u.xr, u.wr, k).then_inc(s.r_ready, 1)
            pe.wait_ge(s.k_done, 4)
            for k in range(4):
                if k >= 2:
                    pe.wait_ge(s.v_done, k - 1)
                pair_product(pe, u.psum[:, 6 + k % 2, :], u.xt, u.wv0, k).then_inc(s.v_ready, 1)

        @block.scalar
        def _(act):
            take_turned(act, u.xt, u, s, 0)
            norm_root(act, u, s, 0)
            take_turned(act, u.x1t[:, :, 1:T + 1], u, s, 1)
            for k in range(4):
                act.wait_ge(s.r_low, k + 1)
                act.activation(pair(u.r, k), pair(u.r, k), ACT.Exp, scale=-1.0).then_inc(s.r_done, 1)
            norm_root(act, u, s, 1)

        @block.vector
        def _(dve):
            link = dve_chain(dve, s.chain)
            link(dve.memset(u.x1t[:, :, 0:1], 0.0))
            for k in range(4):
                dve.wait_ge(s.pj_ready, k + 1)
                dve.tensor_tensor(pair(u.y, k), u.psum[:, 4 + k % 2, :], pair(u.src, k), ALU.add).then_inc(s.y_done, 1)
            dve.wait_ge(s.y_done, 4)
            norm_variance(dve, link, u.y, u, s)
            norm_apply(dve, link, u.y, u.src, u, s, 0).then_inc(s.x1_ready, 1)
            dve.wait_ge(s.taken, 8)
            link(dve.tensor_tensor(u.dx[:, :, :], u.x1t[:, :, 1:T + 1], u.x1t[:, :, 0:T], ALU.subtract))
            for c in range(NC):
                dve.scalar_tensor_tensor(u.xk[:, c, :], u.dx[:, c, :], u.muk[:, c:c + 1], u.x1t[:, c, 0:T],
                                         ALU.mult, ALU.add).then_inc(s.mix_k, 1)
            for c in range(NC):
                dve.scalar_tensor_tensor(u.xr[:, c, :], u.dx[:, c, :], u.mur[:, c:c + 1], u.x1t[:, c, 0:T],
                                         ALU.mult, ALU.add).then_inc(s.mix_r, 1)
            for c in range(NC):
                for h in range(2):
                    j = 2 * c + h
                    dve.wait_ge(s.k_ready, j + 1)
                    link(dve.tensor_scalar(pair(u.y, j), u.psum[:, j, :], 0.0, None, ALU.max))
                    dve.tensor_tensor(u.xt[:, c, BANK * h:BANK * h + BANK], pair(u.y, j), pair(u.y, j), ALU.mult
                                      ).then_inc(s.k_done, 1)
            for k in range(4):
                dve.wait_ge(s.r_ready, k + 1)
                dve.tensor_scalar(pair(u.r, k), u.psum[:, 4 + k % 2, :], -87.0, None, ALU.max).then_inc(s.r_low, 1)
            for k in range(4):
                dve.wait_ge(s.r_done, k + 1)
                link(dve.tensor_scalar(pair(u.r, k), pair(u.r, k), 1.0, None, ALU.add))
                link(dve.reciprocal(pair(u.r, k), pair(u.r, k)))
                dve.wait_ge(s.v_ready, k + 1)
                dve.tensor_tensor(pair(u.r, k), u.psum[:, 6 + k % 2, :], pair(u.r, k), ALU.mult).then_inc(s.v_done, 1)
                dve.wait_ge(s.v_done, k + 1)
                ins = dve.tensor_tensor(pair(u.y, k), pair(u.r, k), pair(u.src, k), ALU.add)
            link(ins)
            norm_variance(dve, link, u.y, u, s)
            link(norm_apply(dve, link, u.y, u.src, u, s, 1))
    clear(nc, s)



LIN_SEMS = ("turned taken q_ready q_min q_exp q_done k_ready k_add k_min k_exp k_done v_ready v_done kv_ready kvm_done "
            "m_ready m_done a_ready a_done out_ready y_done res_ready") + NORM_SEMS


def linear_attention(nc, u, s):
    with nc.Block() as block:
        @block.tensor
        def _(pe):
            turn_tiles(pe, u.src, u, s)
            pe.wait_ge(s.taken, 4)
            for c in range(NC):
                for h in range(2):
                    for a in range(NC):
                        ins = pe.matmul(u.psum[:, 2 * c + h, :], u.wq1[:, a, P * c:P * c + P],
                                        u.xt[:, a, BANK * h:BANK * h + BANK], start=(a == 0), stop=(a == NC - 1))
                    ins.then_inc(s.q_ready, 1)
            for k in range(4):
                if k >= 2:
                    pe.wait_ge(s.k_add, k - 1)
                    pe.wait_ge(s.v_done, k - 1)
                pair_product(pe, u.psum[:, 4 + k % 2, :], u.xt, u.wk1, k).then_inc(s.k_ready, 1)
                pair_product(pe, u.psum[:, 6 + k % 2, :], u.xt, u.wv1, k).then_inc(s.v_ready, 1)
            pe.wait_ge(s.k_done, 4)
            pe.wait_ge(s.v_done, 4)
            for c in range(NC):
                for t in range(NT):
                    ins = pe.matmul(u.psum[:, 4, P * c:P * c + P], u.o[:, t, P * c:P * c + P], u.y[:, t, P * c:P * c + P],
                                    start=(t == 0), stop=(t == NT - 1))
            ins.then_inc(s.kv_ready, 1)
            pe.wait_ge(s.kvm_done, 1)
            for c in range(NC):
                ins = pe.matmul(u.psum[:, 5, P * c:P * c + P], u.kvm[:, c, :], u.bg[:, :], start=True, stop=True)
            ins.then_inc(s.m_ready, 1)
            pe.wait_ge(s.m_done, 1)
            for c in range(NC):
                ins = pe.matmul(u.psum[:, 6, D * c:D * c + D], u.mt[:, c, :], u.wo1[:, c, :], start=True, stop=True)
            ins.then_inc(s.a_ready, 1)
            pe.wait_ge(s.a_done, 1)
            pe.wait_ge(s.q_done, 4)
            for k in range(4):
                pair_product(pe, u.psum[:, k, :], u.phq, u.am, k).then_inc(s.out_ready, 1)

        @block.scalar
        def _(act):
            take_turned(act, u.xt, u, s, 0)
            for j in range(4):
                act.wait_ge(s.q_min, j + 1)
                d = (slice(None), j // 2, slice(BANK * (j % 2), BANK * (j % 2) + BANK))
                act.activation(u.qexp[d], u.qexp[d], ACT.Exp).then_inc(s.q_exp, 1)
            for k in range(4):
                act.wait_ge(s.k_min, k + 1)
                act.activation(pair(u.o, k), pair(u.o, k), ACT.Exp).then_inc(s.k_exp, 1)
            act.wait_ge(s.m_ready, 1)
            act.activation(u.mt[:, :, :].rearrange("p c x -> p (c x)"), u.psum[:, 5, 0:D], ACT.Copy).then_inc(s.m_done, 1)
            act.wait_ge(s.a_ready, 1)
            act.activation(u.am[:, :, :].rearrange("p c x -> p (c x)"), u.psum[:, 6, :], ACT.Copy).then_inc(s.a_done, 1)
            norm_root(act, u, s, 0)
            norm_root(act, u, s, 1)

        @block.gpsimd
        def _(pool):
            pool.wait_ge(s.turned, 4)
            pool.tensor_tensor(u.src[:, :, :], u.src[:, :, :], u.bo[:, :].unsqueeze(1).broadcast_to([P, NT, D]),
                               ALU.add).then_inc(s.res_ready, 1)

        @block.vector
        def _(dve):
            link = dve_chain(dve, s.chain)

            def span(j):
                return (slice(None), j // 2, slice(BANK * (j % 2), BANK * (j % 2) + BANK))
            for j in range(4):
                dve.wait_ge(s.q_ready, j + 1)
                dve.tensor_scalar(u.qexp[span(j)], u.psum[:, j, :], u.bq[:, j // 2:j // 2 + 1], 0.0, ALU.add, ALU.min
                                  ).then_inc(s.q_min, 1)
            for k in range(4):
                dve.wait_ge(s.k_ready, k + 1)
                dve.tensor_tensor(u.kx[:, 2 * k:2 * k + 2, :], bank_pair(u, 4 + k % 2),
                                  u.bk[:, :].unsqueeze(1).broadcast_to([P, 2, D]), ALU.add).then_inc(s.k_add, 1)
                dve.wait_ge(s.k_add, k + 1)
                dve.tensor_scalar(pair(u.o, k), pair(u.kx, k), 0.0, None, ALU.min).then_inc(s.k_min, 1)
                dve.wait_ge(s.v_ready, k + 1)
                dve.tensor_tensor(u.y[:, 2 * k:2 * k + 2, :], bank_pair(u, 6 + k % 2),
                                  u.bv[:, :].unsqueeze(1).broadcast_to([P, 2, D]), ALU.add).then_inc(s.v_done, 1)
                dve.wait_ge(s.q_exp, k + 1)
                dve.scalar_tensor_tensor(u.phq[span(k)], u.psum[:, k, :], u.bq_plus[:, k // 2:k // 2 + 1],
                                         u.qexp[span(k)], ALU.add, ALU.max).then_inc(s.q_done, 1)
            for k in range(4):
                dve.wait_ge(s.k_exp, k + 1)
                dve.scalar_tensor_tensor(pair(u.o, k), pair(u.kx, k), 1.0, pair(u.o, k), ALU.add, ALU.max
                                         ).then_inc(s.k_done, 1)
            dve.wait_ge(s.kv_ready, 1)
            dve.tensor_tensor(u.kvm[:, :, :], u.psum[:, 4, 0:D].rearrange("p (c x) -> p c x", c=NC),
                              u.blocks[:, :].unsqueeze(1).broadcast_to([P, NC, P]), ALU.mult).then_inc(s.kvm_done, 1)
            dve.wait_ge(s.res_ready, 1)
            dve.wait_ge(s.kv_ready, 1)
            for k in range(4):
                dve.wait_ge(s.out_ready, k + 1)
                ins = dve.tensor_tensor(pair(u.y, k), u.psum[:, k, :], pair(u.src, k), ALU.add)
            link(ins)
            norm_variance(dve, link, u.y, u, s)
            link(norm_apply(dve, link, u.y, u.x3, u, s, 0))
            norm_variance(dve, link, u.x3, u, s)
            link(norm_apply(dve, link, u.x3, u.src, u, s, 1))
    clear(nc, s)



ROUTE_SEMS = ("turned taken pj_ready y_done x4_kept z_ready z_out lg_ready shifted exp_done mask_ready pos_ready "
              "slots_ready slots_gathered") + NORM_SEMS


def route(nc, b, u, s, z_dram, slots_dram):
    with nc.Block() as block:
        @block.sync
        def _(sp):
            sp.wait_ge(s.z_ready, 1)
            sp.dma_start(z_dram[bass.ds(b * T, T), :].rearrange("(t p) d -> p t d", p=P), u.src[:, :, :]
                         ).then_inc(s.z_out, 16)
            sp.wait_ge(s.z_out, 16)

        @block.tensor
        def _(pe):
            turn_tiles(pe, u.o, u, s)
            pe.wait_ge(s.taken, 4)
            for k in range(4):
                if k >= 2:
                    pe.wait_ge(s.y_done, k - 1)
                pair_product(pe, u.psum[:, 4 + k % 2, :], u.xt, u.wproj, k).then_inc(s.pj_ready, 1)
            pe.wait_ge(s.z_ready, 1)
            turn_tiles(pe, u.src, u, s)
            pe.wait_ge(s.taken, 8)
            for t in range(NT):
                for c in range(NC):
                    ins = pe.matmul(u.psum[:, 6, E_ * t:E_ * t + E_], u.xt[:, c, P * t:P * t + P], u.wgate[:, c, :],
                                    start=(c == 0), stop=(c == NC - 1))
            ins.then_inc(s.lg_ready, 1)
            pe.wait_ge(s.mask_ready, 1)
            for t in range(NT):
                out = u.psum[:, 7, E_ * t:E_ * t + E_]
                pe.matmul(out, u.upto[:, :], u.chosen[:, t, :], start=True, stop=False)
                for a in range(t):
                    pe.matmul(out, u.ones16[:, :], u.chosen[:, a, :], start=False, stop=False)
                ins = pe.matmul(out, u.ones16[:, :], u.before[:, :], start=False, stop=True)
            ins.then_inc(s.pos_ready, 1)

        @block.scalar
        def _(act):
            take_turned(act, u.xt, u, s, 0)
            norm_root(act, u, s, 0)
            take_turned(act, u.xt, u, s, 1, u.ln2g, u.ln2b)
            act.wait_ge(s.shifted, 1)
            act.activation(u.gexp[:, :, :], u.gexp[:, :, :], ACT.Exp).then_inc(s.exp_done, 1)

        @block.vector
        def _(dve):
            link = dve_chain(dve, s.chain)
            for k in range(4):
                dve.wait_ge(s.pj_ready, k + 1)
                dve.tensor_tensor(pair(u.y, k), u.psum[:, 4 + k % 2, :], pair(u.x3, k), ALU.add).then_inc(s.y_done, 1)
            dve.wait_ge(s.y_done, 4)
            norm_variance(dve, link, u.y, u, s)
            norm_apply(dve, link, u.y, u.src, u, s, 0).then_inc(s.z_ready, 1)
            dve.wait_ge(s.lg_ready, 1)
            lg, top = u.lg, u.top
            link(dve.tensor_copy(lg[:, :, :].rearrange("p t e -> p (t e)"), u.psum[:, 6, 0:NT * E_]))
            for t in range(NT):
                ins = dve.max(top[:, t, :], lg[:, t, :])
            link(ins)
            dve.tensor_tensor(u.gexp[:, :, :], lg[:, :, :], top[:, :, 0:1].broadcast_to([P, NT, E_]), ALU.subtract
                              ).then_inc(s.shifted, 1)
            for t in range(NT):
                ins = dve.max_index(u.topi[:, t, :], top[:, t, :], lg[:, t, :])
            link(ins)
            link(dve.tensor_copy(u.expert[:, :, :].rearrange("p k t -> p t k"), u.topi[:, :, 0:TOPK]))
            for k in range(TOPK):
                ins = dve.tensor_tensor(u.is_it[:, k, :, :], u.iota[:, :].unsqueeze(1).broadcast_to([P, NT, E_]),
                                        u.expert[:, k, :].unsqueeze(2).broadcast_to([P, NT, E_]), ALU.is_equal)
            link(ins)
            dve.tensor_tensor(u.chosen[:, :, :], u.is_it[:, 0, :, :], u.is_it[:, 1, :, :], ALU.add
                              ).then_inc(s.mask_ready, 1)
            dve.wait_ge(s.exp_done, 1)
            link(dve.tensor_reduce(u.gsum[:, :], u.gexp[:, :, :], AX.X, ALU.add))
            dve.reciprocal(u.gsum[:, :], u.gsum[:, :])
            for k in range(TOPK):
                ins = dve.tensor_tensor(u.pick[:, k, :, :], u.is_it[:, k, :, :], u.gexp[:, :, :], ALU.mult)
            link(ins)
            link(dve.tensor_reduce(u.gate[:, :, :], u.pick[:, :, :, :], AX.X, ALU.add))
            link(dve.tensor_tensor(u.gate[:, :, :], u.gate[:, :, :], u.gsum[:, :].unsqueeze(1).broadcast_to([P, TOPK, NT]),
                                   ALU.mult))
            dve.wait_ge(s.pos_ready, 1)
            pos = u.psum[:, 7, 0:NT * E_].rearrange("p (t e) -> p t e", e=E_)
            for k in range(TOPK):
                ins = dve.tensor_tensor(u.pick[:, k, :, :], u.is_it[:, k, :, :], pos, ALU.mult)
            link(ins)
            link(dve.tensor_reduce(u.place[:, :, :], u.pick[:, :, :, :], AX.X, ALU.add))
            link(dve.tensor_scalar(u.keep[:, :, :], u.place[:, :, :], float(CAP), None, ALU.is_le))
            link(dve.tensor_scalar(u.place[:, :, :], u.place[:, :, :], float(CAP), -1.0, ALU.min, ALU.add))
            link(dve.scalar_tensor_tensor(u.place[:, :, :], u.expert[:, :, :], float(CAP), u.place[:, :, :],
                                          ALU.mult, ALU.add))
            dve.tensor_copy(u.read_at[:, :, bass.ds(b * NT, NT)], u.place[:, :, :])
            dve.tensor_tensor(u.gates[:, :, bass.ds(b * NT, NT)], u.gate[:, :, :], u.keep[:, :, :], ALU.mult)
            link(dve.tensor_scalar(u.keep[:, :, :], u.keep[:, :, :], -DROPPED, DROPPED, ALU.mult, ALU.add))
            dve.tensor_tensor(u.write_at[:, :, :], u.place[:, :, :], u.keep[:, :, :], ALU.add).then_inc(s.slots_ready, 1)
            link(dve.tensor_reduce(u.count[:, :], u.chosen[:, :, :].rearrange("p t e -> p e t"), AX.X, ALU.add))
            link(dve.tensor_tensor(u.before[:, :], u.before[:, :], u.count[:, :], ALU.add))
            dve.wait_ge(s.slots_gathered, 16 * TOPK * NT * (b + 1))
            link(dve.tensor_scalar(u.token[:, :], u.token[:, :], float(T), None, ALU.add))

        @block.gpsimd
        def _(pool):
            pool.wait_ge(s.y_done, 4)
            pool.tensor_tensor(u.x4[:, bass.ds(b * NT, NT), :], u.y[:, :, :], u.x3[:, :, :], ALU.add).then_inc(s.x4_kept, 1)
            pool.wait_ge(s.x4_kept, 1)
            pool.wait_ge(s.slots_ready, 1)
            for k in range(TOPK):
                for t in range(NT):
                    pool.indirect_dma_start(
                        out=slots_dram, out_offset=bass.IndirectOffsetOnAxis(ap=u.write_at[:, k, t:t + 1], axis=0),
                        in_=u.token[:, t:t + 1], in_offset=None, bounds_check=E_ * CAP - 1, oob_is_err=False
                    ).then_inc(s.slots_gathered, 16)
            pool.wait_ge(s.slots_gathered, 16 * TOPK * NT * (b + 1))
    clear(nc, s)



MOE_SEMS = ("sliced w0_in w1_in x0_gathered x1_gathered b2_in turned taken h_ready h_done y_ready y_done y0_out y1_out")


def load_expert(eng, e, j, u, w1_dram, w2_dram, sem):
    eng.dma_start(u.w1[j][:, :, :], w1_dram[bass.ds(e, 1), :, :].rearrange("o (c p) f -> p (o c) f", p=P)).then_inc(sem, 16)
    eng.dma_start(u.w2[j][:, :, :], w2_dram[bass.ds(e, 1), :, :].rearrange("o (n p) d -> p (o n) d", p=P)).then_inc(sem, 16)


def experts(nc, i, u, s, z_dram, w1_dram, w2_dram, b2_dram, y_dram):
    with nc.Block() as block:
        @block.sync
        def _(sp):
            load_expert(sp, 2 * i + 1, 1, u, w1_dram, w2_dram, s.w1_in)
            for j in range(2):
                sp.dma_start(u.b2b[j][:, :], b2_dram[bass.ds(2 * i + j, 1), :].partition_broadcast(P)
                             .rearrange("p o d -> p (o d)")).then_inc(s.b2_in, 16)
            for q in range(CT):
                if q == CT // 2:
                    sp.wait_ge(s.y_ready, CT // 2)
                    load_expert(sp, (2 * i + 2) % E_, 0, u, w1_dram, w2_dram, s.w0_in)
                sp.wait_ge(s.y_done, q + 1)
                sp.dma_start(y_dram[bass.ds(2 * CAP * i + 2 * P * q, 2 * P), :].rearrange("(t p) d -> p t d", p=P),
                             u.ye[q % 2][:, :, :]).then_inc((s.y0_out, s.y1_out)[q % 2], 16)
            sp.wait_ge(s.w0_in, 32)
            for q in range(2):
                sp.wait_ge((s.y0_out, s.y1_out)[q], 16 * CT // 2)

        @block.gpsimd
        def _(pool):
            pool.wait_ge(s.sliced, 1)
            for j in range(2):
                for t in range(CT):
                    pool.indirect_dma_start(
                        out=u.xg[j][:, t, :], out_offset=None, in_=z_dram,
                        in_offset=bass.IndirectOffsetOnAxis(ap=u.ids[:, j * CT + t:j * CT + t + 1], axis=0),
                        bounds_check=N - 1, oob_is_err=True).then_inc((s.x0_gathered, s.x1_gathered)[j], 16)

        @block.tensor
        def _(pe):
            def turn(j):
                if j:
                    pe.wait_ge(s.h_done, 16 * j)
                pe.wait_ge((s.x0_gathered, s.x1_gathered)[j], 16 * CT * (i + 1))
                for c in range(NC):
                    for h in range(2):
                        for t in range(4):
                            ins = pe.transpose(u.psum[:, 2 * c + h, P * t:P * t + P],
                                               u.xg[j][:, 4 * h + t, P * c:P * c + P], u.id32[:, :])
                        ins.then_inc(s.turned, 1)

            for j in range(2):
                turn(j)
                pe.wait_ge(s.taken, 4 * (j + 1))
                if j:
                    pe.wait_ge(s.w1_in, 32)
                for n in range(NF):
                    for h in range(2):
                        k = 2 * n + h
                        if k >= 4:
                            pe.wait_ge(s.h_done, 16 * j + k - 3)
                        for c in range(NC):
                            ins = pe.matmul(u.psum[:, k % 4, :], u.w1[j][:, c, P * n:P * n + P],
                                            u.xgt[:, c, BANK * h:BANK * h + BANK], start=(c == 0), stop=(c == NC - 1))
                        ins.then_inc(s.h_ready, 1)
                pe.wait_ge(s.h_done, 16 * (j + 1))
                for k in range(CT // 2):
                    q = CT // 2 * j + k
                    if q >= 4:
                        pe.wait_ge(s.y_done, q - 3)
                    for t in range(2):
                        for n in range(NF):
                            ins = pe.matmul(u.psum[:, 4 + k, D * t:D * t + D],
                                            u.hid[:, n, P * (2 * k + t):P * (2 * k + t + 1)], u.w2[j][:, n, :],
                                            start=(n == 0), stop=(n == NF - 1))
                    ins.then_inc(s.y_ready, 1)

        @block.scalar
        def _(act):
            for j in range(2):
                for c in range(NC):
                    for h in range(2):
                        act.wait_ge(s.turned, 4 * j + 2 * c + h + 1)
                        act.activation(u.xgt[:, c, BANK * h:BANK * h + BANK], u.psum[:, 2 * c + h, :], ACT.Identity,
                                       scale=u.ln2g[:, c:c + 1], bias=u.ln2b[:, c:c + 1]).then_inc(s.taken, 1)
                if j:
                    act.wait_ge(s.y_ready, 4 * j)
                for n in range(NF):
                    for h in range(2):
                        k = 2 * n + h
                        act.wait_ge(s.h_ready, 16 * j + k + 1)
                        act.activation(u.hid[:, n, BANK * h:BANK * h + BANK], u.psum[:, k % 4, :], ACT.Gelu,
                                       bias=u.b1s[:, j * NF + n:j * NF + n + 1]).then_inc(s.h_done, 1)

        @block.vector
        def _(dve):
            dve.tensor_copy(u.ids[:, :], u.slots[:, bass.ds(2 * CT * i, 2 * CT)])
            dve.tensor_copy(u.b1s[:, :], u.b1[:, bass.ds(2 * NF * i, 2 * NF)]).then_inc(s.sliced, 1)
            dve.wait_ge(s.b2_in, 32)
            for q in range(CT):
                j, k = divmod(q, CT // 2)
                dve.wait_ge(s.y_ready, q + 1)
                if q >= 2:
                    dve.wait_ge((s.y0_out, s.y1_out)[q % 2], 16 * (q // 2))
                dve.tensor_tensor(u.ye[q % 2][:, :, :], u.psum[:, 4 + k, :].rearrange("p (t d) -> p t d", t=2),
                                  u.b2b[j][:, :].unsqueeze(1).broadcast_to([P, 2, D]), ALU.add).then_inc(s.y_done, 1)
    clear(nc, s)



COMBINE_SEMS = "sliced r0_gathered r1_gathered r2_gathered r3_gathered r4_gathered r5_gathered r6_gathered r7_gathered sum_done out_ready out_done" + NORM_SEMS


def combine(nc, b, u, s, y_dram, out_dram):
    gathered = (s.r0_gathered, s.r1_gathered, s.r2_gathered, s.r3_gathered, s.r4_gathered, s.r5_gathered,
                s.r6_gathered, s.r7_gathered)
    with nc.Block() as block:
        @block.gpsimd
        def _(pool):
            pool.wait_ge(s.sliced, 1)
            for t in range(NT):
                for k in range(TOPK):
                    pool.indirect_dma_start(
                        out=u.rows[:, TOPK * t + k, :], out_offset=None, in_=y_dram,
                        in_offset=bass.IndirectOffsetOnAxis(ap=u.at[:, k, t:t + 1], axis=0),
                        bounds_check=E_ * CAP - 1, oob_is_err=True).then_inc(gathered[t], 16)

        @block.scalar
        def _(act):
            norm_root(act, u, s, 0)

        @block.vector
        def _(dve):
            link = dve_chain(dve, s.chain)
            dve.tensor_copy(u.at[:, :, :], u.read_at[:, :, bass.ds(b * NT, NT)]).then_inc(s.sliced, 1)
            link(dve.tensor_copy(u.gate[:, :, :], u.gates[:, :, bass.ds(b * NT, NT)]))
            link(dve.tensor_copy(u.y[:, :, :], u.x4[:, bass.ds(b * NT, NT), :]))
            for t in range(NT):
                dve.wait_ge(gathered[t], 16 * TOPK * (b + 1))
                for k in range(TOPK):
                    dve.scalar_tensor_tensor(u.y[:, t, :], u.rows[:, TOPK * t + k, :], u.gate[:, k, t:t + 1],
                                             u.y[:, t, :], ALU.mult, ALU.add).then_inc(s.sum_done, 1)
                    dve.wait_ge(s.sum_done, TOPK * t + k + 1)
            norm_variance(dve, link, u.y, u, s)
            norm_apply(dve, link, u.y, u.y, u, s, 0).then_inc(s.out_ready, 1)

        @block.sync
        def _(sp):
            sp.wait_ge(s.out_ready, 1)
            sp.dma_start(out_dram[bass.ds(b, 1), :, :].rearrange("o (t p) d -> p (o t) d", p=P), u.y[:, :, :]
                         ).then_inc(s.out_done, 16)
            sp.wait_ge(s.out_done, 16)
    clear(nc, s)



def lasting_buffers(nc, ctx, u):
    for name, shape, dtype in (
            ("x4", [P, B * NT, D], F32), ("y", [P, NT, D], F32), ("id32", [P, P], F32),
            ("gates", [P, TOPK, B * NT], F32), ("read_at", [P, TOPK, B * NT], U32), ("gate", [P, TOPK, NT], F32),
            ("bn", [P, NT, 6], F32), ("mv", [P, NT, 2], F32), ("var", [P, NT], F32), ("lnv", [P, NT], F32),
            ("root", [P, NT], F32), ("nt", [P, NT], F32), ("rstd", [P, NT], F32),
            ("ln2g", [P, NC], F32), ("ln2b", [P, NC], F32)):
        sbuf(nc, ctx, u, name, shape, dtype)
    u["psum"] = ctx.enter_context(nc.psum_tensor("b_psum", [P, 8, BANK], F32))


def layer_buffers(nc, ctx, u):
    for name in "wout wr wk0 wv0 wq1 wk1 wv1 wo1 wproj".split():
        sbuf(nc, ctx, u, name, [P, NC, D])
    sbuf(nc, ctx, u, "wqkv0", [P, NC, NG, 192])
    sbuf(nc, ctx, u, "wqkv1", [P, NC, NG, 192])
    sbuf(nc, ctx, u, "wgate", [P, NC, E_])
    for name in "mur muk bq bq_plus ln1g ln1b".split():
        sbuf(nc, ctx, u, name, [P, NC])
    for name in "bk bv bo".split():
        sbuf(nc, ctx, u, name, [P, D])
    sbuf(nc, ctx, u, "rft", [64, P])
    sbuf(nc, ctx, u, "blocks", [P, P])
    sbuf(nc, ctx, u, "bg", [P, P])
    sbuf(nc, ctx, u, "kvm", [P, NC, P])
    sbuf(nc, ctx, u, "mt", [P, NC, P])
    sbuf(nc, ctx, u, "am", [P, NC, D])
    sbuf(nc, ctx, u, "x3", [P, NT, D])
    for name, shape, dtype in (
            ("lg", [P, NT, E_], F32), ("top", [P, NT, 8], F32), ("topi", [P, NT, 8], U32), ("gexp", [P, NT, E_], F32),
            ("expert", [P, TOPK, NT], F32), ("is_it", [P, TOPK, NT, E_], F32), ("pick", [P, TOPK, NT, E_], F32),
            ("place", [P, TOPK, NT], F32), ("keep", [P, TOPK, NT], F32), ("write_at", [P, TOPK, NT], U32),
            ("gsum", [P, NT], F32), ("count", [P, E_], F32), ("chosen", [P, NT, E_], BF16), ("before", [P, E_], BF16),
            ("token", [P, NT], U32), ("iota", [P, E_], F32), ("upto", [P, P], BF16), ("ones16", [P, P], BF16),
            ("no_token", [E_ * CAP // P, P], U32)):
        sbuf(nc, ctx, u, name, shape, dtype)
    def part(i, j):
        return u["probs"][i][:, 2 * j:2 * j + 2, :]

    def tiles(x):
        return x.rearrange("p a (t d) -> p (a t) d", d=D)
    flat = u["probs"][0][:, :, :].rearrange("p h t -> p (h t)")
    u["x1t"] = flat[:, 0:NC * (T + 1)].rearrange("p (c t) -> p c t", c=NC)
    u["xk"], u["xr"] = part(1, 0), part(1, 1)
    u["r"] = u["o"]
    u["dx"] = u["o"][:, :, :].rearrange("p (c a) d -> p c (a d)", c=NC)
    u["qexp"], u["phq"], u["kx"] = part(0, 0), part(0, 1), tiles(part(1, 0))


def set_up(nc, ctx, made, a, slots_dram):
    u = named(made)
    loaded = ctx.enter_context(nc.semaphore("weights_in"))
    zeroed = ctx.enter_context(nc.semaphore("zeroed"))
    fixed = ctx.enter_context(nc.semaphore("fixed"))
    gram = ctx.enter_context(nc.semaphore("gram_ready"))
    names = ("wqkv0 wout wr wk0 wv0 mur muk wq1 wk1 wv1 wo1 wproj wqkv1 wgate bq ln1g ln1b ln2g ln2b "
             "cos sin id32 blocks iota token").split()
    count = len(names) + 4 + P // HD
    bf16_tables = (u.id16[:, :], u.mask_q[:, :, :], u.mask_k[:, :, :], u.causal_q[:, :], u.causal_k[:, :], u.upto[:, :])
    width = [P, 2 * WQ, 2 * WQ, P, P, P]
    tables = u.y[:, :, :].rearrange("p t d -> p (t d)")[:, 0:sum(width)]
    with nc.Block() as block:
        @block.sync
        def _(sp):
            for n in names:
                sp.dma_start(made[n][:], a[n]).then_inc(loaded, 16)
            sp.dma_start(tables, a["tables"]).then_inc(loaded, 16)
            for n in ("bk", "bv", "bo"):
                sp.dma_start(made[n][:, :], a[n].partition_broadcast(P).rearrange("p o d -> p (o d)")).then_inc(loaded, 16)
            for j in range(P // HD):
                sp.dma_start(u.rft[:, HD * j:HD * j + HD], a["rft"]).then_inc(loaded, 16)
            sp.wait_ge(zeroed, 1)
            sp.dma_start(slots_dram.rearrange("(r p) o -> r (p o)", p=P), u.no_token[:, :]).then_inc(loaded, 16)
            sp.wait_ge(loaded, 16 * (count + 1))

        @block.vector
        def _(dve):
            dve.memset(u.no_token[:, :], 0).then_inc(zeroed, 1)
            for i in range(2):
                dve.memset(u.v[i][:, :, :, HD:32], 1.0)
                dve.memset(u.qk[i][KS:KS + 32, HG:2 * HG, :], 1.0)
            dve.memset(u.before[:, :], 0.0)
            dve.memset(u.ones16[:, :], 1.0)
            dve.wait_ge(loaded, 16 * (count + 1))
            for i, t in enumerate(bf16_tables):
                part = tables[:, sum(width[:i]):sum(width[:i + 1])]
                dve.tensor_copy(t, part if width[i] == P else part.rearrange("p (h w) -> p h w", h=2))
            dve.tensor_scalar(u.bq_plus[:, :], u.bq[:, :], 1.0, None, ALU.add).then_inc(fixed, 1)
            dve.wait_ge(gram, 1)
            dve.tensor_tensor(u.bg[:, :], u.psum[:, 0, 0:P], u.blocks[:, :], ALU.mult).then_inc(fixed, 1)

        @block.tensor
        def _(pe):
            pe.wait_ge(loaded, 16 * (count + 1))
            pe.matmul(u.psum[:, 0, 0:P], u.rft[:, :], u.rft[:, :], start=True, stop=True).then_inc(gram, 1)


def table_of_slots(nc, ctx, u, slots_dram):
    s = semaphores(nc, ctx, "table", "read floats turned taken")
    with nc.Block() as block:
        @block.sync
        def _(sp):
            sp.dma_start(u.slot_rows[:, :], slots_dram.rearrange("(r p) o -> r (p o)", p=P)).then_inc(s.read, 16)

        @block.vector
        def _(dve):
            dve.wait_ge(s.read, 16)
            dve.tensor_copy(u.slot_floats[:, :], u.slot_rows[:, :]).then_inc(s.floats, 1)
            dve.wait_ge(s.turned, 1)
            dve.tensor_copy(u.slots[:, :], u.psum[:, 0, 0:E_ * CT]).then_inc(s.taken, 1)

        @block.tensor
        def _(pe):
            pe.wait_ge(s.floats, 1)
            pe.transpose(u.psum[:, 0, 0:E_ * CT], u.slot_floats[:, :], u.id32[0:E_ * CT, 0:E_ * CT]).then_inc(s.turned, 1)


def two_layers(nc, a, out):
    slots_dram = nc.dram_tensor("slots", (E_ * CAP, 1), U32, kind="Internal").ap()
    z_dram = nc.dram_tensor("normed", (N, D), F32, kind="Internal").ap()
    y_dram = nc.dram_tensor("expert_rows", (E_ * CAP, D), F32, kind="Internal").ap()
    with ExitStack() as ctx:
        lasting = {}
        lasting_buffers(nc, ctx, lasting)
        att = semaphores(nc, ctx, "att", ATT_SEMS)
        mix = semaphores(nc, ctx, "mix", POST0_SEMS)
        lin = semaphores(nc, ctx, "lin", LIN_SEMS)
        rt = semaphores(nc, ctx, "route", ROUTE_SEMS)
        moe = semaphores(nc, ctx, "moe", MOE_SEMS)
        comb = semaphores(nc, ctx, "comb", COMBINE_SEMS)
        nc.scalar.preload_act_table_set("natural_log_exp_and_others")
        with ExitStack() as layer:
            made = dict(lasting)
            attention_buffers(nc, layer, made)
            layer_buffers(nc, layer, made)
            set_up(nc, ctx, made, a, slots_dram)
            u = named(made)
            with nc.Fori(0, B) as b:
                attention(nc, b, u, att, True, a["x"])
                mixing(nc, u, mix)
                linear_attention(nc, u, lin)
                attention(nc, b, u, att, False)
                route(nc, b, u, rt, z_dram, slots_dram)
        with ExitStack() as layer:
            made = dict(lasting)
            for i in range(2):
                sbuf(nc, layer, made, f"w1{i}", [P, NC, F_])
                sbuf(nc, layer, made, f"w2{i}", [P, NF, D])
                sbuf(nc, layer, made, f"xg{i}", [P, CT, D])
                sbuf(nc, layer, made, f"ye{i}", [P, 2, D])
                sbuf(nc, layer, made, f"b2b{i}", [P, D])
            for n in ("w1", "w2", "xg", "ye", "b2b"):
                made[n] = [made[n + "0"], made[n + "1"]]
            sbuf(nc, layer, made, "xgt", [P, NC, CAP])
            sbuf(nc, layer, made, "hid", [P, NF, CAP])
            sbuf(nc, layer, made, "slot_rows", [E_ * CT, P], U32)
            sbuf(nc, layer, made, "slot_floats", [E_ * CT, P])
            sbuf(nc, layer, made, "slots", [P, E_ * CT], U32)
            sbuf(nc, layer, made, "ids", [P, 2 * CT], U32)
            sbuf(nc, layer, made, "b1", [P, E_ * NF])
            sbuf(nc, layer, made, "b1s", [P, 2 * NF])
            sbuf(nc, layer, made, "rows", [P, TOPK * NT, D])
            sbuf(nc, layer, made, "at", [P, TOPK, NT], U32)
            u = named(made)
            first = layer.enter_context(nc.semaphore("first_expert_in"))
            table_of_slots(nc, ctx, u, slots_dram)
            with nc.Block() as block:
                @block.sync
                def _(sp):
                    sp.dma_start(u.b1[:, :], a["b1"]).then_inc(first, 16)
                    load_expert(sp, 0, 0, u, a["W1"], a["W2"], first)
                    sp.wait_ge(first, 48)
            with nc.Fori(0, E_ // 2) as i:
                experts(nc, i, u, moe, z_dram, a["W1"], a["W2"], a["b2"], y_dram)
            with nc.Fori(0, B) as b:
                combine(nc, b, u, comb, y_dram, out)



def kernel(**inputs):
    import concourse.bacc as bacc
    from concourse.bass_utils import run_bass_kernel_spmd as run

    x = {k: np.asarray(v) for k, v in inputs.items()}

    def rows(w):
        return np.ascontiguousarray(w.reshape(NC, P, -1).transpose(1, 0, 2))

    def cols(v):
        return np.ascontiguousarray(v.reshape(-1, P).T)

    def grouped(w):
        return np.ascontiguousarray(w.reshape(NC, P, 3, NG, HG * HD).transpose(1, 0, 3, 2, 4).reshape(P, NC, NG, 192))

    by_head = x["L1_ffn_Wqkv"].reshape(D, H, 3, HD).transpose(0, 2, 1, 3)
    arrays = {
        "x": x["L0_attn_x"],
        "wqkv0": grouped(x["L0_attn_w_qkv"].T.reshape(D, 3, H, HD)),
        "wout": rows(x["L0_attn_w_out"].T), "wr": rows(x["L0_ffn_W_r"].T), "wk0": rows(x["L0_ffn_W_k"].T),
        "wv0": rows(x["L0_ffn_W_v"].T), "mur": cols(x["L0_ffn_mu_r"]), "muk": cols(x["L0_ffn_mu_k"]),
        "wq1": rows(x["L1_attn_Wq"]), "wk1": rows(x["L1_attn_Wk"]), "wv1": rows(x["L1_attn_Wv"]),
        "wo1": rows(x["L1_attn_Wo"]), "bq": cols(x["L1_attn_bq"]), "bk": x["L1_attn_bk"][None],
        "bv": x["L1_attn_bv"][None], "bo": x["L1_attn_bo"][None],
        "rft": np.ascontiguousarray(x["L1_attn_random_features"].T),
        "ln1g": cols(x["L1_ffn_ln1_g"]), "ln1b": cols(x["L1_ffn_ln1_b"]),
        "ln2g": cols(x["L1_ffn_ln2_g"]), "ln2b": cols(x["L1_ffn_ln2_b"]),
        "wqkv1": grouped(by_head), "wproj": rows(x["L1_ffn_Wproj"]), "wgate": rows(x["L1_ffn_Wgate"]),
        "W1": x["L1_ffn_W1"], "b1": cols(x["L1_ffn_b1"]), "W2": x["L1_ffn_W2"], "b2": x["L1_ffn_b2"],
    }
    for name, table in constants().items():
        arrays[name[2:]] = table
    nc = bacc.Bacc("TRN2", target_bir_lowering=False, num_devices=1)
    sent, a = {}, {}
    for name, v in arrays.items():
        sent["in_" + name] = np.ascontiguousarray(v)
        a[name] = nc.dram_tensor("in_" + name, v.shape, mybir.dt.from_np(v.dtype), kind="ExternalInput").ap()
    out = nc.dram_tensor("out", (B, T, D), F32, kind="ExternalOutput").ap()
    two_layers(nc, a, out)
    return run(nc, [sent], core_ids=[0]).results[0]["out"]
```

```python
from collections import namedtuple
from contextlib import ExitStack

import numpy as np

import concourse.bass as bass
from concourse import mybir

ALU = mybir.AluOpType
ACT = mybir.ActivationFunctionType
AX = mybir.AxisListType
F32 = mybir.dt.float32
BF16 = mybir.dt.bfloat16
U32 = mybir.dt.uint32

P = 128
B, T, D = 4, 1024, 256
NT = T // P
NC = D // P
H, HD = 16, 16
HG = 4
NG = H // HG
WINDOW = 64
HALF = HD // 2
SCALE = HD ** -0.5
SLOTS = 6
KS = SLOTS * HD
KM = KS + 3
WQ = P + WINDOW
E_, F_, TOPK = 8, 1024, 2
N = B * T
CAP = 2 * N // E_
NF = F_ // P
CT = CAP // P
NEG = -2.0 ** 100
EPS = 1e-5
BANK = 512
DROPPED = 65536.0


def named(things):
    return namedtuple("Named", list(things))(*things.values())


def semaphores(nc, ctx, prefix, names):
    made = {n: ctx.enter_context(nc.semaphore(f"{prefix}_{n}")) for n in names.split()}
    return named(dict(made, all=[h for n, h in made.items() if not n.endswith("_gathered")]))


def clear(nc, sems):
    with nc.Block() as block:
        @block.gpsimd
        def _(pool):
            for s in sems.all:
                pool.sem_clear(s)


def dve_chain(dve, sem):
    count = [0]

    def link(ins):
        count[0] += 1
        ins.then_inc(sem, 1)
        dve.wait_ge(sem, count[0])
    return link



class Script:

    RING = 4

    def __init__(self, windowed):
        def pieces(t, keys):
            if windowed:
                return [((2 * j, 2 * j + 1), 0, 0) for j in range(2)]
            first, last = (0, P * t + P) if keys else (P * t, T)
            cuts = [first] + [c for c in (BANK,) if first < c < last] + [last]
            return [((h,), a, e) for h in range(HG) for a, e in zip(cuts[:-1], cuts[1:])]

        def prep(g):
            out = []
            for k in range(5):
                cuts = [(x, g, k) for x in ("proj", "rot", "high", "rest", "mid", "low")] if k < 4 else []
                turns = [("turn", g, 2 * k - 2), ("turn", g, 2 * k - 1)] if k else []
                out += cuts[:3] + turns[:1] + cuts[3:5] + turns[1:] + cuts[5:]
            return out if g < NG else []

        def maxima(g):
            return [("max", g, t, x) for t in range(NT) for x in pieces(t, True)] + [("rows", g)] if g < NG else []

        def exps(g):
            out = []
            for t in range(NT):
                mine = [("exp", g, t, x) for x in pieces(t, False)]
                out += beside((mine, 1.0), (values(g, t - 1), 1.0)) if t else mine
            return out + values(g, NT - 1) + [("collect", g)]

        def values(g, t):
            end = min(T, P * t + WQ) if windowed else T
            cuts = [P * t] + [c for c in (BANK,) if P * t < c < end] + [end]
            return [("values", g, t, x) for x in zip(cuts[:-1], cuts[1:])]

        def beside(*lists):
            at = [((i + 1) * share / len(x), n, i) for n, (x, share) in enumerate(lists) for i in range(len(x))]
            return [lists[n][0][i] for _, n, i in sorted(at)]

        steps = prep(0) + beside((maxima(0), 1.0), (prep(1), 1.0))
        for g in range(NG):
            before = [("out", g - 1, 0), ("out", g - 1, 1)] if g else []
            steps += beside((exps(g), 1.0), (maxima(g + 1), 0.85), (prep(g + 2), 0.9), (before, 0.3))
        steps += [("out", NG - 1, 0), ("out", NG - 1, 1)]
        self.steps = steps
        self.order, self.bank, self.after = {}, {}, {}
        count, ring = {}, []
        for x in steps:
            kind = {"rows": "turn", "rot": "cut", "high": "cut", "rest": "cut", "mid": "cut", "low": "cut"}.get(x[0], x[0])
            self.order[x] = count[kind] = count.get(kind, -1) + 1
            if kind in ("max", "exp", "out"):
                self.bank[x] = len(ring) % self.RING
                self.after[x] = ring[-self.RING] if len(ring) >= self.RING else None
                ring.append(x)
        self.last_exp = {x[1:3]: self.order[x] for x in steps if x[0] == "exp"}
        self.last_values = {x[1:3]: self.order[x] for x in steps if x[0] == "values"}
        self.first = {}
        for x in steps:
            self.first.setdefault((x[0],) + x[1:3] if x[0] == "exp" else x[:2], x)

    def wait_bank(self, eng, x, s):
        y = self.after[x]
        if y is not None:
            eng.wait_ge({"max": s.max_read, "exp": s.exp_done, "out": s.out_read}[y[0]], self.order[y] + 1)


def attention(nc, b, u, s, windowed, x_dram=None):
    plan = Script(windowed)
    order = plan.order
    w_sb = u.wqkv0 if windowed else u.wqkv1

    def heads_in_bank(x, w):
        return u.psum[:, plan.bank[x], 0:2 * WQ].rearrange("p (h w) -> p h w", h=2)[:, :, 0:w]

    with nc.Block() as block:
        @block.sync
        def _(sp):
            if x_dram is not None:
                for h in range(2):
                    sp.dma_start(u.src[:, 4 * h:4 * h + 4, :], x_dram[bass.ds(b, 1), BANK * h:BANK * (h + 1), :]
                                 .rearrange("o (t p) d -> p (o t) d", p=P)).then_inc(s.src_in, 16)
            for g in range(NG):
                sp.wait_ge(s.tr_read, order[("rows", g)] + 1)
                for j in range(3):
                    sp.dma_start(u.qk[g % 3][KS + j:KS + j + 1, 0:HG, :].rearrange("o h (t q) -> o (h t) q", q=P),
                                 u.mrow[32 * j:32 * j + 32, :]).then_inc(s.m_rows, 16)
            sp.wait_ge(s.m_rows, 48 * NG)

        @block.tensor
        def _(pe):
            if x_dram is not None:
                pe.wait_ge(s.src_in, 32)
            for c in range(NC):
                for h in range(2):
                    for t in range(4):
                        i = pe.transpose(u.psum[:, 2 * c + h, P * t:P * t + P],
                                         u.src[:, 4 * h + t, P * c:P * c + P], u.id32[:, :])
                    i.then_inc(s.xt_ready, 1)
            pe.wait_ge(s.xt_read, 4)

            for x in plan.steps:
                kind, g = x[:2]
                q, n = u.qk[g % 3], order.get(x)
                if kind == "proj":
                    k = x[2]
                    if n:
                        pe.wait_ge(s.pj_read, n)
                    for t in range(2):
                        out = u.pj[:, 0:384].rearrange("p (a t c) -> p a t c", a=3, t=2)[:, :, t, :]
                        for c in range(NC):
                            ins = pe.matmul(out, u.xt[:, c, P * (2 * k + t):P * (2 * k + t + 1)],
                                            w_sb[:, c, g, :].rearrange("p (a c) -> p a c", a=3),
                                            start=(c == 0), stop=(c == NC - 1))
                    ins.then_inc(s.pj_ready, 1)
                elif kind == "turn":
                    t = x[2]
                    if n:
                        pe.wait_ge(s.tr_read, n)
                    pe.wait_ge(s.cut, order[("low", g, t // 2)] + 1)
                    pe.wait_ge(s.repeated, 4 * g + t // 2 + 1)
                    st = u.stack[(t // 2) % 2]
                    for h in range(2 * HG):
                        ins = pe.transpose(u.tr[0:KS, h, :], st[:, h // HG, (t % 2) * HG + h % HG, :], u.id16[:, :])
                    ins.then_inc(s.tr_ready, 1)
                elif kind == "rows":
                    pe.wait_ge(s.tr_read, n)
                    pe.wait_ge(s.m_parts, g + 1)
                    pe.transpose(u.tr[0:KS, 0, :], u.mparts[:, :], u.id16[:, :]).then_inc(s.tr_ready, 1)
                elif kind == "max":
                    t, (heads, a, e) = x[2:]
                    if plan.first[x[:2]] == x:
                        pe.wait_ge(s.tr_read, order[("turn", g, NT - 1)] + 1)
                    plan.wait_bank(pe, x, s)
                    r = u.psum[:, plan.bank[x], :]
                    if windowed:
                        k0, w = max(0, P * t - WINDOW), min(WQ, P * t + P)
                        out = heads_in_bank(x, w)
                        pe.matmul(out, u.id16[:, :], u.mask_q[:, :, WQ - w:WQ], start=True, stop=True,
                                  skip_group_check=True)
                        for h in heads:
                            ins = pe.matmul(out[:, h % 2, :], q[0:KS, h, P * t:P * t + P], q[0:KS, HG + h, k0:k0 + w],
                                            start=False, stop=True, skip_group_check=True)
                    else:
                        h, last = heads[0], e == P * t + P
                        if last:
                            pe.matmul(r[:, P * t - a:P * t - a + P], u.id16[:, :], u.causal_q[:, :], start=True,
                                      stop=True, skip_group_check=True)
                        ins = pe.matmul(r[:, 0:e - a], q[0:KS, h, P * t:P * t + P], q[0:KS, HG + h, a:e],
                                        start=not last, stop=True, skip_group_check=True)
                    ins.then_inc(s.max_ready, 1)
                elif kind == "exp":
                    t, (heads, a, e) = x[2:]
                    if t == 0:
                        pe.wait_ge(s.m_rows, 48 * (g + 1))
                    plan.wait_bank(pe, x, s)
                    r = u.psum[:, plan.bank[x], :]
                    if windowed:
                        q0, w = P * t, min(WQ, T - P * t)
                        out = heads_in_bank(x, w)
                        pe.matmul(out, u.id16[:, :], u.mask_k[:, :, 0:w], start=True, stop=True,
                                  skip_group_check=True)
                        for h in heads:
                            ins = pe.matmul(out[:, h % 2, :], q[0:KM, HG + h, P * t:P * t + P], q[0:KM, h, q0:q0 + w],
                                            start=False, stop=True, skip_group_check=True)
                    else:
                        h, first = heads[0], a == P * t
                        if first:
                            pe.matmul(r[:, 0:P], u.id16[:, :], u.causal_k[:, :], start=True, stop=True,
                                      skip_group_check=True)
                        ins = pe.matmul(r[:, 0:e - a], q[0:KM, HG + h, P * t:P * t + P], q[0:KM, h, a:e],
                                        start=not first, stop=True, skip_group_check=True)
                    ins.then_inc(s.exp_ready, 1)
                elif kind == "values":
                    t, (a, e) = x[2:]
                    pe.wait_ge(s.exp_done, plan.last_exp[(g, t)] + 1)
                    if t == 0 and g:
                        pe.wait_ge(s.o_read, g)
                    first = a in (0, BANK) and (t == 0 or a > P * t) if windowed else t == 0
                    shift = P * t if windowed else 0
                    for h in range(HG):
                        ins = pe.matmul(u.ot[32 * h:32 * h + 32, a:e], u.v[g % 3][:, t, h, :],
                                        u.probs[t % 2][:, h, a - shift:e - shift], start=first, stop=True,
                                        tile_position=(0, 32 * h), skip_group_check=True)
                    ins.then_inc(s.pv_done, 1)
                elif kind == "out":
                    pe.wait_ge(s.o_read, g + 1)
                    plan.wait_bank(pe, x, s)
                    for t in range(4):
                        ins = pe.transpose(u.psum[:, plan.bank[x], P * t:P * t + P],
                                           u.ot_sb[:, BANK * x[2] + P * t:BANK * x[2] + P * t + P], u.id32[:, :])
                    ins.then_inc(s.out_ready, 1)

        @block.scalar
        def _(act):
            for c in range(NC):
                for h in range(2):
                    act.wait_ge(s.xt_ready, 2 * c + h + 1)
                    if windowed:
                        act.activation(u.xt[:, c, BANK * h:BANK * h + BANK], u.psum[:, 2 * c + h, :], ACT.Copy
                                       ).then_inc(s.xt_read, 1)
                    else:
                        act.activation(u.xt[:, c, BANK * h:BANK * h + BANK], u.psum[:, 2 * c + h, :], ACT.Identity,
                                       scale=u.ln1g[:, c:c + 1], bias=u.ln1b[:, c:c + 1]).then_inc(s.xt_read, 1)
            for x in plan.steps:
                kind, g = x[:2]
                n = order.get(x)
                if kind == "exp":
                    t, (heads, a, e) = x[2:]
                    act.wait_ge(s.exp_ready, n + 1)
                    if plan.first[x[:3]] == x and NT * g + t >= 2:
                        back = divmod(NT * g + t - 2, NT)
                        act.wait_ge(s.pv_done, plan.last_values[back] + 1)
                    if windowed:
                        w = min(WQ, T - P * t)
                        act.activation(u.probs[t % 2][:, heads[0]:heads[0] + 2, 0:w], heads_in_bank(x, w),
                                       ACT.Exp, scale=SCALE).then_inc(s.exp_done, 1)
                    else:
                        act.activation(u.probs[t % 2][:, heads[0], a:e], u.psum[:, plan.bank[x], 0:e - a],
                                       ACT.Exp, scale=SCALE).then_inc(s.exp_done, 1)
                elif kind == "turn":
                    t = x[2]
                    act.wait_ge(s.tr_ready, n + 1)
                    act.activation(u.qk[g % 3][0:KS, :, P * t:P * t + P], u.tr[0:KS, :, :], ACT.Copy
                                   ).then_inc(s.tr_read, 1)
                elif kind == "rows":
                    act.wait_ge(s.tr_ready, n + 1)
                    if g:
                        act.wait_ge(s.m_rows, 48 * g)
                    act.activation(u.mrow[0:KS, :], u.tr[0:KS, 0, :], ACT.Copy).then_inc(s.tr_read, 1)
                elif kind == "collect":
                    act.wait_ge(s.pv_done, plan.last_values[(g, NT - 1)] + 1)
                    if g:
                        act.wait_ge(s.out_ready, 2 * g)
                    act.activation(u.ot_sb[:, :], u.ot[:, :], ACT.Copy).then_inc(s.o_read, 1)

        @block.vector
        def _(dve):
            link = dve_chain(dve, s.chain)

            def rotate(x):
                _, g, k = x
                i = order[x]
                dve.wait_ge(s.pj_ready, i + 1)
                if i:
                    dve.wait_ge(s.cut, order[("rot", (i - 1) // 4, (i - 1) % 4)] + 1)
                src = u.pj[:, 0:256].rearrange("p (a y) -> p a y", a=2)
                table = (slice(None), slice(2 * k, 2 * k + 2), slice(None))
                cos = u.cos[table].rearrange("p t y -> p (t y)").unsqueeze(1).broadcast_to([P, 2, P])
                sin = u.sin[table].rearrange("p t (h d) -> p (t h) d", d=HD)
                dve.tensor_tensor(u.ra[:, :, :], src, cos, ALU.mult)
                halves = src.rearrange("p a (h d) -> p a h d", d=HD)
                for y in range(2):
                    dve.tensor_tensor(u.rb[:, :, :].rearrange("p a (h d) -> p a h d", d=HD)[:, :, :, HALF * y:HALF * y + HALF],
                                      halves[:, :, :, HALF * (1 - y):HALF * (1 - y) + HALF],
                                      sin[:, :, HALF * y:HALF * y + HALF].unsqueeze(1).broadcast_to([P, 2, 2 * HG, HALF]),
                                      ALU.mult)
                dve.tensor_copy(u.v[g % 3][:, 2 * k:2 * k + 2, :, 0:HD].rearrange("p t h d -> p (t h) d"),
                                u.pj[:, 256:384].rearrange("p (h d) -> p h d", d=HD)).then_inc(s.pj_read, 1)

            def cut(x):
                kind, g, k = x
                st = u.stack[k % 2][:, :, :, :].rearrange("p a x (s d) -> p (a x) s d", d=HD)
                rot = u.rot[:, :, :].rearrange("p a (h d) -> p (a h) d", d=HD)
                rest = u.rest[:, :, :].rearrange("p a (h d) -> p (a h) d", d=HD)
                half = 2 * HG
                if order[x]:
                    dve.wait_ge(s.cut, order[x])
                if kind == "rot":
                    dve.wait_ge(s.pj_read, order[("proj", g, k)] + 1)
                    ins = dve.tensor_tensor(u.rot[:, :, :], u.ra[:, :, :], u.rb[:, :, :], ALU.add)
                elif kind == "high":
                    i = 4 * g + k - 2
                    if i >= 0:
                        dve.wait_ge(s.tr_ready, order[("turn", i // 4, 2 * (i % 4) + 1)] + 1)
                    ins = dve.tensor_copy(st[:, :, 0, :], rot)
                elif kind == "rest":
                    ins = dve.tensor_tensor(rest, rot, st[:, :, 0, :], ALU.subtract)
                elif kind == "mid":
                    ins = dve.tensor_copy(st[:, :, 3, :], rest)
                else:
                    dve.tensor_tensor(st[:, 0:half, 5, :], rest[:, 0:half, :], st[:, 0:half, 3, :], ALU.subtract)
                    ins = dve.tensor_tensor(st[:, half:2 * half, 2, :], rest[:, half:2 * half, :],
                                            st[:, half:2 * half, 3, :], ALU.subtract)
                ins.then_inc(s.cut, 1)

            def parts_of_maxima(g):
                dve.wait_ge(s.max_read, max(order[y] for y in plan.steps if y[:2] == ("max", g)) + 1)
                m = u.mneg[:, :, :]
                if not windowed:
                    link(dve.tensor_tensor(m[:, :, 4:NT], m[:, :, 4:NT], u.mhalf[:, :, :], ALU.min))
                m = m.rearrange("p h t -> p (h t)")
                if g:
                    dve.wait_ge(s.tr_ready, order[("rows", g - 1)] + 1)
                link(dve.tensor_copy(u.mparts[:, 0:32], m))
                link(dve.tensor_tensor(u.mrest[:, :], m, u.mparts[:, 0:32], ALU.subtract))
                link(dve.tensor_copy(u.mparts[:, 32:64], u.mrest[:, :]))
                dve.tensor_tensor(u.mparts[:, 64:96], u.mrest[:, :], u.mparts[:, 32:64], ALU.subtract
                                  ).then_inc(s.m_parts, 1)
                dve.wait_ge(s.m_parts, g + 1)

            for x in plan.steps:
                kind, g = x[:2]
                n = order.get(x)
                if kind == "proj":
                    rotate(x)
                elif kind in ("rot", "high", "rest", "mid", "low"):
                    cut(x)
                elif kind == "max":
                    t, (heads, a, e) = x[2:]
                    dve.wait_ge(s.max_ready, n + 1)
                    if windowed:
                        ins = dve.tensor_reduce(u.mneg[:, heads[0]:heads[0] + 2, t], heads_in_bank(x, min(WQ, P * t + P)),
                                                AX.X, ALU.max, negate=True)
                    else:
                        h = heads[0]
                        out = u.mneg[:, h, t:t + 1] if e == P * t + P else u.mhalf[:, h, t - 4:t - 3]
                        ins = dve.tensor_reduce(out, u.psum[:, plan.bank[x], 0:e - a], AX.X, ALU.max, negate=True)
                    ins.then_inc(s.max_read, 1)
                elif kind == "rows":
                    parts_of_maxima(g)
                elif kind == "out":
                    y = x[2]
                    dve.wait_ge(s.out_ready, n + 1)
                    r = u.psum[:, plan.bank[x], :].rearrange("p (t h x) -> p t h x", t=4, h=HG)
                    if n:
                        dve.wait_ge(s.out_read, n)
                    link(dve.reciprocal(u.rden[:, :, :], r[:, :, :, HD]))
                    dve.tensor_tensor(
                        u.o[:, 4 * y:4 * y + 4, HG * HD * g:HG * HD * (g + 1)].rearrange("p t (h d) -> p t h d", h=HG),
                        r[:, :, :, 0:HD], u.rden[:, :, :].unsqueeze(3).broadcast_to([P, 4, HG, HD]),
                        ALU.mult).then_inc(s.out_read, 1)

        @block.gpsimd
        def _(pool):
            for i in range(4 * NG):
                st = u.stack[i % 2][:, :, :, :].rearrange("p a x (s d) -> p a x s d", d=HD)
                q, k = st[:, 0, :, :, :], st[:, 1, :, :, :]
                pool.wait_ge(s.cut, order[("high", i // 4, i % 4)] + 1)
                pool.tensor_copy(q[:, :, 1:3, :], q[:, :, 0:1, :].broadcast_to([P, 2 * HG, 2, HD]))
                pool.tensor_copy(k[:, :, 4:6, :], k[:, :, 0:1, :].broadcast_to([P, 2 * HG, 2, HD]))
                pool.wait_ge(s.cut, order[("mid", i // 4, i % 4)] + 1)
                pool.tensor_copy(q[:, :, 4, :], q[:, :, 3, :])
                pool.tensor_copy(k[:, :, 1, :], k[:, :, 3, :]).then_inc(s.repeated, 1)
    clear(nc, s)


ATT_SEMS = ("src_in xt_ready xt_read pj_ready pj_read cut repeated tr_ready tr_read "
            "max_ready max_read m_parts m_rows exp_ready exp_done pv_done o_read out_ready out_read chain")



def constants():
    inv = 1.0 / 10000.0 ** (np.arange(0, HD, 2, dtype=np.float32) / HD)
    angle = (np.arange(T, dtype=np.float32)[:, None] * inv.astype(np.float32)).astype(np.float32)
    cos, sin = np.cos(angle), np.sin(angle)

    def by_tile(x):
        return np.tile(x.reshape(NT, P, HD).transpose(1, 0, 2), HG).astype(np.float32)
    p, w, f = np.arange(P)[:, None], np.arange(WQ)[None], np.arange(P)[None]
    behind = p + WINDOW - w
    mask_q = np.where((behind >= 0) & (behind < WINDOW), 0.0, NEG)
    ahead = w - p
    mask_k = np.where((ahead >= 0) & (ahead < WINDOW), 0.0, NEG)
    return {
        "c_cos": by_tile(np.concatenate([cos, cos], -1)),
        "c_sin": by_tile(np.concatenate([-sin, sin], -1)),
        "c_id32": np.eye(P, dtype=np.float32),
        "c_tables": np.concatenate(
            [np.eye(P), mask_q, mask_q, mask_k, mask_k, np.where(f <= p, 0.0, NEG), np.where(f >= p, 0.0, NEG),
             f >= p], 1).astype(np.float32),
        "c_blocks": (p // HD == f // HD).astype(np.float32),
        "c_iota": np.repeat(np.arange(E_, dtype=np.float32)[None], P, 0),
        "c_token": (P * np.arange(NT)[None] + p).astype(np.uint32),
    }


def sbuf(nc, ctx, made, name, shape, dtype=F32):
    made[name] = ctx.enter_context(nc.sbuf_tensor(f"b_{name}", shape, dtype))


def attention_buffers(nc, ctx, u):
    sbuf(nc, ctx, u, "cos", [P, NT, HG * HD])
    sbuf(nc, ctx, u, "sin", [P, NT, HG * HD])
    sbuf(nc, ctx, u, "id16", [P, P], BF16)
    sbuf(nc, ctx, u, "mask_q", [P, 2, WQ], BF16)
    sbuf(nc, ctx, u, "mask_k", [P, 2, WQ], BF16)
    sbuf(nc, ctx, u, "causal_q", [P, P], BF16)
    sbuf(nc, ctx, u, "causal_k", [P, P], BF16)
    sbuf(nc, ctx, u, "src", [P, NT, D])
    sbuf(nc, ctx, u, "xt", [P, NC, T])
    sbuf(nc, ctx, u, "o", [P, NT, D])
    for name in "ra rb rot rest".split():
        sbuf(nc, ctx, u, name, [P, 2, P])
    sbuf(nc, ctx, u, "mneg", [P, HG, NT])
    sbuf(nc, ctx, u, "mhalf", [P, HG, NT - 4])
    sbuf(nc, ctx, u, "mrest", [P, HG * NT])
    sbuf(nc, ctx, u, "mparts", [P, KS], BF16)
    sbuf(nc, ctx, u, "mrow", [P, P], BF16)
    sbuf(nc, ctx, u, "ot_sb", [P, T])
    sbuf(nc, ctx, u, "rden", [P, 4, HG])
    for name, shape, dtype, n in (("stack", [P, 2, 2 * HG, KS], BF16, 2), ("qk", [P, 2 * HG, T], BF16, 3),
                                  ("v", [P, NT, HG, 32], F32, 3), ("probs", [P, HG, T], F32, 2)):
        for i in range(n):
            sbuf(nc, ctx, u, f"{name}{i}", shape, dtype)
        u[name] = [u[f"{name}{i}"] for i in range(n)]
    psum = u["psum"]
    u["ot"] = psum[:, 4:6, :].rearrange("p a x -> p (a x)")
    u["pj"] = psum[:, 6, :]
    u["tr"] = psum[:, 7, :].bitcast(BF16).rearrange("p (h x) -> p h x", x=P)



def norm_variance(dve, link, y, u, s):
    for t in range(NT):
        ins = dve.bn_stats(u.bn[:, t, :], y[:, t, :])
    link(ins)
    for t in range(NT):
        ins = dve.bn_aggr(u.mv[:, t, :], u.bn[:, t, :])
    link(ins)
    dve.tensor_scalar(u.var[:, :], u.mv[:, :, 1], EPS, None, ALU.add).then_inc(s.var_ready, 1)


def norm_root(act, u, s, k):
    act.wait_ge(s.var_ready, k + 1)
    act.activation(u.lnv[:, :], u.var[:, :], ACT.Ln).then_inc(s.ln_done, 1)
    act.wait_ge(s.ln_done, k + 1)
    act.activation(u.root[:, :], u.lnv[:, :], ACT.Exp, scale=-0.5).then_inc(s.root_ready, 1)


def norm_apply(dve, link, y, out, u, s, k):
    dve.wait_ge(s.root_ready, k + 1)
    link(dve.tensor_tensor(u.nt[:, :], u.root[:, :], u.root[:, :], ALU.mult))
    link(dve.tensor_tensor(u.nt[:, :], u.nt[:, :], u.var[:, :], ALU.mult))
    link(dve.tensor_scalar(u.nt[:, :], u.nt[:, :], -0.5, 1.5, ALU.mult, ALU.add))
    link(dve.tensor_tensor(u.rstd[:, :], u.root[:, :], u.nt[:, :], ALU.mult))
    for t in range(NT):
        ins = dve.tensor_scalar(out[:, t, :], y[:, t, :], u.mv[:, t, 0:1], u.rstd[:, t:t + 1],
                                ALU.subtract, ALU.mult)
    return ins


NORM_SEMS = " var_ready ln_done root_ready chain "


def turn_tiles(pe, src, u, s):
    for c in range(NC):
        for h in range(2):
            for t in range(4):
                ins = pe.transpose(u.psum[:, 2 * c + h, P * t:P * t + P], src[:, 4 * h + t, P * c:P * c + P], u.id32[:, :])
            ins.then_inc(s.turned, 1)


def take_turned(act, dst, u, s, k, gain=None, offset=None):
    for c in range(NC):
        for h in range(2):
            act.wait_ge(s.turned, 4 * k + 2 * c + h + 1)
            d = dst[:, c, BANK * h:BANK * h + BANK]
            if gain is None:
                act.activation(d, u.psum[:, 2 * c + h, :], ACT.Copy).then_inc(s.taken, 1)
            else:
                act.activation(d, u.psum[:, 2 * c + h, :], ACT.Identity, scale=gain[:, c:c + 1],
                               bias=offset[:, c:c + 1]).then_inc(s.taken, 1)


def pair_product(pe, bank, lhs, rhs, k):
    for t in range(2):
        for c in range(NC):
            ins = pe.matmul(bank[:, D * t:D * t + D], lhs[:, c, P * (2 * k + t):P * (2 * k + t + 1)], rhs[:, c, :],
                            start=(c == 0), stop=(c == NC - 1))
    return ins


def bank_pair(u, bank):
    return u.psum[:, bank, :].rearrange("p (t d) -> p t d", t=2)


def pair(x, k):
    return x[:, 2 * k:2 * k + 2, :].rearrange("p t d -> p (t d)")



POST0_SEMS = "turned taken pj_ready y_done x1_ready mix_r mix_k k_ready k_done r_ready r_low r_done v_ready v_done" + NORM_SEMS


def mixing(nc, u, s):
    with nc.Block() as block:
        @block.tensor
        def _(pe):
            turn_tiles(pe, u.o, u, s)
            pe.wait_ge(s.taken, 4)
            for k in range(4):
                if k >= 2:
                    pe.wait_ge(s.y_done, k - 1)
                pair_product(pe, u.psum[:, 4 + k % 2, :], u.xt, u.wout, k).then_inc(s.pj_ready, 1)
            pe.wait_ge(s.x1_ready, 1)
            turn_tiles(pe, u.src, u, s)
            pe.wait_ge(s.taken, 8)
            pe.wait_ge(s.mix_k, 2)
            for c in range(NC):
                for h in range(2):
                    for a in range(NC):
                        ins = pe.matmul(u.psum[:, 2 * c + h, :], u.wk0[:, a, P * c:P * c + P],
                                        u.xk[:, a, BANK * h:BANK * h + BANK], start=(a == 0), stop=(a == NC - 1))
                    ins.then_inc(s.k_ready, 1)
            pe.wait_ge(s.mix_r, 2)
            for k in range(4):
                if k >= 2:
                    pe.wait_ge(s.r_low, k - 1)
                pair_product(pe, u.psum[:, 4 + k % 2, :], u.xr, u.wr, k).then_inc(s.r_ready, 1)
            pe.wait_ge(s.k_done, 4)
            for k in range(4):
                if k >= 2:
                    pe.wait_ge(s.v_done, k - 1)
                pair_product(pe, u.psum[:, 6 + k % 2, :], u.xt, u.wv0, k).then_inc(s.v_ready, 1)

        @block.scalar
        def _(act):
            take_turned(act, u.xt, u, s, 0)
            norm_root(act, u, s, 0)
            take_turned(act, u.x1t[:, :, 1:T + 1], u, s, 1)
            for k in range(4):
                act.wait_ge(s.r_low, k + 1)
                act.activation(pair(u.r, k), pair(u.r, k), ACT.Exp, scale=-1.0).then_inc(s.r_done, 1)
            norm_root(act, u, s, 1)

        @block.vector
        def _(dve):
            link = dve_chain(dve, s.chain)
            link(dve.memset(u.x1t[:, :, 0:1], 0.0))
            for k in range(4):
                dve.wait_ge(s.pj_ready, k + 1)
                dve.tensor_tensor(pair(u.y, k), u.psum[:, 4 + k % 2, :], pair(u.src, k), ALU.add).then_inc(s.y_done, 1)
            dve.wait_ge(s.y_done, 4)
            norm_variance(dve, link, u.y, u, s)
            norm_apply(dve, link, u.y, u.src, u, s, 0).then_inc(s.x1_ready, 1)
            dve.wait_ge(s.taken, 8)
            link(dve.tensor_tensor(u.dx[:, :, :], u.x1t[:, :, 1:T + 1], u.x1t[:, :, 0:T], ALU.subtract))
            for c in range(NC):
                dve.scalar_tensor_tensor(u.xk[:, c, :], u.dx[:, c, :], u.muk[:, c:c + 1], u.x1t[:, c, 0:T],
                                         ALU.mult, ALU.add).then_inc(s.mix_k, 1)
            for c in range(NC):
                dve.scalar_tensor_tensor(u.xr[:, c, :], u.dx[:, c, :], u.mur[:, c:c + 1], u.x1t[:, c, 0:T],
                                         ALU.mult, ALU.add).then_inc(s.mix_r, 1)
            for c in range(NC):
                for h in range(2):
                    j = 2 * c + h
                    dve.wait_ge(s.k_ready, j + 1)
                    link(dve.tensor_scalar(pair(u.y, j), u.psum[:, j, :], 0.0, None, ALU.max))
                    dve.tensor_tensor(u.xt[:, c, BANK * h:BANK * h + BANK], pair(u.y, j), pair(u.y, j), ALU.mult
                                      ).then_inc(s.k_done, 1)
            for k in range(4):
                dve.wait_ge(s.r_ready, k + 1)
                dve.tensor_scalar(pair(u.r, k), u.psum[:, 4 + k % 2, :], -87.0, None, ALU.max).then_inc(s.r_low, 1)
            for k in range(4):
                dve.wait_ge(s.r_done, k + 1)
                link(dve.tensor_scalar(pair(u.r, k), pair(u.r, k), 1.0, None, ALU.add))
                link(dve.reciprocal(pair(u.r, k), pair(u.r, k)))
                dve.wait_ge(s.v_ready, k + 1)
                dve.tensor_tensor(pair(u.r, k), u.psum[:, 6 + k % 2, :], pair(u.r, k), ALU.mult).then_inc(s.v_done, 1)
                dve.wait_ge(s.v_done, k + 1)
                ins = dve.tensor_tensor(pair(u.y, k), pair(u.r, k), pair(u.src, k), ALU.add)
            link(ins)
            norm_variance(dve, link, u.y, u, s)
            link(norm_apply(dve, link, u.y, u.src, u, s, 1))
    clear(nc, s)



LIN_SEMS = ("turned taken q_ready q_min q_exp q_done k_ready k_add k_min k_exp k_done v_ready v_done kv_ready kvm_done "
            "m_ready m_done a_ready a_done out_ready y_done res_ready") + NORM_SEMS


def linear_attention(nc, u, s):
    with nc.Block() as block:
        @block.tensor
        def _(pe):
            turn_tiles(pe, u.src, u, s)
            pe.wait_ge(s.taken, 4)
            for c in range(NC):
                for h in range(2):
                    for a in range(NC):
                        ins = pe.matmul(u.psum[:, 2 * c + h, :], u.wq1[:, a, P * c:P * c + P],
                                        u.xt[:, a, BANK * h:BANK * h + BANK], start=(a == 0), stop=(a == NC - 1))
                    ins.then_inc(s.q_ready, 1)
            for k in range(4):
                if k >= 2:
                    pe.wait_ge(s.k_add, k - 1)
                    pe.wait_ge(s.v_done, k - 1)
                pair_product(pe, u.psum[:, 4 + k % 2, :], u.xt, u.wk1, k).then_inc(s.k_ready, 1)
                pair_product(pe, u.psum[:, 6 + k % 2, :], u.xt, u.wv1, k).then_inc(s.v_ready, 1)
            pe.wait_ge(s.k_done, 4)
            pe.wait_ge(s.v_done, 4)
            for c in range(NC):
                for t in range(NT):
                    ins = pe.matmul(u.psum[:, 4, P * c:P * c + P], u.o[:, t, P * c:P * c + P], u.y[:, t, P * c:P * c + P],
                                    start=(t == 0), stop=(t == NT - 1))
            ins.then_inc(s.kv_ready, 1)
            pe.wait_ge(s.kvm_done, 1)
            for c in range(NC):
                ins = pe.matmul(u.psum[:, 5, P * c:P * c + P], u.kvm[:, c, :], u.bg[:, :], start=True, stop=True)
            ins.then_inc(s.m_ready, 1)
            pe.wait_ge(s.m_done, 1)
            for c in range(NC):
                ins = pe.matmul(u.psum[:, 6, D * c:D * c + D], u.mt[:, c, :], u.wo1[:, c, :], start=True, stop=True)
            ins.then_inc(s.a_ready, 1)
            pe.wait_ge(s.a_done, 1)
            pe.wait_ge(s.q_done, 4)
            for k in range(4):
                pair_product(pe, u.psum[:, k, :], u.phq, u.am, k).then_inc(s.out_ready, 1)

        @block.scalar
        def _(act):
            take_turned(act, u.xt, u, s, 0)
            for j in range(4):
                act.wait_ge(s.q_min, j + 1)
                d = (slice(None), j // 2, slice(BANK * (j % 2), BANK * (j % 2) + BANK))
                act.activation(u.qexp[d], u.qexp[d], ACT.Exp).then_inc(s.q_exp, 1)
            for k in range(4):
                act.wait_ge(s.k_min, k + 1)
                act.activation(pair(u.o, k), pair(u.o, k), ACT.Exp).then_inc(s.k_exp, 1)
            act.wait_ge(s.m_ready, 1)
            act.activation(u.mt[:, :, :].rearrange("p c x -> p (c x)"), u.psum[:, 5, 0:D], ACT.Copy).then_inc(s.m_done, 1)
            act.wait_ge(s.a_ready, 1)
            act.activation(u.am[:, :, :].rearrange("p c x -> p (c x)"), u.psum[:, 6, :], ACT.Copy).then_inc(s.a_done, 1)
            norm_root(act, u, s, 0)
            norm_root(act, u, s, 1)

        @block.gpsimd
        def _(pool):
            pool.wait_ge(s.turned, 4)
            pool.tensor_tensor(u.src[:, :, :], u.src[:, :, :], u.bo[:, :].unsqueeze(1).broadcast_to([P, NT, D]),
                               ALU.add).then_inc(s.res_ready, 1)

        @block.vector
        def _(dve):
            link = dve_chain(dve, s.chain)

            def span(j):
                return (slice(None), j // 2, slice(BANK * (j % 2), BANK * (j % 2) + BANK))
            for j in range(4):
                dve.wait_ge(s.q_ready, j + 1)
                dve.tensor_scalar(u.qexp[span(j)], u.psum[:, j, :], u.bq[:, j // 2:j // 2 + 1], 0.0, ALU.add, ALU.min
                                  ).then_inc(s.q_min, 1)
            for k in range(4):
                dve.wait_ge(s.k_ready, k + 1)
                dve.tensor_tensor(u.kx[:, 2 * k:2 * k + 2, :], bank_pair(u, 4 + k % 2),
                                  u.bk[:, :].unsqueeze(1).broadcast_to([P, 2, D]), ALU.add).then_inc(s.k_add, 1)
                dve.wait_ge(s.k_add, k + 1)
                dve.tensor_scalar(pair(u.o, k), pair(u.kx, k), 0.0, None, ALU.min).then_inc(s.k_min, 1)
                dve.wait_ge(s.v_ready, k + 1)
                dve.tensor_tensor(u.y[:, 2 * k:2 * k + 2, :], bank_pair(u, 6 + k % 2),
                                  u.bv[:, :].unsqueeze(1).broadcast_to([P, 2, D]), ALU.add).then_inc(s.v_done, 1)
                dve.wait_ge(s.q_exp, k + 1)
                dve.scalar_tensor_tensor(u.phq[span(k)], u.psum[:, k, :], u.bq_plus[:, k // 2:k // 2 + 1],
                                         u.qexp[span(k)], ALU.add, ALU.max).then_inc(s.q_done, 1)
            for k in range(4):
                dve.wait_ge(s.k_exp, k + 1)
                dve.scalar_tensor_tensor(pair(u.o, k), pair(u.kx, k), 1.0, pair(u.o, k), ALU.add, ALU.max
                                         ).then_inc(s.k_done, 1)
            dve.wait_ge(s.kv_ready, 1)
            dve.tensor_tensor(u.kvm[:, :, :], u.psum[:, 4, 0:D].rearrange("p (c x) -> p c x", c=NC),
                              u.blocks[:, :].unsqueeze(1).broadcast_to([P, NC, P]), ALU.mult).then_inc(s.kvm_done, 1)
            dve.wait_ge(s.res_ready, 1)
            dve.wait_ge(s.kv_ready, 1)
            for k in range(4):
                dve.wait_ge(s.out_ready, k + 1)
                ins = dve.tensor_tensor(pair(u.y, k), u.psum[:, k, :], pair(u.src, k), ALU.add)
            link(ins)
            norm_variance(dve, link, u.y, u, s)
            link(norm_apply(dve, link, u.y, u.x3, u, s, 0))
            norm_variance(dve, link, u.x3, u, s)
            link(norm_apply(dve, link, u.x3, u.src, u, s, 1))
    clear(nc, s)



ROUTE_SEMS = ("turned taken pj_ready y_done x4_ready z_ready z_out lg_ready shifted exp_done mask_ready pos_ready "
              "slots_ready slots_gathered") + NORM_SEMS


def route(nc, b, u, s, z_dram, x4_dram, slots_dram):
    with nc.Block() as block:
        @block.sync
        def _(sp):
            sp.wait_ge(s.z_ready, 1)
            sp.dma_start(z_dram[bass.ds(b * T, T), :].rearrange("(t p) d -> p t d", p=P), u.src[:, :, :]
                         ).then_inc(s.z_out, 16)
            sp.wait_ge(s.x4_ready, 1)
            sp.dma_start(x4_dram[bass.ds(b * T, T), :].rearrange("(t p) d -> p t d", p=P), u.x3[:, :, :]
                         ).then_inc(s.z_out, 16)
            sp.wait_ge(s.z_out, 32)

        @block.tensor
        def _(pe):
            turn_tiles(pe, u.o, u, s)
            pe.wait_ge(s.taken, 4)
            for k in range(4):
                if k >= 2:
                    pe.wait_ge(s.y_done, k - 1)
                pair_product(pe, u.psum[:, 4 + k % 2, :], u.xt, u.wproj, k).then_inc(s.pj_ready, 1)
            pe.wait_ge(s.z_ready, 1)
            turn_tiles(pe, u.src, u, s)
            pe.wait_ge(s.taken, 8)
            for t in range(NT):
                for c in range(NC):
                    ins = pe.matmul(u.psum[:, 6, E_ * t:E_ * t + E_], u.xt[:, c, P * t:P * t + P], u.wgate[:, c, :],
                                    start=(c == 0), stop=(c == NC - 1))
            ins.then_inc(s.lg_ready, 1)
            pe.wait_ge(s.mask_ready, 1)
            for t in range(NT):
                out = u.psum[:, 7, E_ * t:E_ * t + E_]
                pe.matmul(out, u.upto[:, :], u.chosen[:, t, :], start=True, stop=False)
                for a in range(t):
                    pe.matmul(out, u.ones16[:, :], u.chosen[:, a, :], start=False, stop=False)
                ins = pe.matmul(out, u.ones16[:, :], u.before[:, :], start=False, stop=True)
            ins.then_inc(s.pos_ready, 1)

        @block.scalar
        def _(act):
            take_turned(act, u.xt, u, s, 0)
            norm_root(act, u, s, 0)
            take_turned(act, u.xt, u, s, 1, u.ln2g, u.ln2b)
            act.wait_ge(s.shifted, 1)
            act.activation(u.gexp[:, :, :], u.gexp[:, :, :], ACT.Exp).then_inc(s.exp_done, 1)

        @block.vector
        def _(dve):
            link = dve_chain(dve, s.chain)
            for k in range(4):
                dve.wait_ge(s.pj_ready, k + 1)
                dve.tensor_tensor(pair(u.y, k), u.psum[:, 4 + k % 2, :], pair(u.x3, k), ALU.add).then_inc(s.y_done, 1)
            dve.wait_ge(s.y_done, 4)
            norm_variance(dve, link, u.y, u, s)
            norm_apply(dve, link, u.y, u.src, u, s, 0).then_inc(s.z_ready, 1)
            dve.wait_ge(s.lg_ready, 1)
            lg, top = u.lg, u.top
            link(dve.tensor_copy(lg[:, :, :].rearrange("p t e -> p (t e)"), u.psum[:, 6, 0:NT * E_]))
            for t in range(NT):
                ins = dve.max(top[:, t, :], lg[:, t, :])
            link(ins)
            dve.tensor_tensor(u.gexp[:, :, :], lg[:, :, :], top[:, :, 0:1].broadcast_to([P, NT, E_]), ALU.subtract
                              ).then_inc(s.shifted, 1)
            for t in range(NT):
                ins = dve.max_index(u.topi[:, t, :], top[:, t, :], lg[:, t, :])
            link(ins)
            link(dve.tensor_copy(u.expert[:, :, :].rearrange("p k t -> p t k"), u.topi[:, :, 0:TOPK]))
            for k in range(TOPK):
                ins = dve.tensor_tensor(u.is_it[:, k, :, :], u.iota[:, :].unsqueeze(1).broadcast_to([P, NT, E_]),
                                        u.expert[:, k, :].unsqueeze(2).broadcast_to([P, NT, E_]), ALU.is_equal)
            link(ins)
            dve.tensor_tensor(u.chosen[:, :, :], u.is_it[:, 0, :, :], u.is_it[:, 1, :, :], ALU.add
                              ).then_inc(s.mask_ready, 1)
            dve.wait_ge(s.exp_done, 1)
            link(dve.tensor_reduce(u.gsum[:, :], u.gexp[:, :, :], AX.X, ALU.add))
            dve.reciprocal(u.gsum[:, :], u.gsum[:, :])
            for k in range(TOPK):
                ins = dve.tensor_tensor(u.pick[:, k, :, :], u.is_it[:, k, :, :], u.gexp[:, :, :], ALU.mult)
            link(ins)
            link(dve.tensor_reduce(u.gate[:, :, :], u.pick[:, :, :, :], AX.X, ALU.add))
            link(dve.tensor_tensor(u.gate[:, :, :], u.gate[:, :, :], u.gsum[:, :].unsqueeze(1).broadcast_to([P, TOPK, NT]),
                                   ALU.mult))
            dve.wait_ge(s.pos_ready, 1)
            pos = u.psum[:, 7, 0:NT * E_].rearrange("p (t e) -> p t e", e=E_)
            for k in range(TOPK):
                ins = dve.tensor_tensor(u.pick[:, k, :, :], u.is_it[:, k, :, :], pos, ALU.mult)
            link(ins)
            link(dve.tensor_reduce(u.place[:, :, :], u.pick[:, :, :, :], AX.X, ALU.add))
            link(dve.tensor_scalar(u.keep[:, :, :], u.place[:, :, :], float(CAP), None, ALU.is_le))
            link(dve.tensor_scalar(u.place[:, :, :], u.place[:, :, :], float(CAP), -1.0, ALU.min, ALU.add))
            link(dve.scalar_tensor_tensor(u.place[:, :, :], u.expert[:, :, :], float(CAP), u.place[:, :, :],
                                          ALU.mult, ALU.add))
            dve.tensor_copy(u.read_at[:, :, bass.ds(b * NT, NT)], u.place[:, :, :])
            dve.tensor_tensor(u.gates[:, :, bass.ds(b * NT, NT)], u.gate[:, :, :], u.keep[:, :, :], ALU.mult)
            link(dve.tensor_scalar(u.keep[:, :, :], u.keep[:, :, :], -DROPPED, DROPPED, ALU.mult, ALU.add))
            dve.tensor_tensor(u.write_at[:, :, :], u.place[:, :, :], u.keep[:, :, :], ALU.add).then_inc(s.slots_ready, 1)
            link(dve.tensor_reduce(u.count[:, :], u.chosen[:, :, :].rearrange("p t e -> p e t"), AX.X, ALU.add))
            link(dve.tensor_tensor(u.before[:, :], u.before[:, :], u.count[:, :], ALU.add))
            dve.wait_ge(s.slots_gathered, 16 * TOPK * NT * (b + 1))
            link(dve.tensor_scalar(u.token[:, :], u.token[:, :], float(T), None, ALU.add))

        @block.gpsimd
        def _(pool):
            pool.wait_ge(s.y_done, 4)
            pool.tensor_tensor(u.x3[:, :, :], u.y[:, :, :], u.x3[:, :, :], ALU.add).then_inc(s.x4_ready, 1)
            pool.wait_ge(s.slots_ready, 1)
            for k in range(TOPK):
                for t in range(NT):
                    pool.indirect_dma_start(
                        out=slots_dram, out_offset=bass.IndirectOffsetOnAxis(ap=u.write_at[:, k, t:t + 1], axis=0),
                        in_=u.token[:, t:t + 1], in_offset=None, bounds_check=E_ * CAP - 1, oob_is_err=False
                    ).then_inc(s.slots_gathered, 16)
            pool.wait_ge(s.slots_gathered, 16 * TOPK * NT * (b + 1))
    clear(nc, s)



MOE_SEMS = ("sliced w0_in w1_in x0_gathered x1_gathered b2_in turned taken h_ready h_done y_ready y_done y0_out y1_out")


def load_expert(eng, e, j, u, w1_dram, w2_dram, sem):
    eng.dma_start(u.w1[j][:, :, :], w1_dram[bass.ds(e, 1), :, :].rearrange("o (c p) f -> p (o c) f", p=P)).then_inc(sem, 16)
    eng.dma_start(u.w2[j][:, :, :], w2_dram[bass.ds(e, 1), :, :].rearrange("o (n p) d -> p (o n) d", p=P)).then_inc(sem, 16)


def experts(nc, i, u, s, z_dram, w1_dram, w2_dram, b2_dram, y_dram):
    with nc.Block() as block:
        @block.sync
        def _(sp):
            load_expert(sp, 2 * i + 1, 1, u, w1_dram, w2_dram, s.w1_in)
            for j in range(2):
                sp.dma_start(u.b2b[j][:, :], b2_dram[bass.ds(2 * i + j, 1), :].partition_broadcast(P)
                             .rearrange("p o d -> p (o d)")).then_inc(s.b2_in, 16)
            for q in range(CT):
                if q == CT // 2:
                    sp.wait_ge(s.y_ready, CT // 2)
                    load_expert(sp, (2 * i + 2) % E_, 0, u, w1_dram, w2_dram, s.w0_in)
                sp.wait_ge(s.y_done, q + 1)
                sp.dma_start(y_dram[bass.ds(2 * CAP * i + 2 * P * q, 2 * P), :].rearrange("(t p) d -> p t d", p=P),
                             u.ye[q % 2][:, :, :]).then_inc((s.y0_out, s.y1_out)[q % 2], 16)
            sp.wait_ge(s.w0_in, 32)
            for q in range(2):
                sp.wait_ge((s.y0_out, s.y1_out)[q], 16 * CT // 2)

        @block.gpsimd
        def _(pool):
            pool.wait_ge(s.sliced, 1)
            for j in range(2):
                for t in range(CT):
                    pool.indirect_dma_start(
                        out=u.xg[j][:, t, :], out_offset=None, in_=z_dram,
                        in_offset=bass.IndirectOffsetOnAxis(ap=u.ids[:, j * CT + t:j * CT + t + 1], axis=0),
                        bounds_check=N - 1, oob_is_err=True).then_inc((s.x0_gathered, s.x1_gathered)[j], 16)

        @block.tensor
        def _(pe):
            def turn(j):
                if j:
                    pe.wait_ge(s.h_done, 16 * j)
                pe.wait_ge((s.x0_gathered, s.x1_gathered)[j], 16 * CT * (i + 1))
                for c in range(NC):
                    for h in range(2):
                        for t in range(4):
                            ins = pe.transpose(u.psum[:, 2 * c + h, P * t:P * t + P],
                                               u.xg[j][:, 4 * h + t, P * c:P * c + P], u.id32[:, :])
                        ins.then_inc(s.turned, 1)

            for j in range(2):
                turn(j)
                pe.wait_ge(s.taken, 4 * (j + 1))
                if j:
                    pe.wait_ge(s.w1_in, 32)
                for n in range(NF):
                    for h in range(2):
                        k = 2 * n + h
                        if k >= 4:
                            pe.wait_ge(s.h_done, 16 * j + k - 3)
                        for c in range(NC):
                            ins = pe.matmul(u.psum[:, k % 4, :], u.w1[j][:, c, P * n:P * n + P],
                                            u.xgt[:, c, BANK * h:BANK * h + BANK], start=(c == 0), stop=(c == NC - 1))
                        ins.then_inc(s.h_ready, 1)
                pe.wait_ge(s.h_done, 16 * (j + 1))
                for k in range(CT // 2):
                    q = CT // 2 * j + k
                    if q >= 4:
                        pe.wait_ge(s.y_done, q - 3)
                    for t in range(2):
                        for n in range(NF):
                            ins = pe.matmul(u.psum[:, 4 + k, D * t:D * t + D],
                                            u.hid[:, n, P * (2 * k + t):P * (2 * k + t + 1)], u.w2[j][:, n, :],
                                            start=(n == 0), stop=(n == NF - 1))
                    ins.then_inc(s.y_ready, 1)

        @block.scalar
        def _(act):
            for j in range(2):
                for c in range(NC):
                    for h in range(2):
                        act.wait_ge(s.turned, 4 * j + 2 * c + h + 1)
                        act.activation(u.xgt[:, c, BANK * h:BANK * h + BANK], u.psum[:, 2 * c + h, :], ACT.Identity,
                                       scale=u.ln2g[:, c:c + 1], bias=u.ln2b[:, c:c + 1]).then_inc(s.taken, 1)
                if j:
                    act.wait_ge(s.y_ready, 4 * j)
                for n in range(NF):
                    for h in range(2):
                        k = 2 * n + h
                        act.wait_ge(s.h_ready, 16 * j + k + 1)
                        act.activation(u.hid[:, n, BANK * h:BANK * h + BANK], u.psum[:, k % 4, :], ACT.Gelu,
                                       bias=u.b1s[:, j * NF + n:j * NF + n + 1]).then_inc(s.h_done, 1)

        @block.vector
        def _(dve):
            dve.tensor_copy(u.ids[:, :], u.slots[:, bass.ds(2 * CT * i, 2 * CT)])
            dve.tensor_copy(u.b1s[:, :], u.b1[:, bass.ds(2 * NF * i, 2 * NF)]).then_inc(s.sliced, 1)
            dve.wait_ge(s.b2_in, 32)
            for q in range(CT):
                j, k = divmod(q, CT // 2)
                dve.wait_ge(s.y_ready, q + 1)
                if q >= 2:
                    dve.wait_ge((s.y0_out, s.y1_out)[q % 2], 16 * (q // 2))
                dve.tensor_tensor(u.ye[q % 2][:, :, :], u.psum[:, 4 + k, :].rearrange("p (t d) -> p t d", t=2),
                                  u.b2b[j][:, :].unsqueeze(1).broadcast_to([P, 2, D]), ALU.add).then_inc(s.y_done, 1)
    clear(nc, s)



COMBINE_SEMS = "sliced x4_in r0_gathered r1_gathered r2_gathered r3_gathered r4_gathered r5_gathered r6_gathered r7_gathered sum_done out_ready out_done" + NORM_SEMS


def combine(nc, b, u, s, x4_dram, y_dram, out_dram):
    gathered = (s.r0_gathered, s.r1_gathered, s.r2_gathered, s.r3_gathered, s.r4_gathered, s.r5_gathered,
                s.r6_gathered, s.r7_gathered)
    with nc.Block() as block:
        @block.gpsimd
        def _(pool):
            pool.wait_ge(s.sliced, 1)
            for t in range(NT):
                for k in range(TOPK):
                    pool.indirect_dma_start(
                        out=u.rows[:, TOPK * t + k, :], out_offset=None, in_=y_dram,
                        in_offset=bass.IndirectOffsetOnAxis(ap=u.at[:, k, t:t + 1], axis=0),
                        bounds_check=E_ * CAP - 1, oob_is_err=True).then_inc(gathered[t], 16)

        @block.scalar
        def _(act):
            norm_root(act, u, s, 0)

        @block.vector
        def _(dve):
            link = dve_chain(dve, s.chain)
            dve.tensor_copy(u.at[:, :, :], u.read_at[:, :, bass.ds(b * NT, NT)]).then_inc(s.sliced, 1)
            link(dve.tensor_copy(u.gate[:, :, :], u.gates[:, :, bass.ds(b * NT, NT)]))
            dve.wait_ge(s.x4_in, 16)
            for t in range(NT):
                dve.wait_ge(gathered[t], 16 * TOPK * (b + 1))
                for k in range(TOPK):
                    dve.scalar_tensor_tensor(u.y[:, t, :], u.rows[:, TOPK * t + k, :], u.gate[:, k, t:t + 1],
                                             u.y[:, t, :], ALU.mult, ALU.add).then_inc(s.sum_done, 1)
                    dve.wait_ge(s.sum_done, TOPK * t + k + 1)
            norm_variance(dve, link, u.y, u, s)
            norm_apply(dve, link, u.y, u.y, u, s, 0).then_inc(s.out_ready, 1)

        @block.sync
        def _(sp):
            sp.dma_start(u.y[:, :, :], x4_dram[bass.ds(b * T, T), :].rearrange("(t p) d -> p t d", p=P)
                         ).then_inc(s.x4_in, 16)
            sp.wait_ge(s.out_ready, 1)
            sp.dma_start(out_dram[bass.ds(b, 1), :, :].rearrange("o (t p) d -> p (o t) d", p=P), u.y[:, :, :]
                         ).then_inc(s.out_done, 16)
            sp.wait_ge(s.out_done, 16)
    clear(nc, s)



def lasting_buffers(nc, ctx, u):
    for name, shape, dtype in (
            ("y", [P, NT, D], F32), ("id32", [P, P], F32),
            ("gates", [P, TOPK, B * NT], F32), ("read_at", [P, TOPK, B * NT], U32), ("gate", [P, TOPK, NT], F32),
            ("bn", [P, NT, 6], F32), ("mv", [P, NT, 2], F32), ("var", [P, NT], F32), ("lnv", [P, NT], F32),
            ("root", [P, NT], F32), ("nt", [P, NT], F32), ("rstd", [P, NT], F32),
            ("ln2g", [P, NC], F32), ("ln2b", [P, NC], F32)):
        sbuf(nc, ctx, u, name, shape, dtype)
    u["psum"] = ctx.enter_context(nc.psum_tensor("b_psum", [P, 8, BANK], F32))


def layer_buffers(nc, ctx, u):
    for name in "wout wr wk0 wv0 wq1 wk1 wv1 wo1 wproj".split():
        sbuf(nc, ctx, u, name, [P, NC, D])
    sbuf(nc, ctx, u, "wqkv0", [P, NC, NG, 192])
    sbuf(nc, ctx, u, "wqkv1", [P, NC, NG, 192])
    sbuf(nc, ctx, u, "wgate", [P, NC, E_])
    for name in "mur muk bq bq_plus ln1g ln1b".split():
        sbuf(nc, ctx, u, name, [P, NC])
    for name in "bk bv bo".split():
        sbuf(nc, ctx, u, name, [P, D])
    sbuf(nc, ctx, u, "rft", [64, P])
    sbuf(nc, ctx, u, "blocks", [P, P])
    sbuf(nc, ctx, u, "bg", [P, P])
    sbuf(nc, ctx, u, "kvm", [P, NC, P])
    sbuf(nc, ctx, u, "mt", [P, NC, P])
    sbuf(nc, ctx, u, "am", [P, NC, D])
    sbuf(nc, ctx, u, "x3", [P, NT, D])
    for name, shape, dtype in (
            ("lg", [P, NT, E_], F32), ("top", [P, NT, 8], F32), ("topi", [P, NT, 8], U32), ("gexp", [P, NT, E_], F32),
            ("expert", [P, TOPK, NT], F32), ("is_it", [P, TOPK, NT, E_], F32), ("pick", [P, TOPK, NT, E_], F32),
            ("place", [P, TOPK, NT], F32), ("keep", [P, TOPK, NT], F32), ("write_at", [P, TOPK, NT], U32),
            ("gsum", [P, NT], F32), ("count", [P, E_], F32), ("chosen", [P, NT, E_], BF16), ("before", [P, E_], BF16),
            ("token", [P, NT], U32), ("iota", [P, E_], F32), ("upto", [P, P], BF16), ("ones16", [P, P], BF16),
            ("no_token", [E_ * CAP // P, P], U32)):
        sbuf(nc, ctx, u, name, shape, dtype)
    def part(i, j):
        return u["probs"][i][:, 2 * j:2 * j + 2, :]

    def tiles(x):
        return x.rearrange("p a (t d) -> p (a t) d", d=D)
    flat = u["probs"][0][:, :, :].rearrange("p h t -> p (h t)")
    u["x1t"] = flat[:, 0:NC * (T + 1)].rearrange("p (c t) -> p c t", c=NC)
    u["xk"], u["xr"] = part(1, 0), part(1, 1)
    u["r"] = u["o"]
    u["dx"] = u["o"][:, :, :].rearrange("p (c a) d -> p c (a d)", c=NC)
    u["qexp"], u["phq"], u["kx"] = part(0, 0), part(0, 1), tiles(part(1, 0))


def set_up(nc, ctx, made, a, slots_dram):
    u = named(made)
    loaded = ctx.enter_context(nc.semaphore("weights_in"))
    zeroed = ctx.enter_context(nc.semaphore("zeroed"))
    fixed = ctx.enter_context(nc.semaphore("fixed"))
    gram = ctx.enter_context(nc.semaphore("gram_ready"))
    names = ("wqkv0 wout wr wk0 wv0 mur muk wq1 wk1 wv1 wo1 wproj wqkv1 wgate bq ln1g ln1b ln2g ln2b "
             "cos sin id32 blocks iota token").split()
    count = len(names) + 4 + P // HD
    bf16_tables = (u.id16[:, :], u.mask_q[:, :, :], u.mask_k[:, :, :], u.causal_q[:, :], u.causal_k[:, :], u.upto[:, :])
    width = [P, 2 * WQ, 2 * WQ, P, P, P]
    tables = u.y[:, :, :].rearrange("p t d -> p (t d)")[:, 0:sum(width)]
    with nc.Block() as block:
        @block.sync
        def _(sp):
            for n in names:
                sp.dma_start(made[n][:], a[n]).then_inc(loaded, 16)
            sp.dma_start(tables, a["tables"]).then_inc(loaded, 16)
            for n in ("bk", "bv", "bo"):
                sp.dma_start(made[n][:, :], a[n].partition_broadcast(P).rearrange("p o d -> p (o d)")).then_inc(loaded, 16)
            for j in range(P // HD):
                sp.dma_start(u.rft[:, HD * j:HD * j + HD], a["rft"]).then_inc(loaded, 16)
            sp.wait_ge(zeroed, 1)
            sp.dma_start(slots_dram.rearrange("(r p) o -> r (p o)", p=P), u.no_token[:, :]).then_inc(loaded, 16)
            sp.wait_ge(loaded, 16 * (count + 1))

        @block.vector
        def _(dve):
            dve.memset(u.no_token[:, :], 0).then_inc(zeroed, 1)
            for i in range(3):
                dve.memset(u.v[i][:, :, :, HD:32], 1.0)
                dve.memset(u.qk[i][KS:KS + 32, HG:2 * HG, :], 1.0)
            dve.memset(u.before[:, :], 0.0)
            dve.memset(u.ones16[:, :], 1.0)
            dve.wait_ge(loaded, 16 * (count + 1))
            for i, t in enumerate(bf16_tables):
                part = tables[:, sum(width[:i]):sum(width[:i + 1])]
                dve.tensor_copy(t, part if width[i] == P else part.rearrange("p (h w) -> p h w", h=2))
            dve.tensor_scalar(u.bq_plus[:, :], u.bq[:, :], 1.0, None, ALU.add).then_inc(fixed, 1)
            dve.wait_ge(gram, 1)
            dve.tensor_tensor(u.bg[:, :], u.psum[:, 0, 0:P], u.blocks[:, :], ALU.mult).then_inc(fixed, 1)

        @block.tensor
        def _(pe):
            pe.wait_ge(loaded, 16 * (count + 1))
            pe.matmul(u.psum[:, 0, 0:P], u.rft[:, :], u.rft[:, :], start=True, stop=True).then_inc(gram, 1)


def table_of_slots(nc, ctx, u, slots_dram):
    s = semaphores(nc, ctx, "table", "read floats turned taken")
    with nc.Block() as block:
        @block.sync
        def _(sp):
            sp.dma_start(u.slot_rows[:, :], slots_dram.rearrange("(r p) o -> r (p o)", p=P)).then_inc(s.read, 16)

        @block.vector
        def _(dve):
            dve.wait_ge(s.read, 16)
            dve.tensor_copy(u.slot_floats[:, :], u.slot_rows[:, :]).then_inc(s.floats, 1)
            dve.wait_ge(s.turned, 1)
            dve.tensor_copy(u.slots[:, :], u.psum[:, 0, 0:E_ * CT]).then_inc(s.taken, 1)

        @block.tensor
        def _(pe):
            pe.wait_ge(s.floats, 1)
            pe.transpose(u.psum[:, 0, 0:E_ * CT], u.slot_floats[:, :], u.id32[0:E_ * CT, 0:E_ * CT]).then_inc(s.turned, 1)


def two_layers(nc, a, out):
    slots_dram = nc.dram_tensor("slots", (E_ * CAP, 1), U32, kind="Internal").ap()
    z_dram = nc.dram_tensor("normed", (N, D), F32, kind="Internal").ap()
    x4_dram = nc.dram_tensor("before_last_norm", (N, D), F32, kind="Internal").ap()
    y_dram = nc.dram_tensor("expert_rows", (E_ * CAP, D), F32, kind="Internal").ap()
    with ExitStack() as ctx:
        lasting = {}
        lasting_buffers(nc, ctx, lasting)
        att = semaphores(nc, ctx, "att", ATT_SEMS)
        mix = semaphores(nc, ctx, "mix", POST0_SEMS)
        lin = semaphores(nc, ctx, "lin", LIN_SEMS)
        rt = semaphores(nc, ctx, "route", ROUTE_SEMS)
        moe = semaphores(nc, ctx, "moe", MOE_SEMS)
        comb = semaphores(nc, ctx, "comb", COMBINE_SEMS)
        nc.scalar.preload_act_table_set("natural_log_exp_and_others")
        with ExitStack() as layer:
            made = dict(lasting)
            attention_buffers(nc, layer, made)
            layer_buffers(nc, layer, made)
            set_up(nc, ctx, made, a, slots_dram)
            u = named(made)
            with nc.Fori(0, B) as b:
                attention(nc, b, u, att, True, a["x"])
                mixing(nc, u, mix)
                linear_attention(nc, u, lin)
                attention(nc, b, u, att, False)
                route(nc, b, u, rt, z_dram, x4_dram, slots_dram)
        with ExitStack() as layer:
            made = dict(lasting)
            for i in range(2):
                sbuf(nc, layer, made, f"w1{i}", [P, NC, F_])
                sbuf(nc, layer, made, f"w2{i}", [P, NF, D])
                sbuf(nc, layer, made, f"xg{i}", [P, CT, D])
                sbuf(nc, layer, made, f"ye{i}", [P, 2, D])
                sbuf(nc, layer, made, f"b2b{i}", [P, D])
            for n in ("w1", "w2", "xg", "ye", "b2b"):
                made[n] = [made[n + "0"], made[n + "1"]]
            sbuf(nc, layer, made, "xgt", [P, NC, CAP])
            sbuf(nc, layer, made, "hid", [P, NF, CAP])
            sbuf(nc, layer, made, "slot_rows", [E_ * CT, P], U32)
            sbuf(nc, layer, made, "slot_floats", [E_ * CT, P])
            sbuf(nc, layer, made, "slots", [P, E_ * CT], U32)
            sbuf(nc, layer, made, "ids", [P, 2 * CT], U32)
            sbuf(nc, layer, made, "b1", [P, E_ * NF])
            sbuf(nc, layer, made, "b1s", [P, 2 * NF])
            sbuf(nc, layer, made, "rows", [P, TOPK * NT, D])
            sbuf(nc, layer, made, "at", [P, TOPK, NT], U32)
            u = named(made)
            first = layer.enter_context(nc.semaphore("first_expert_in"))
            table_of_slots(nc, ctx, u, slots_dram)
            with nc.Block() as block:
                @block.sync
                def _(sp):
                    sp.dma_start(u.b1[:, :], a["b1"]).then_inc(first, 16)
                    load_expert(sp, 0, 0, u, a["W1"], a["W2"], first)
                    sp.wait_ge(first, 48)
            with nc.Fori(0, E_ // 2) as i:
                experts(nc, i, u, moe, z_dram, a["W1"], a["W2"], a["b2"], y_dram)
            with nc.Fori(0, B) as b:
                combine(nc, b, u, comb, x4_dram, y_dram, out)



def kernel(**inputs):
    import concourse.bacc as bacc
    from concourse.bass_utils import run_bass_kernel_spmd as run

    x = {k: np.asarray(v) for k, v in inputs.items()}

    def rows(w):
        return np.ascontiguousarray(w.reshape(NC, P, -1).transpose(1, 0, 2))

    def cols(v):
        return np.ascontiguousarray(v.reshape(-1, P).T)

    def grouped(w):
        return np.ascontiguousarray(w.reshape(NC, P, 3, NG, HG * HD).transpose(1, 0, 3, 2, 4).reshape(P, NC, NG, 192))

    by_head = x["L1_ffn_Wqkv"].reshape(D, H, 3, HD).transpose(0, 2, 1, 3)
    arrays = {
        "x": x["L0_attn_x"],
        "wqkv0": grouped(x["L0_attn_w_qkv"].T.reshape(D, 3, H, HD)),
        "wout": rows(x["L0_attn_w_out"].T), "wr": rows(x["L0_ffn_W_r"].T), "wk0": rows(x["L0_ffn_W_k"].T),
        "wv0": rows(x["L0_ffn_W_v"].T), "mur": cols(x["L0_ffn_mu_r"]), "muk": cols(x["L0_ffn_mu_k"]),
        "wq1": rows(x["L1_attn_Wq"]), "wk1": rows(x["L1_attn_Wk"]), "wv1": rows(x["L1_attn_Wv"]),
        "wo1": rows(x["L1_attn_Wo"]), "bq": cols(x["L1_attn_bq"]), "bk": x["L1_attn_bk"][None],
        "bv": x["L1_attn_bv"][None], "bo": x["L1_attn_bo"][None],
        "rft": np.ascontiguousarray(x["L1_attn_random_features"].T),
        "ln1g": cols(x["L1_ffn_ln1_g"]), "ln1b": cols(x["L1_ffn_ln1_b"]),
        "ln2g": cols(x["L1_ffn_ln2_g"]), "ln2b": cols(x["L1_ffn_ln2_b"]),
        "wqkv1": grouped(by_head), "wproj": rows(x["L1_ffn_Wproj"]), "wgate": rows(x["L1_ffn_Wgate"]),
        "W1": x["L1_ffn_W1"], "b1": cols(x["L1_ffn_b1"]), "W2": x["L1_ffn_W2"], "b2": x["L1_ffn_b2"],
    }
    for name, table in constants().items():
        arrays[name[2:]] = table
    nc = bacc.Bacc("TRN2", target_bir_lowering=False, num_devices=1)
    sent, a = {}, {}
    for name, v in arrays.items():
        sent["in_" + name] = np.ascontiguousarray(v)
        a[name] = nc.dram_tensor("in_" + name, v.shape, mybir.dt.from_np(v.dtype), kind="ExternalInput").ap()
    out = nc.dram_tensor("out", (B, T, D), F32, kind="ExternalOutput").ap()
    two_layers(nc, a, out)
    return run(nc, [sent], core_ids=[0]).results[0]["out"]
```

```python
from collections import namedtuple
from contextlib import ExitStack

import numpy as np

import concourse.bass as bass
from concourse import mybir

ALU = mybir.AluOpType
ACT = mybir.ActivationFunctionType
AX = mybir.AxisListType
F32 = mybir.dt.float32
BF16 = mybir.dt.bfloat16
U32 = mybir.dt.uint32

P = 128
B, T, D = 4, 1024, 256
NT = T // P
NC = D // P
H, HD = 16, 16
HG = 4
NG = H // HG
WINDOW = 64
HALF = HD // 2
SCALE = HD ** -0.5
SLOTS = 6
KS = SLOTS * HD
KM = KS + 3
WQ = P + WINDOW
E_, F_, TOPK = 8, 1024, 2
N = B * T
CAP = 2 * N // E_
NF = F_ // P
CT = CAP // P
NEG = -2.0 ** 100
EPS = 1e-5
BANK = 512
DROPPED = 65536.0


def named(things):
    return namedtuple("Named", list(things))(*things.values())


def semaphores(nc, ctx, prefix, names):
    made = {n: ctx.enter_context(nc.semaphore(f"{prefix}_{n}")) for n in names.split()}
    return named(dict(made, all=[h for n, h in made.items() if not n.endswith("_gathered")]))


def zero(pool, sems):
    for x in sems.all:
        pool.sem_clear(x)


def clear(nc, sems):
    with nc.Block() as block:
        @block.gpsimd
        def _(pool):
            zero(pool, sems)


def dve_chain(dve, sem):
    count = [0]

    def link(ins):
        count[0] += 1
        ins.then_inc(sem, 1)
        dve.wait_ge(sem, count[0])
    return link



Timing = namedtuple("Timing", "prep maxima out next_proj turns behind scalar_repeats")
WINDOWED = Timing(prep=((-1.263, -0.198), (-0.782, -0.008), (0, 1)),
                  maxima=((-0.427, -0.015), (0.016, 0.85), (-0.165, 0.85)),
                  out=0.454, next_proj=(3, 4, -1), turns=(3, 6), behind=1, scalar_repeats=2)
CAUSAL = Timing(prep=((-1.384, -0.5), (-0.474, -0.06), (-0.024, 0.823)),
                  maxima=((-0.688, -0.06), (-0.037, 0.812), (-0.275, 0.812)),
                  out=0.524, next_proj=(-1, -1, 2), turns=(2, 7), behind=3, scalar_repeats=2)


class Script:

    RING = 4

    def __init__(self, windowed):
        def pieces(t, keys):
            if windowed:
                return [((2 * j, 2 * j + 1), 0, 0) for j in range(2)]
            first, last = (0, P * t + P) if keys else (P * t, T)
            cuts = [first] + [c for c in (BANK,) if first < c < last] + [last]
            return [((h,), a, e) for h in range(HG) for a, e in zip(cuts[:-1], cuts[1:])]

        time = WINDOWED if windowed else CAUSAL

        def prep(g):
            out = [("proj", g, 0)]
            for k in range(5):
                cuts = [(x, g, k) for x in ("rotate", "rot", "high", "rest", "mid", "low")] if k < 4 else []
                at = time.next_proj[min(g, 2)]
                if at < 0:
                    cuts[0:0] = [("proj", g, k)] if 0 < k < 4 else []
                else:
                    cuts[at:at] = [("proj", g, k + 1)] if k < 3 else []
                turns = [("turn", g, 2 * k - 2), ("turn", g, 2 * k - 1)] if k else []
                i, j = time.turns
                out += cuts[:i] + turns[:1] + cuts[i:j] + turns[1:] + cuts[j:]
            return out if g < NG else []

        def maxima(g):
            return [("max", g, t, x) for t in range(NT) for x in pieces(t, True)] + [("rows", g)] if g < NG else []

        def exps(g):
            out = []
            for t in range(NT):
                mine = [("exp", g, t, x) for x in pieces(t, False)]
                out += beside((mine, 0, 1), (values(g, t - 1), 0, 1)) if t else mine
            return out + values(g, NT - 1) + [("collect", g)]

        def values(g, t):
            end = min(T, P * t + WQ) if windowed else T
            cuts = [P * t] + [c for c in (BANK,) if P * t < c < end] + [end]
            return [("values", g, t, x) for x in zip(cuts[:-1], cuts[1:])]

        def beside(*lists):
            at = [(start + (i + 1) * (end - start) / len(x), n, i)
                  for n, (x, start, end) in enumerate(lists) for i in range(len(x))]
            return [lists[n][0][i] for _, n, i in sorted(at)]

        parts = [(prep(g), *time.prep[g]) for g in range(2)] + [(maxima(0), *time.maxima[0])]
        for g in range(NG):
            start, end = time.maxima[min(g + 1, 2)]
            parts += [(exps(g), g, g + 1), (maxima(g + 1), g + start, g + end),
                      (prep(g + 2), g + time.prep[2][0], g + time.prep[2][1]),
                      ([("out", g, 0), ("out", g, 1)], g + 1, g + 1 + time.out)]
        queue_of = {"exp": "exps", "values": "exps", "collect": "exps", "max": "maxima", "rows": "maxima", "out": "out"}

        def behind(x):
            kind, g = x[:2]
            if kind == "max":
                return [("turn", g, min(x[2] + time.behind, NT - 1))] + ([("rows", g - 1)] if g else [])
            if kind == "proj" and x[2] == 0:
                return ([("turn", g - 1, NT - 1)] if g else []) + ([("collect", g - 3)] if g >= 3 else [])
            if kind == "exp":
                return [("rows", g)] + ([("collect", g - 1)] if g else [])
            return [("collect", g)] if kind == "out" else []

        steps, done, queues = [], set(), {}
        for x in beside(*[x for x in parts if x[0]]):
            queues.setdefault((queue_of.get(x[0], "prep"), x[1]), []).append(x)
            moved = True
            while moved:
                moved = False
                for q in queues.values():
                    while q and done.issuperset(behind(q[0])):
                        done.add(q[0])
                        steps.append(q.pop(0))
                        moved = True
        at = steps.index(("out", NG - 1, 0))
        steps[at:at] = [("back", 0), ("back", 1)]
        self.steps = steps
        self.order, self.bank, self.after = {}, {}, {}
        count, ring = {}, []
        for x in steps:
            kind = {"rows": "turn", "rot": "cut", "high": "cut", "rest": "cut", "mid": "cut", "low": "cut"}.get(x[0], x[0])
            self.order[x] = count[kind] = count.get(kind, -1) + 1
            if kind in ("max", "exp", "out"):
                self.bank[x] = len(ring) % self.RING
                self.after[x] = ring[-self.RING] if len(ring) >= self.RING else None
                ring.append(x)
        turns = [x for x in steps if x[0] in ("turn", "rows")]
        self.spare = {x: n % 2 == 1 and n < turns.index(("rows", 0)) for n, x in enumerate(turns)}
        self.turned_before = {x: max([self.order[y] for y in turns[:n] if self.spare[y] == self.spare[x]], default=-1)
                              for n, x in enumerate(turns)}
        self.last_exp = {x[1:3]: self.order[x] for x in steps if x[0] == "exp"}
        self.last_values = {x[1:3]: self.order[x] for x in steps if x[0] == "values"}
        self.first = {}
        for x in steps:
            self.first.setdefault((x[0],) + x[1:3] if x[0] == "exp" else x[:2], x)

    def wait_bank(self, eng, x, s):
        y = self.after[x]
        if y is not None:
            eng.wait_ge({"max": s.max_read, "exp": s.exp_done, "out": s.out_read}[y[0]], self.order[y] + 1)


def attention(nc, u, s, over, windowed, later):
    plan = Script(windowed)
    filling = (WINDOWED if windowed else CAUSAL).scalar_repeats
    order = plan.order
    w_sb = u.wqkv0 if windowed else u.wqkv1

    def heads_in_bank(x, w):
        return u.psum[:, plan.bank[x], 0:2 * WQ].rearrange("p (h w) -> p h w", h=2)[:, :, 0:w]

    def turned(x):
        return u.tr_spare if plan.spare[x] else u.tr

    def repeats(i):
        st = u.stack[i % 2][:, :, :, :].rearrange("p a x (s d) -> p a x s d", d=HD)
        q, k = st[:, 0, :, :, :], st[:, 1, :, :, :]
        return (((q[:, :, 1:3, :], q[:, :, 0:1, :].broadcast_to([P, 2 * HG, 2, HD])),
                 (k[:, :, 4:6, :], k[:, :, 0:1, :].broadcast_to([P, 2 * HG, 2, HD]))),
                ((q[:, :, 4, :], q[:, :, 3, :]), (k[:, :, 1, :], k[:, :, 3, :])))

    with nc.Block() as block:
        @block.sync
        def _(sp):
            for g in range(NG):
                sp.wait_ge(s.tr_read, order[("rows", g)] + 1)
                for j in range(3):
                    sp.dma_start(u.qk[g % 3][KS + j:KS + j + 1, 0:HG, :].rearrange("o h (t q) -> o (h t) q", q=P),
                                 u.mrow[32 * j:32 * j + 32, :]).then_inc(s.m_rows, 16)
            sp.wait_ge(s.m_rows, 48 * NG)
            sp.wait_ge(later, 16 * len(LATER_WEIGHTS))

        @block.tensor
        def _(pe):
            for x in plan.steps:
                kind, g = x[:2]
                q, n = u.qk[g % 3], order.get(x)
                if kind == "proj":
                    k = x[2]
                    if n:
                        pe.wait_ge(s.pj_read, n)
                    for t in range(2):
                        out = u.pj[:, 0:384].rearrange("p (a t c) -> p a t c", a=3, t=2)[:, :, t, :]
                        for c in range(NC):
                            ins = pe.matmul(out, u.xt[:, c, P * (2 * k + t):P * (2 * k + t + 1)],
                                            w_sb[:, c, g, :].rearrange("p (a c) -> p a c", a=3),
                                            start=(c == 0), stop=(c == NC - 1))
                    ins.then_inc(s.pj_ready, 1)
                elif kind == "turn":
                    t = x[2]
                    if plan.turned_before[x] >= 0:
                        pe.wait_ge(s.tr_read, plan.turned_before[x] + 1)
                    pe.wait_ge(s.cut, order[("low", g, t // 2)] + 1)
                    pe.wait_ge(s.repeated, 4 * g + t // 2 + 1)
                    st = u.stack[(t // 2) % 2]
                    for h in range(2 * HG):
                        ins = pe.transpose(turned(x)[0:KS, h, :], st[:, h // HG, (t % 2) * HG + h % HG, :], u.id16[:, :])
                    ins.then_inc(s.tr_ready, 1)
                elif kind == "rows":
                    pe.wait_ge(s.tr_read, n)
                    pe.wait_ge(s.m_parts, g + 1)
                    pe.transpose(u.tr[0:KS, 0, :], u.mparts[:, :], u.id16[:, :]).then_inc(s.tr_ready, 1)
                elif kind == "max":
                    t, (heads, a, e) = x[2:]
                    pe.wait_ge(s.tr_read, order[("turn", g, t)] + 1)
                    plan.wait_bank(pe, x, s)
                    r = u.psum[:, plan.bank[x], :]
                    if windowed:
                        k0, w = max(0, P * t - WINDOW), min(WQ, P * t + P)
                        out = heads_in_bank(x, w)
                        pe.matmul(out, u.id16[:, :], u.mask_q[:, :, WQ - w:WQ], start=True, stop=True,
                                  skip_group_check=True)
                        for h in heads:
                            ins = pe.matmul(out[:, h % 2, :], q[0:KS, h, P * t:P * t + P], q[0:KS, HG + h, k0:k0 + w],
                                            start=False, stop=True, skip_group_check=True)
                    else:
                        h, last = heads[0], e == P * t + P
                        if last:
                            pe.matmul(r[:, P * t - a:P * t - a + P], u.id16[:, :], u.causal_q[:, :], start=True,
                                      stop=True, skip_group_check=True)
                        ins = pe.matmul(r[:, 0:e - a], q[0:KS, h, P * t:P * t + P], q[0:KS, HG + h, a:e],
                                        start=not last, stop=True, skip_group_check=True)
                    ins.then_inc(s.max_ready, 1)
                elif kind == "exp":
                    t, (heads, a, e) = x[2:]
                    if t == 0:
                        pe.wait_ge(s.m_rows, 48 * (g + 1))
                    plan.wait_bank(pe, x, s)
                    r = u.psum[:, plan.bank[x], :]
                    if windowed:
                        q0, w = P * t, min(WQ, T - P * t)
                        out = heads_in_bank(x, w)
                        pe.matmul(out, u.id16[:, :], u.mask_k[:, :, 0:w], start=True, stop=True,
                                  skip_group_check=True)
                        for h in heads:
                            ins = pe.matmul(out[:, h % 2, :], q[0:KM, HG + h, P * t:P * t + P], q[0:KM, h, q0:q0 + w],
                                            start=False, stop=True, skip_group_check=True)
                    else:
                        h, first = heads[0], a == P * t
                        if first:
                            pe.matmul(r[:, 0:P], u.id16[:, :], u.causal_k[:, :], start=True, stop=True,
                                      skip_group_check=True)
                        ins = pe.matmul(r[:, 0:e - a], q[0:KM, HG + h, P * t:P * t + P], q[0:KM, h, a:e],
                                        start=not first, stop=True, skip_group_check=True)
                    ins.then_inc(s.exp_ready, 1)
                elif kind == "back":
                    pe.wait_ge(s.out_read, order[("out", NG // 2 - 1, 1)] + 1)
                    pe.wait_ge(s.pj_read, 4 * NG)
                    pe.wait_ge(s.tr_read, order[("rows", NG - 1)] + 1)
                    for t in range(4):
                        ins = pe.transpose(u.psum[:, 6 + g, P * t:P * t + P], u.o[:, 4 * g + t, 0:P], u.id32[:, :])
                    ins.then_inc(s.back_ready, 1)
                elif kind == "values":
                    t, (a, e) = x[2:]
                    pe.wait_ge(s.exp_done, plan.last_exp[(g, t)] + 1)
                    if t == 0 and g:
                        pe.wait_ge(s.o_read, g)
                    first = a in (0, BANK) and (t == 0 or a > P * t) if windowed else t == 0
                    shift = P * t if windowed else 0
                    for h in range(HG):
                        ins = pe.matmul(u.ot[32 * h:32 * h + 32, a:e], u.v[g % 3][:, t, h, :],
                                        u.probs[t % 2][:, h, a - shift:e - shift], start=first, stop=True,
                                        tile_position=(0, 32 * h), skip_group_check=True)
                    ins.then_inc(s.pv_done, 1)
                elif kind == "out":
                    pe.wait_ge(s.o_read, g + 1)
                    plan.wait_bank(pe, x, s)
                    for t in range(4):
                        ins = pe.transpose(u.psum[:, plan.bank[x], P * t:P * t + P],
                                           u.ot_sb[:, BANK * x[2] + P * t:BANK * x[2] + P * t + P], u.id32[:, :])
                    ins.then_inc(s.out_ready, 1)

        @block.scalar
        def _(act):
            for x in plan.steps:
                kind, g = x[:2]
                n = order.get(x)
                if kind == "exp":
                    t, (heads, a, e) = x[2:]
                    act.wait_ge(s.exp_ready, n + 1)
                    if plan.first[x[:3]] == x and NT * g + t >= 2:
                        back = divmod(NT * g + t - 2, NT)
                        act.wait_ge(s.pv_done, plan.last_values[back] + 1)
                    if windowed:
                        w = min(WQ, T - P * t)
                        act.activation(u.probs[t % 2][:, heads[0]:heads[0] + 2, 0:w], heads_in_bank(x, w),
                                       ACT.Exp, scale=SCALE).then_inc(s.exp_done, 1)
                    else:
                        act.activation(u.probs[t % 2][:, heads[0], a:e], u.psum[:, plan.bank[x], 0:e - a],
                                       ACT.Exp, scale=SCALE).then_inc(s.exp_done, 1)
                elif kind in ("high", "mid") and g < filling:
                    act.wait_ge(s.cut, order[x] + 1)
                    for d, y in repeats(4 * g + x[2])[kind == "mid"]:
                        ins = act.activation(d, y, ACT.Copy)
                    if kind == "mid":
                        ins.then_inc(s.repeated, 1)
                elif kind == "turn":
                    t = x[2]
                    act.wait_ge(s.tr_ready, n + 1)
                    act.activation(u.qk[g % 3][0:KS, :, P * t:P * t + P], turned(x)[0:KS, :, :], ACT.Copy
                                   ).then_inc(s.tr_read, 1)
                elif kind == "rows":
                    act.wait_ge(s.tr_ready, n + 1)
                    if g:
                        act.wait_ge(s.m_rows, 48 * g)
                    act.activation(u.mrow[0:KS, :], u.tr[0:KS, 0, :], ACT.Copy).then_inc(s.tr_read, 1)
                elif kind == "back":
                    act.wait_ge(s.back_ready, g + 1)
                    act.activation(u.xt[:, 0, BANK * g:BANK * g + BANK], u.psum[:, 6 + g, :], ACT.Copy)
                elif kind == "collect":
                    act.wait_ge(s.pv_done, plan.last_values[(g, NT - 1)] + 1)
                    if g:
                        act.wait_ge(s.out_ready, 2 * g)
                    act.activation(u.ot_sb[:, :], u.ot[:, :], ACT.Copy).then_inc(s.o_read, 1)

        @block.vector
        def _(dve):
            link = dve_chain(dve, s.chain)

            def rotate(x):
                _, g, k = x
                i = order[("proj", g, k)]
                dve.wait_ge(s.pj_ready, i + 1)
                if i:
                    dve.wait_ge(s.cut, order[("rot", (i - 1) // 4, (i - 1) % 4)] + 1)
                src = u.pj[:, 0:256].rearrange("p (a y) -> p a y", a=2)
                table = (slice(None), slice(2 * k, 2 * k + 2), slice(None))
                cos = u.cos[table].rearrange("p t y -> p (t y)").unsqueeze(1).broadcast_to([P, 2, P])
                sin = u.sin[table].rearrange("p t (h d) -> p (t h) d", d=HD)
                dve.tensor_tensor(u.ra[:, :, :], src, cos, ALU.mult)
                halves = src.rearrange("p a (h d) -> p a h d", d=HD)
                for y in range(2):
                    dve.tensor_tensor(u.rb[:, :, :].rearrange("p a (h d) -> p a h d", d=HD)[:, :, :, HALF * y:HALF * y + HALF],
                                      halves[:, :, :, HALF * (1 - y):HALF * (1 - y) + HALF],
                                      sin[:, :, HALF * y:HALF * y + HALF].unsqueeze(1).broadcast_to([P, 2, 2 * HG, HALF]),
                                      ALU.mult)
                dve.tensor_copy(u.v[g % 3][:, 2 * k:2 * k + 2, :, 0:HD].rearrange("p t h d -> p (t h) d"),
                                u.pj[:, 256:384].rearrange("p (h d) -> p h d", d=HD)).then_inc(s.pj_read, 1)

            def cut(x):
                kind, g, k = x
                st = u.stack[k % 2][:, :, :, :].rearrange("p a x (s d) -> p (a x) s d", d=HD)
                rot = u.rot[:, :, :].rearrange("p a (h d) -> p (a h) d", d=HD)
                rest = u.rest[:, :, :].rearrange("p a (h d) -> p (a h) d", d=HD)
                half = 2 * HG
                if order[x]:
                    dve.wait_ge(s.cut, order[x])
                if kind == "rot":
                    dve.wait_ge(s.pj_read, order[("proj", g, k)] + 1)
                    ins = dve.tensor_tensor(u.rot[:, :, :], u.ra[:, :, :], u.rb[:, :, :], ALU.add)
                elif kind == "high":
                    i = 4 * g + k - 2
                    if i >= 0:
                        dve.wait_ge(s.tr_ready, order[("turn", i // 4, 2 * (i % 4) + 1)] + 1)
                    ins = dve.tensor_copy(st[:, :, 0, :], rot)
                elif kind == "rest":
                    ins = dve.tensor_tensor(rest, rot, st[:, :, 0, :], ALU.subtract)
                elif kind == "mid":
                    ins = dve.tensor_copy(st[:, :, 3, :], rest)
                else:
                    dve.tensor_tensor(st[:, 0:half, 5, :], rest[:, 0:half, :], st[:, 0:half, 3, :], ALU.subtract)
                    ins = dve.tensor_tensor(st[:, half:2 * half, 2, :], rest[:, half:2 * half, :],
                                            st[:, half:2 * half, 3, :], ALU.subtract)
                ins.then_inc(s.cut, 1)

            def parts_of_maxima(g):
                dve.wait_ge(s.max_read, max(order[y] for y in plan.steps if y[:2] == ("max", g)) + 1)
                m = u.mneg[:, :, :]
                if not windowed:
                    link(dve.tensor_tensor(m[:, :, 4:NT], m[:, :, 4:NT], u.mhalf[:, :, :], ALU.min))
                m = m.rearrange("p h t -> p (h t)")
                if g:
                    dve.wait_ge(s.tr_ready, order[("rows", g - 1)] + 1)
                link(dve.tensor_copy(u.mparts[:, 0:32], m))
                link(dve.tensor_tensor(u.mrest[:, :], m, u.mparts[:, 0:32], ALU.subtract))
                link(dve.tensor_copy(u.mparts[:, 32:64], u.mrest[:, :]))
                dve.tensor_tensor(u.mparts[:, 64:96], u.mrest[:, :], u.mparts[:, 32:64], ALU.subtract
                                  ).then_inc(s.m_parts, 1)
                dve.wait_ge(s.m_parts, g + 1)

            for x in plan.steps:
                kind, g = x[:2]
                n = order.get(x)
                if kind == "rotate":
                    rotate(x)
                elif kind in ("rot", "high", "rest", "mid", "low"):
                    cut(x)
                elif kind == "max":
                    t, (heads, a, e) = x[2:]
                    dve.wait_ge(s.max_ready, n + 1)
                    if windowed:
                        ins = dve.tensor_reduce(u.mneg[:, heads[0]:heads[0] + 2, t], heads_in_bank(x, min(WQ, P * t + P)),
                                                AX.X, ALU.max, negate=True)
                    else:
                        h = heads[0]
                        out = u.mneg[:, h, t:t + 1] if e == P * t + P else u.mhalf[:, h, t - 4:t - 3]
                        ins = dve.tensor_reduce(out, u.psum[:, plan.bank[x], 0:e - a], AX.X, ALU.max, negate=True)
                    ins.then_inc(s.max_read, 1)
                elif kind == "rows":
                    parts_of_maxima(g)
                elif kind == "out":
                    y = x[2]
                    dve.wait_ge(s.out_ready, n + 1)
                    r = u.psum[:, plan.bank[x], :].rearrange("p (t h x) -> p t h x", t=4, h=HG)
                    if n:
                        dve.wait_ge(s.out_read, n)
                    link(dve.reciprocal(u.rden[:, :, :], r[:, :, :, HD]))
                    dve.tensor_tensor(
                        u.o[:, 4 * y:4 * y + 4, HG * HD * g:HG * HD * (g + 1)].rearrange("p t (h d) -> p t h d", h=HG),
                        r[:, :, :, 0:HD], u.rden[:, :, :].unsqueeze(3).broadcast_to([P, 4, HG, HD]),
                        ALU.mult).then_inc(s.out_read, 1)

        @block.gpsimd
        def _(pool):
            zero(pool, over)
            for i in range(4 * filling, 4 * NG):
                pool.wait_ge(s.cut, order[("high", i // 4, i % 4)] + 1)
                for d, x in repeats(i)[0]:
                    pool.tensor_copy(d, x)
                pool.wait_ge(s.cut, order[("mid", i // 4, i % 4)] + 1)
                for d, x in repeats(i)[1]:
                    ins = pool.tensor_copy(d, x)
                ins.then_inc(s.repeated, 1)


ATT_SEMS = ("back_ready pj_ready pj_read cut repeated tr_ready tr_read "
            "max_ready max_read m_parts m_rows exp_ready exp_done pv_done o_read out_ready out_read chain")



def constants():
    inv = 1.0 / 10000.0 ** (np.arange(0, HD, 2, dtype=np.float32) / HD)
    angle = (np.arange(T, dtype=np.float32)[:, None] * inv.astype(np.float32)).astype(np.float32)
    cos, sin = np.cos(angle), np.sin(angle)

    def by_tile(x):
        return np.tile(x.reshape(NT, P, HD).transpose(1, 0, 2), HG).astype(np.float32)
    p, w, f = np.arange(P)[:, None], np.arange(WQ)[None], np.arange(P)[None]
    behind = p + WINDOW - w
    mask_q = np.where((behind >= 0) & (behind < WINDOW), 0.0, NEG)
    ahead = w - p
    mask_k = np.where((ahead >= 0) & (ahead < WINDOW), 0.0, NEG)
    return {
        "c_cos": by_tile(np.concatenate([cos, cos], -1)),
        "c_sin": by_tile(np.concatenate([-sin, sin], -1)),
        "c_id32": np.eye(P, dtype=np.float32),
        "c_tables": np.concatenate(
            [np.eye(P), mask_q, mask_q, mask_k, mask_k, np.where(f <= p, 0.0, NEG), np.where(f >= p, 0.0, NEG),
             f >= p], 1).astype(np.float32),
        "c_blocks": (p // HD == f // HD).astype(np.float32),
        "c_iota": np.repeat(np.arange(E_, dtype=np.float32)[None], P, 0),
        "c_next_token": (P * np.arange(NT)[None] + p).astype(np.uint32),
    }


def sbuf(nc, ctx, made, name, shape, dtype=F32):
    made[name] = ctx.enter_context(nc.sbuf_tensor(f"b_{name}", shape, dtype))


def attention_buffers(nc, ctx, u):
    sbuf(nc, ctx, u, "cos", [P, NT, HG * HD])
    sbuf(nc, ctx, u, "sin", [P, NT, HG * HD])
    sbuf(nc, ctx, u, "id16", [P, P], BF16)
    sbuf(nc, ctx, u, "mask_q", [P, 2, WQ], BF16)
    sbuf(nc, ctx, u, "mask_k", [P, 2, WQ], BF16)
    sbuf(nc, ctx, u, "causal_q", [P, P], BF16)
    sbuf(nc, ctx, u, "causal_k", [P, P], BF16)
    sbuf(nc, ctx, u, "src", [P, NT, D])
    sbuf(nc, ctx, u, "xt", [P, NC, T])
    sbuf(nc, ctx, u, "o", [P, NT, D])
    for name in "ra rb rot rest".split():
        sbuf(nc, ctx, u, name, [P, 2, P])
    sbuf(nc, ctx, u, "mneg", [P, HG, NT])
    sbuf(nc, ctx, u, "mhalf", [P, HG, NT - 4])
    sbuf(nc, ctx, u, "mrest", [P, HG * NT])
    sbuf(nc, ctx, u, "mparts", [P, KS], BF16)
    sbuf(nc, ctx, u, "mrow", [P, P], BF16)
    sbuf(nc, ctx, u, "ot_sb", [P, T])
    sbuf(nc, ctx, u, "rden", [P, 4, HG])
    for name, shape, dtype, n in (("stack", [P, 2, 2 * HG, KS], BF16, 2), ("qk", [P, 2 * HG, T], BF16, 3),
                                  ("v", [P, NT, HG, 32], F32, 3), ("probs", [P, HG, T], F32, 2)):
        for i in range(n):
            sbuf(nc, ctx, u, f"{name}{i}", shape, dtype)
        u[name] = [u[f"{name}{i}"] for i in range(n)]
    psum = u["psum"]
    u["ot"] = psum[:, 4:6, :].rearrange("p a x -> p (a x)")
    u["pj"] = psum[:, 6, :]
    for name, bank in ("tr", 7), ("tr_spare", 4):
        u[name] = psum[:, bank, :].bitcast(BF16).rearrange("p (h x) -> p h x", x=P)



def norm_stats(dve, y, u, tiles):
    for t in tiles:
        ins = dve.bn_stats(u.bn[:, t, :], y[:, t, :])
    return ins


def norm_variance(dve, link, u, s):
    for t in range(NT):
        ins = dve.bn_aggr(u.mv[:, t, :], u.bn[:, t, :])
    link(ins)
    dve.tensor_scalar(u.var[:, :], u.mv[:, :, 1], EPS, None, ALU.add).then_inc(s.var_ready, 1)


def norm_root(act, u, s, k):
    act.wait_ge(s.var_ready, k + 1)
    act.activation(u.lnv[:, :], u.var[:, :], ACT.Ln).then_inc(s.ln_done, 1)
    act.wait_ge(s.ln_done, k + 1)
    act.activation(u.root[:, :], u.lnv[:, :], ACT.Exp, scale=-0.5).then_inc(s.root_ready, 1)


def norm_apply(dve, link, y, out, u, s, k, half_ready=None):
    dve.wait_ge(s.root_ready, k + 1)
    link(dve.tensor_tensor(u.nt[:, :], u.root[:, :], u.root[:, :], ALU.mult))
    link(dve.tensor_tensor(u.nt[:, :], u.nt[:, :], u.var[:, :], ALU.mult))
    link(dve.tensor_scalar(u.nt[:, :], u.nt[:, :], -0.5, 1.5, ALU.mult, ALU.add))
    link(dve.tensor_tensor(u.rstd[:, :], u.root[:, :], u.nt[:, :], ALU.mult))
    for t in range(NT):
        ins = dve.tensor_scalar(out[:, t, :], y[:, t, :], u.mv[:, t, 0:1], u.rstd[:, t:t + 1],
                                ALU.subtract, ALU.mult)
        if half_ready is not None and t % 4 == 3:
            ins.then_inc(half_ready, 1)
    return ins


NORM_SEMS = " var_ready ln_done root_ready chain "


def turn_tiles(pe, src, u, s, chunks=range(NC), half_ready=None):
    for h in range(2):
        if half_ready is not None:
            pe.wait_ge(half_ready, h + 1)
        for c in chunks:
            for t in range(4):
                ins = pe.transpose(u.psum[:, 2 * c + h, P * t:P * t + P], src[:, 4 * h + t, P * c:P * c + P], u.id32[:, :])
            ins.then_inc(s.turned, 1)


def take_turned(act, dst, u, s, before, gain=None, offset=None, chunks=range(NC)):
    for h in range(2):
        for n, c in enumerate(chunks):
            act.wait_ge(s.turned, before + len(chunks) * h + n + 1)
            d = dst[:, c, BANK * h:BANK * h + BANK]
            if gain is None:
                act.activation(d, u.psum[:, 2 * c + h, :], ACT.Copy).then_inc(s.taken, 1)
            else:
                act.activation(d, u.psum[:, 2 * c + h, :], ACT.Identity, scale=gain[:, c:c + 1],
                               bias=offset[:, c:c + 1]).then_inc(s.taken, 1)


def pair_product(pe, bank, lhs, rhs, k):
    for t in range(2):
        for c in range(NC):
            ins = pe.matmul(bank[:, D * t:D * t + D], lhs[:, c, P * (2 * k + t):P * (2 * k + t + 1)], rhs[:, c, :],
                            start=(c == 0), stop=(c == NC - 1))
    return ins


def bank_pair(u, bank):
    return u.psum[:, bank, :].rearrange("p (t d) -> p t d", t=2)


def pair(x, k):
    return x[:, 2 * k:2 * k + 2, :].rearrange("p t d -> p (t d)")



POST0_SEMS = ("turned taken pj_ready y_done x1_ready x2_ready mix_r mix_k r_ready r_abs r_exp r_ln r_used r_done k_ready k_done "
              "v_ready v_done sum_done") + NORM_SEMS


def scatter_slots(pool, u, slots_dram, gathered):
    for k in range(TOPK):
        for t in range(NT):
            pool.indirect_dma_start(
                out=slots_dram, out_offset=bass.IndirectOffsetOnAxis(ap=u.write_at[:, k, t:t + 1], axis=0),
                in_=u.token[:, t:t + 1], in_offset=None, bounds_check=E_ * CAP - 1, oob_is_err=False
            ).then_inc(gathered, 16)


def mixing(nc, u, s, over, slots_dram, slots_gathered):
    with nc.Block() as block:
        @block.gpsimd
        def _(pool):
            zero(pool, over)
            scatter_slots(pool, u, slots_dram, slots_gathered)

        @block.tensor
        def _(pe):
            turn_tiles(pe, u.o, u, s, chunks=(1,))
            for k in range(4):
                if k % 2 == 0:
                    pe.wait_ge(s.taken, k // 2 + 1)
                if k >= 2:
                    pe.wait_ge(s.y_done, k - 1)
                pair_product(pe, u.psum[:, 4 + k % 2, :], u.xt, u.wout, k).then_inc(s.pj_ready, 1)
            turn_tiles(pe, u.src, u, s, half_ready=s.x1_ready)
            for k in range(4):
                if k % 2 == 0:
                    pe.wait_ge(s.mix_r, k + 2)
                pair_product(pe, u.psum[:, 4 + k, :], u.xr, u.wr, k).then_inc(s.r_ready, 1)
            for h in range(2):
                pe.wait_ge(s.mix_k, 2 * h + 2)
                for c in range(NC):
                    for a in range(NC):
                        ins = pe.matmul(u.psum[:, 2 * c + h, :], u.wk0[:, a, P * c:P * c + P],
                                        u.xk[:, a, BANK * h:BANK * h + BANK], start=(a == 0), stop=(a == NC - 1))
                    ins.then_inc(s.k_ready, 1)
            for k in range(4):
                if k % 2 == 0:
                    pe.wait_ge(s.k_done, k + 2)
                pe.wait_ge(s.r_used, k + 1)
                pair_product(pe, u.psum[:, 4 + k, :], u.xt, u.wv0, k).then_inc(s.v_ready, 1)
            turn_tiles(pe, u.src, u, s, half_ready=s.x2_ready)

        @block.scalar
        def _(act):
            take_turned(act, u.xt, u, s, 0, chunks=(1,))
            norm_root(act, u, s, 0)
            take_turned(act, u.x1t[:, :, 1:T + 1], u, s, 2)
            for j in range(2):
                for k in (2 * j, 2 * j + 1):
                    act.wait_ge(s.r_ready, k + 1)
                    act.activation(pair(u.r, k), u.psum[:, 4 + k, :], ACT.Abs).then_inc(s.r_abs, 1)
                for k in (2 * j, 2 * j + 1):
                    act.wait_ge(s.r_abs, k + 1)
                    act.activation(pair(u.r, k), pair(u.r, k), ACT.Exp, scale=-1.0).then_inc(s.r_exp, 1)
                for k in (2 * j, 2 * j + 1):
                    act.wait_ge(s.r_exp, k + 1)
                    act.activation(pair(u.r, k), pair(u.r, k), ACT.Ln, bias=u.one[:, :]).then_inc(s.r_ln, 1)
            for k in range(4):
                act.wait_ge(s.r_used, k + 1)
                act.activation(pair(u.r, k), pair(u.r, k), ACT.Exp).then_inc(s.r_done, 1)
            norm_root(act, u, s, 1)
            take_turned(act, u.xt, u, s, 6)

        @block.vector
        def _(dve):
            link = dve_chain(dve, s.chain)
            dve.memset(u.x1t[:, :, 0:1], 0.0)
            for k in range(4):
                dve.wait_ge(s.pj_ready, k + 1)
                dve.tensor_tensor(pair(u.y, k), u.psum[:, 4 + k % 2, :], pair(u.src, k), ALU.add).then_inc(s.y_done, 1)
                dve.wait_ge(s.y_done, k + 1)
                ins = norm_stats(dve, u.y, u, (2 * k, 2 * k + 1))
            link(ins)
            norm_variance(dve, link, u, s)
            norm_apply(dve, link, u.y, u.src, u, s, 0, half_ready=s.x1_ready)

            def mix(h, out, mu, done):
                span = slice(BANK * h, BANK * h + BANK)
                for c in range(NC):
                    dve.scalar_tensor_tensor(out[:, c, span], u.dx[:, c, span], mu[:, c:c + 1], u.x1t[:, c, span],
                                             ALU.mult, ALU.add).then_inc(done, 1)
            for h in range(2):
                dve.wait_ge(s.taken, 2 + 2 * h + 2)
                link(dve.tensor_tensor(u.dx[:, :, BANK * h:BANK * h + BANK], u.x1t[:, :, BANK * h + 1:BANK * h + BANK + 1],
                                       u.x1t[:, :, BANK * h:BANK * h + BANK], ALU.subtract))
                mix(h, u.xr, u.mur, s.mix_r)
            for h in range(2):
                mix(h, u.xk, u.muk, s.mix_k)

            def arguments(k):
                dve.wait_ge(s.r_ln, k + 1)
                dve.scalar_tensor_tensor(pair(u.r, k), u.psum[:, 4 + k, :], 0.0, pair(u.r, k), ALU.min, ALU.subtract
                                         ).then_inc(s.r_used, 1)
            dve.wait_ge(s.mix_k, 4)
            for k in range(4):
                arguments(k)
                h, c = divmod(k, NC)
                bank = u.psum[:, 2 * c + h, :]
                dve.wait_ge(s.k_ready, k + 1)
                link(dve.tensor_scalar(pair(u.y, k), bank, 0.0, None, ALU.max))
                dve.tensor_tensor(u.xt[:, c, BANK * h:BANK * h + BANK], pair(u.y, k), bank, ALU.mult).then_inc(s.k_done, 1)
            dve.wait_ge(s.k_done, 4)
            for k in range(4):
                dve.wait_ge(s.r_done, k + 1)
                dve.wait_ge(s.v_ready, k + 1)
                dve.tensor_tensor(pair(u.r, k), u.psum[:, 4 + k, :], pair(u.r, k), ALU.mult).then_inc(s.v_done, 1)
                dve.wait_ge(s.v_done, k + 1)
                dve.tensor_tensor(pair(u.y, k), pair(u.r, k), pair(u.src, k), ALU.add).then_inc(s.sum_done, 1)
                dve.wait_ge(s.sum_done, k + 1)
                ins = norm_stats(dve, u.y, u, (2 * k, 2 * k + 1))
            link(ins)
            norm_variance(dve, link, u, s)
            norm_apply(dve, link, u.y, u.src, u, s, 1, half_ready=s.x2_ready)



LIN_SEMS = ("turned taken x3_ready q_ready q_min q_exp q_done k_ready k_add k_min k_exp k_done v_ready v_done kv_ready kvm_done "
            "m_ready m_done a_ready a_done out_ready y_done res_ready") + NORM_SEMS


def linear_attention(nc, u, s, over):
    with nc.Block() as block:
        @block.tensor
        def _(pe):
            for k in range(4):
                if k >= 2:
                    pe.wait_ge(s.k_add, k - 1)
                    pe.wait_ge(s.v_done, k - 1)
                pair_product(pe, u.psum[:, 4 + k % 2, :], u.xt, u.wk1, k).then_inc(s.k_ready, 1)
                pair_product(pe, u.psum[:, 6 + k % 2, :], u.xt, u.wv1, k).then_inc(s.v_ready, 1)

            def q_product(j):
                c, h = divmod(j, 2)
                for a in range(NC):
                    ins = pe.matmul(u.psum[:, j, :], u.wq1[:, a, P * c:P * c + P],
                                    u.xt[:, a, BANK * h:BANK * h + BANK], start=(a == 0), stop=(a == NC - 1))
                ins.then_inc(s.q_ready, 1)
            for j in range(3):
                q_product(j)
            pe.wait_ge(s.k_done, 4)
            pe.wait_ge(s.v_done, 4)
            for c in range(NC):
                for t in range(NT):
                    ins = pe.matmul(u.psum[:, 4, P * c:P * c + P], u.o[:, t, P * c:P * c + P], u.y[:, t, P * c:P * c + P],
                                    start=(t == 0), stop=(t == NT - 1))
            ins.then_inc(s.kv_ready, 1)
            q_product(3)
            pe.wait_ge(s.kvm_done, 1)
            for c in range(NC):
                ins = pe.matmul(u.psum[:, 5, P * c:P * c + P], u.kvm[:, c, :], u.bg[:, :], start=True, stop=True)
            ins.then_inc(s.m_ready, 1)
            pe.wait_ge(s.m_done, 1)
            for c in range(NC):
                ins = pe.matmul(u.psum[:, 6, D * c:D * c + D], u.mt[:, c, :], u.wo1[:, c, :], start=True, stop=True)
            ins.then_inc(s.a_ready, 1)
            pe.wait_ge(s.a_done, 1)
            pe.wait_ge(s.q_done, 4)
            for k in range(4):
                pair_product(pe, u.psum[:, k, :], u.phq, u.am, k).then_inc(s.out_ready, 1)
            turn_tiles(pe, u.src, u, s, half_ready=s.x3_ready)

        @block.scalar
        def _(act):
            for k in range(4):
                act.wait_ge(s.k_min, k + 1)
                act.activation(pair(u.o, k), pair(u.o, k), ACT.Exp).then_inc(s.k_exp, 1)
            for j in range(3):
                act.wait_ge(s.q_min, j + 1)
                d = (slice(None), j // 2, slice(BANK * (j % 2), BANK * (j % 2) + BANK))
                act.activation(u.qexp[d], u.qexp[d], ACT.Exp).then_inc(s.q_exp, 1)
            act.wait_ge(s.m_ready, 1)
            act.activation(u.mt[:, :, :].rearrange("p c x -> p (c x)"), u.psum[:, 5, 0:D], ACT.Copy).then_inc(s.m_done, 1)
            act.wait_ge(s.q_min, 4)
            act.activation(u.qexp[:, 1, BANK:T], u.qexp[:, 1, BANK:T], ACT.Exp).then_inc(s.q_exp, 1)
            act.wait_ge(s.a_ready, 1)
            act.activation(u.am[:, :, :].rearrange("p c x -> p (c x)"), u.psum[:, 6, :], ACT.Copy).then_inc(s.a_done, 1)
            norm_root(act, u, s, 0)
            norm_root(act, u, s, 1)
            take_turned(act, u.xt, u, s, 0, u.ln1g, u.ln1b)

        @block.gpsimd
        def _(pool):
            zero(pool, over)
            pool.tensor_tensor(u.src[:, :, :], u.src[:, :, :], u.bo[:, :].unsqueeze(1).broadcast_to([P, NT, D]),
                               ALU.add).then_inc(s.res_ready, 1)

        @block.vector
        def _(dve):
            link = dve_chain(dve, s.chain)

            def span(j):
                return (slice(None), j // 2, slice(BANK * (j % 2), BANK * (j % 2) + BANK))
            def k_features(k):
                dve.wait_ge(s.k_exp, k + 1)
                dve.scalar_tensor_tensor(pair(u.o, k), pair(u.kx, k), 1.0, pair(u.o, k), ALU.add, ALU.max
                                         ).then_inc(s.k_done, 1)

            def q_low(j):
                dve.wait_ge(s.q_ready, j + 1)
                dve.tensor_scalar(u.qexp[span(j)], u.psum[:, j, :], u.bq[:, j // 2:j // 2 + 1], 0.0, ALU.add, ALU.min
                                  ).then_inc(s.q_min, 1)

            def q_features(j):
                dve.wait_ge(s.q_exp, j + 1)
                dve.scalar_tensor_tensor(u.phq[span(j)], u.psum[:, j, :], u.bq_plus[:, j // 2:j // 2 + 1],
                                         u.qexp[span(j)], ALU.add, ALU.max).then_inc(s.q_done, 1)
            for k in range(4):
                dve.wait_ge(s.k_ready, k + 1)
                dve.tensor_tensor(u.kx[:, 2 * k:2 * k + 2, :], bank_pair(u, 4 + k % 2),
                                  u.bk[:, :].unsqueeze(1).broadcast_to([P, 2, D]), ALU.add).then_inc(s.k_add, 1)
                dve.wait_ge(s.k_add, k + 1)
                dve.tensor_scalar(pair(u.o, k), pair(u.kx, k), 0.0, None, ALU.min).then_inc(s.k_min, 1)
                dve.wait_ge(s.v_ready, k + 1)
                dve.tensor_tensor(u.y[:, 2 * k:2 * k + 2, :], bank_pair(u, 6 + k % 2),
                                  u.bv[:, :].unsqueeze(1).broadcast_to([P, 2, D]), ALU.add).then_inc(s.v_done, 1)
                if k:
                    k_features(k - 1)
            k_features(3)
            for j in range(3):
                q_low(j)
                if j:
                    q_features(j - 1)
            q_features(2)
            dve.wait_ge(s.kv_ready, 1)
            dve.tensor_tensor(u.kvm[:, :, :], u.psum[:, 4, 0:D].rearrange("p (c x) -> p c x", c=NC),
                              u.blocks[:, :].unsqueeze(1).broadcast_to([P, NC, P]), ALU.mult).then_inc(s.kvm_done, 1)
            q_low(3)
            q_features(3)
            dve.wait_ge(s.res_ready, 1)
            dve.wait_ge(s.kv_ready, 1)
            for k in range(4):
                dve.wait_ge(s.out_ready, k + 1)
                dve.tensor_tensor(pair(u.y, k), u.psum[:, k, :], pair(u.src, k), ALU.add).then_inc(s.y_done, 1)
                dve.wait_ge(s.y_done, k + 1)
                ins = norm_stats(dve, u.y, u, (2 * k, 2 * k + 1))
            link(ins)
            norm_variance(dve, link, u, s)
            link(norm_apply(dve, link, u.y, u.x3, u, s, 0))
            link(norm_stats(dve, u.x3, u, range(NT)))
            norm_variance(dve, link, u, s)
            norm_apply(dve, link, u.x3, u.src, u, s, 1, half_ready=s.x3_ready)



ROUTE_SEMS = ("turned taken pj_ready y_done x4_ready z_ready z_out lg_ready shifted exp_done mask_ready pos_ready "
              "src_in slots_gathered") + NORM_SEMS


def route(nc, b, u, s, over, x_dram, z_dram, x4_dram):
    with nc.Block() as block:
        @block.sync
        def _(sp):
            sp.dma_start(u.src[:, :, :], x_dram[bass.ds((b + 1) % B, 1), :, :].rearrange("o (t p) d -> p (o t) d", p=P)
                         ).then_inc(s.src_in, 16)
            sp.wait_ge(s.z_ready, 2)
            sp.dma_start(z_dram[bass.ds(b * T, T), :].rearrange("(t p) d -> p t d", p=P), u.z[:, :, :]
                         ).then_inc(s.z_out, 16)
            sp.wait_ge(s.x4_ready, 1)
            sp.dma_start(x4_dram[bass.ds(b * T, T), :].rearrange("(t p) d -> p t d", p=P), u.x3[:, :, :]
                         ).then_inc(s.z_out, 16)
            sp.wait_ge(s.z_out, 32)
            sp.wait_ge(s.src_in, 16)

        @block.tensor
        def _(pe):
            turn_tiles(pe, u.o, u, s, chunks=(1,))
            for k in range(4):
                if k % 2 == 0:
                    pe.wait_ge(s.taken, k // 2 + 1)
                if k >= 2:
                    pe.wait_ge(s.y_done, k - 1)
                pair_product(pe, u.psum[:, 4 + k % 2, :], u.xt, u.wproj, k).then_inc(s.pj_ready, 1)
            turn_tiles(pe, u.z, u, s, half_ready=s.z_ready)
            for t in range(NT):
                if t % 4 == 0:
                    pe.wait_ge(s.taken, 2 + t // 2 + 2)
                for c in range(NC):
                    ins = pe.matmul(u.psum[:, 6, E_ * t:E_ * t + E_], u.xt[:, c, P * t:P * t + P], u.wgate[:, c, :],
                                    start=(c == 0), stop=(c == NC - 1))
            ins.then_inc(s.lg_ready, 1)
            pe.wait_ge(s.src_in, 16)
            turn_tiles(pe, u.src, u, s)
            pe.wait_ge(s.mask_ready, 1)
            for t in range(NT):
                out = u.psum[:, 7, E_ * t:E_ * t + E_]
                pe.matmul(out, u.upto[:, :], u.chosen[:, t, :], start=True, stop=False)
                for a in range(t):
                    pe.matmul(out, u.ones16[:, :], u.chosen[:, a, :], start=False, stop=False)
                ins = pe.matmul(out, u.ones16[:, :], u.before[:, :], start=False, stop=True)
            ins.then_inc(s.pos_ready, 1)

        @block.scalar
        def _(act):
            take_turned(act, u.xt, u, s, 0, chunks=(1,))
            norm_root(act, u, s, 0)
            take_turned(act, u.xt, u, s, 2, u.ln2g, u.ln2b)
            act.wait_ge(s.shifted, 1)
            act.activation(u.gexp[:, :, :], u.gexp[:, :, :], ACT.Exp).then_inc(s.exp_done, 1)
            take_turned(act, u.xt, u, s, 6)

        @block.vector
        def _(dve):
            link = dve_chain(dve, s.chain)
            for k in range(4):
                dve.wait_ge(s.pj_ready, k + 1)
                dve.tensor_tensor(pair(u.y, k), u.psum[:, 4 + k % 2, :], pair(u.x3, k), ALU.add).then_inc(s.y_done, 1)
                dve.wait_ge(s.y_done, k + 1)
                ins = norm_stats(dve, u.y, u, (2 * k, 2 * k + 1))
            link(ins)
            norm_variance(dve, link, u, s)
            norm_apply(dve, link, u.y, u.z, u, s, 0, half_ready=s.z_ready)
            dve.wait_ge(s.slots_gathered, 16 * TOPK * NT * (b + 1))
            link(dve.tensor_copy(u.token[:, :], u.next_token[:, :]))
            dve.tensor_scalar(u.next_token[:, :], u.next_token[:, :], float(T), None, ALU.add)
            dve.wait_ge(s.lg_ready, 1)
            lg, top = u.lg, u.top
            link(dve.tensor_copy(lg[:, :, :].rearrange("p t e -> p (t e)"), u.psum[:, 6, 0:NT * E_]))
            for t in range(NT):
                ins = dve.max(top[:, t, :], lg[:, t, :])
            link(ins)
            dve.tensor_tensor(u.gexp[:, :, :], lg[:, :, :], top[:, :, 0:1].broadcast_to([P, NT, E_]), ALU.subtract
                              ).then_inc(s.shifted, 1)
            for t in range(NT):
                ins = dve.max_index(u.topi[:, t, :], top[:, t, :], lg[:, t, :])
            link(ins)
            link(dve.tensor_copy(u.expert[:, :, :].rearrange("p k t -> p t k"), u.topi[:, :, 0:TOPK]))
            for k in range(TOPK):
                ins = dve.tensor_tensor(u.is_it[:, k, :, :], u.iota[:, :].unsqueeze(1).broadcast_to([P, NT, E_]),
                                        u.expert[:, k, :].unsqueeze(2).broadcast_to([P, NT, E_]), ALU.is_equal)
            link(ins)
            dve.tensor_tensor(u.chosen[:, :, :], u.is_it[:, 0, :, :], u.is_it[:, 1, :, :], ALU.add
                              ).then_inc(s.mask_ready, 1)
            dve.wait_ge(s.exp_done, 1)
            link(dve.tensor_reduce(u.gsum[:, :], u.gexp[:, :, :], AX.X, ALU.add))
            dve.reciprocal(u.gsum[:, :], u.gsum[:, :])
            for k in range(TOPK):
                ins = dve.tensor_tensor(u.pick[:, k, :, :], u.is_it[:, k, :, :], u.gexp[:, :, :], ALU.mult)
            link(ins)
            link(dve.tensor_reduce(u.gate[:, :, :], u.pick[:, :, :, :], AX.X, ALU.add))
            link(dve.tensor_tensor(u.gate[:, :, :], u.gate[:, :, :], u.gsum[:, :].unsqueeze(1).broadcast_to([P, TOPK, NT]),
                                   ALU.mult))
            dve.wait_ge(s.pos_ready, 1)
            pos = u.psum[:, 7, 0:NT * E_].rearrange("p (t e) -> p t e", e=E_)
            for k in range(TOPK):
                ins = dve.tensor_tensor(u.pick[:, k, :, :], u.is_it[:, k, :, :], pos, ALU.mult)
            link(ins)
            link(dve.tensor_reduce(u.place[:, :, :], u.pick[:, :, :, :], AX.X, ALU.add))
            link(dve.tensor_scalar(u.keep[:, :, :], u.place[:, :, :], float(CAP), None, ALU.is_le))
            link(dve.tensor_scalar(u.place[:, :, :], u.place[:, :, :], float(CAP), -1.0, ALU.min, ALU.add))
            link(dve.scalar_tensor_tensor(u.place[:, :, :], u.expert[:, :, :], float(CAP), u.place[:, :, :],
                                          ALU.mult, ALU.add))
            dve.tensor_copy(u.read_at[:, :, bass.ds(b * NT, NT)], u.place[:, :, :])
            dve.tensor_tensor(u.gates[:, :, bass.ds(b * NT, NT)], u.gate[:, :, :], u.keep[:, :, :], ALU.mult)
            link(dve.tensor_scalar(u.keep[:, :, :], u.keep[:, :, :], -DROPPED, DROPPED, ALU.mult, ALU.add))
            dve.tensor_tensor(u.write_at[:, :, :], u.place[:, :, :], u.keep[:, :, :], ALU.add)
            link(dve.tensor_reduce(u.count[:, :], u.chosen[:, :, :].rearrange("p t e -> p e t"), AX.X, ALU.add))
            link(dve.tensor_tensor(u.before[:, :], u.before[:, :], u.count[:, :], ALU.add))

        @block.gpsimd
        def _(pool):
            zero(pool, over)
            pool.wait_ge(s.y_done, 4)
            pool.tensor_tensor(u.x3[:, :, :], u.y[:, :, :], u.x3[:, :, :], ALU.add).then_inc(s.x4_ready, 1)



MOE_SEMS = ("sliced b1_sliced w0_in w1_in x0_gathered x1_gathered b2_in turned taken h_ready h_done y_ready y_done y0_out y1_out")


def load_expert(eng, e, j, u, w1_dram, w2_dram, sem):
    eng.dma_start(u.w1[j][:, :, :], w1_dram[bass.ds(e, 1), :, :].rearrange("o (c p) f -> p (o c) f", p=P)).then_inc(sem, 16)
    eng.dma_start(u.w2[j][:, :, :], w2_dram[bass.ds(e, 1), :, :].rearrange("o (n p) d -> p (o n) d", p=P)).then_inc(sem, 16)


def gather_tokens(pool, j, ids, u, z_dram, sem):
    for t in range(CT):
        pool.indirect_dma_start(
            out=u.xg[j][:, t, :], out_offset=None, in_=z_dram,
            in_offset=bass.IndirectOffsetOnAxis(ap=ids[:, t:t + 1], axis=0),
            bounds_check=N - 1, oob_is_err=True).then_inc(sem, 16)


def first_expert(nc, u, s, first, b1_dram, w1_dram, w2_dram, z_dram):
    with nc.Block() as block:
        @block.sync
        def _(sp):
            sp.dma_start(u.b1[:, :], b1_dram).then_inc(first, 16)
            load_expert(sp, 0, 0, u, w1_dram, w2_dram, first)
            sp.wait_ge(first, 48)

        @block.vector
        def _(dve):
            dve.tensor_copy(u.ids[:, 0:CT], u.slots[:, 0:CT]).then_inc(s.sliced, 1)

        @block.gpsimd
        def _(pool):
            pool.wait_ge(s.sliced, 1)
            gather_tokens(pool, 0, u.ids[:, 0:CT], u, z_dram, s.x0_gathered)

        @block.tensor
        def _(pe):
            pe.wait_ge(s.x0_gathered, 16 * CT)
            turn_tiles(pe, u.xg[0], u, s)

        @block.scalar
        def _(act):
            take_turned(act, u.xgt, u, s, 0, u.ln2g, u.ln2b)
    clear(nc, s)


def experts(nc, i, u, s, z_dram, w1_dram, w2_dram, b2_dram, y_dram):
    with nc.Block() as block:
        @block.sync
        def _(sp):
            load_expert(sp, 2 * i + 1, 1, u, w1_dram, w2_dram, s.w1_in)
            for j in range(2):
                sp.dma_start(u.b2b[j][:, :], b2_dram[bass.ds(2 * i + j, 1), :].partition_broadcast(P)
                             .rearrange("p o d -> p (o d)")).then_inc(s.b2_in, 16)
            for q in range(CT):
                if q == CT // 2:
                    sp.wait_ge(s.y_ready, CT // 2)
                    load_expert(sp, (2 * i + 2) % E_, 0, u, w1_dram, w2_dram, s.w0_in)
                sp.wait_ge(s.y_done, q + 1)
                sp.dma_start(y_dram[bass.ds(2 * CAP * i + 2 * P * q, 2 * P), :].rearrange("(t p) d -> p t d", p=P),
                             u.ye[q % 2][:, :, :]).then_inc((s.y0_out, s.y1_out)[q % 2], 16)
            sp.wait_ge(s.w0_in, 32)
            for q in range(2):
                sp.wait_ge((s.y0_out, s.y1_out)[q], 16 * CT // 2)

        @block.gpsimd
        def _(pool):
            pool.wait_ge(s.sliced, 1)
            gather_tokens(pool, 1, u.ids[:, 0:CT], u, z_dram, s.x1_gathered)
            gather_tokens(pool, 0, u.ids[:, CT:2 * CT], u, z_dram, s.x0_gathered)

        @block.tensor
        def _(pe):
            for j in range(2):
                if j:
                    pe.wait_ge(s.taken, 4)
                    pe.wait_ge(s.w1_in, 32)
                for n in range(NF):
                    for h in range(2):
                        k = 2 * n + h
                        if k >= 4:
                            pe.wait_ge(s.h_done, 16 * j + k - 3)
                        for c in range(NC):
                            ins = pe.matmul(u.psum[:, k % 4, :], u.w1[j][:, c, P * n:P * n + P],
                                            u.xgt[:, c, BANK * h:BANK * h + BANK], start=(c == 0), stop=(c == NC - 1))
                        ins.then_inc(s.h_ready, 1)
                pe.wait_ge(s.h_done, 16 * (j + 1))
                for k in range(CT // 2):
                    q = CT // 2 * j + k
                    if k == 1:
                        pe.wait_ge(s.x0_gathered if j else s.x1_gathered, 16 * CT * (i + 1 + j))
                        turn_tiles(pe, u.xg[1 - j], u, s)
                    if q >= 4:
                        pe.wait_ge(s.y_done, q - 3)
                    for t in range(2):
                        for n in range(NF):
                            ins = pe.matmul(u.psum[:, 4 + k, D * t:D * t + D],
                                            u.hid[:, n, P * (2 * k + t):P * (2 * k + t + 1)], u.w2[j][:, n, :],
                                            start=(n == 0), stop=(n == NF - 1))
                    ins.then_inc(s.y_ready, 1)

        @block.scalar
        def _(act):
            for j in range(2):
                if j == 0:
                    act.wait_ge(s.b1_sliced, 1)
                else:
                    act.wait_ge(s.y_ready, 4)
                for n in range(NF):
                    for h in range(2):
                        k = 2 * n + h
                        act.wait_ge(s.h_ready, 16 * j + k + 1)
                        act.activation(u.hid[:, n, BANK * h:BANK * h + BANK], u.psum[:, k % 4, :], ACT.Gelu,
                                       bias=u.b1s[:, j * NF + n:j * NF + n + 1]).then_inc(s.h_done, 1)
                take_turned(act, u.xgt, u, s, 4 * j, u.ln2g, u.ln2b)

        @block.vector
        def _(dve):
            dve.tensor_copy(u.b1s[:, :], u.b1[:, bass.ds(2 * NF * i, 2 * NF)]).then_inc(s.b1_sliced, 1)
            dve.tensor_copy(u.ids[:, :], u.slots[:, bass.ds(CT * (2 * i + 1), 2 * CT)]).then_inc(s.sliced, 1)
            dve.wait_ge(s.b2_in, 32)
            for q in range(CT):
                j, k = divmod(q, CT // 2)
                dve.wait_ge(s.y_ready, q + 1)
                if q >= 2:
                    dve.wait_ge((s.y0_out, s.y1_out)[q % 2], 16 * (q // 2))
                dve.tensor_tensor(u.ye[q % 2][:, :, :], u.psum[:, 4 + k, :].rearrange("p (t d) -> p t d", t=2),
                                  u.b2b[j][:, :].unsqueeze(1).broadcast_to([P, 2, D]), ALU.add).then_inc(s.y_done, 1)
    clear(nc, s)



COMBINE_SEMS = "sliced x4_in sum_done out_ready out_done " + " ".join(f"r{n}_gathered" for n in range(2 * NT)) + NORM_SEMS


def combine(nc, i, u, s, x4_dram, y_dram, out_dram):
    gathered = [h for n, h in s._asdict().items() if n.endswith("_gathered")]
    with nc.Block() as block:
        @block.gpsimd
        def _(pool):
            pool.wait_ge(s.sliced, 1)
            for j in range(2):
                for t in range(NT):
                    for k in range(TOPK):
                        pool.indirect_dma_start(
                            out=u.rows[j][:, TOPK * t + k, :], out_offset=None, in_=y_dram,
                            in_offset=bass.IndirectOffsetOnAxis(ap=u.at[:, k, NT * j + t:NT * j + t + 1], axis=0),
                            bounds_check=E_ * CAP - 1, oob_is_err=True).then_inc(gathered[NT * j + t], 16)

        @block.scalar
        def _(act):
            norm_root(act, u, s, 0)
            norm_root(act, u, s, 1)

        @block.vector
        def _(dve):
            link = dve_chain(dve, s.chain)
            dve.tensor_copy(u.at[:, :, :], u.read_at[:, :, bass.ds(2 * i * NT, 2 * NT)]).then_inc(s.sliced, 1)
            link(dve.tensor_copy(u.gate_pair[:, :, :], u.gates[:, :, bass.ds(2 * i * NT, 2 * NT)]))
            dve.wait_ge(s.x4_in, 32)
            for j in range(2):
                y = u.sums[j]
                for t in range(NT):
                    dve.wait_ge(gathered[NT * j + t], 16 * TOPK * (i + 1))
                    for k in range(TOPK):
                        dve.scalar_tensor_tensor(y[:, t, :], u.rows[j][:, TOPK * t + k, :],
                                                 u.gate_pair[:, k, NT * j + t:NT * j + t + 1],
                                                 y[:, t, :], ALU.mult, ALU.add).then_inc(s.sum_done, 1)
                        dve.wait_ge(s.sum_done, TOPK * (NT * j + t) + k + 1)
                    ins = norm_stats(dve, y, u, (t,))
                link(ins)
                norm_variance(dve, link, u, s)
                norm_apply(dve, link, y, y, u, s, j, half_ready=s.out_ready)

        @block.sync
        def _(sp):
            for j in range(2):
                sp.dma_start(u.sums[j][:, :, :], x4_dram[bass.ds((2 * i + j) * T, T), :].rearrange("(t p) d -> p t d", p=P)
                             ).then_inc(s.x4_in, 16)
            for j in range(2):
                for h in range(2):
                    sp.wait_ge(s.out_ready, 2 * j + h + 1)
                    sp.dma_start(out_dram[bass.ds(2 * i + j, 1), BANK * h:BANK * h + BANK, :]
                                 .rearrange("o (t p) d -> p (o t) d", p=P), u.sums[j][:, 4 * h:4 * h + 4, :]
                                 ).then_inc(s.out_done, 16)
            sp.wait_ge(s.out_done, 64)
    clear(nc, s)



def lasting_buffers(nc, ctx, u):
    for name, shape, dtype in (
            ("y", [P, NT, D], F32), ("id32", [P, P], F32),
            ("gates", [P, TOPK, B * NT], F32), ("read_at", [P, TOPK, B * NT], U32), ("gate", [P, TOPK, NT], F32),
            ("bn", [P, NT, 6], F32), ("mv", [P, NT, 2], F32), ("var", [P, NT], F32), ("lnv", [P, NT], F32),
            ("root", [P, NT], F32), ("nt", [P, NT], F32), ("rstd", [P, NT], F32),
            ("ln2g", [P, NC], F32), ("ln2b", [P, NC], F32)):
        sbuf(nc, ctx, u, name, shape, dtype)
    u["psum"] = ctx.enter_context(nc.psum_tensor("b_psum", [P, 8, BANK], F32))


def layer_buffers(nc, ctx, u):
    for name in "wout wr wk0 wv0 wq1 wk1 wv1 wo1 wproj".split():
        sbuf(nc, ctx, u, name, [P, NC, D])
    sbuf(nc, ctx, u, "wqkv0", [P, NC, NG, 192])
    sbuf(nc, ctx, u, "wqkv1", [P, NC, NG, 192])
    sbuf(nc, ctx, u, "wgate", [P, NC, E_])
    for name in "mur muk bq bq_plus ln1g ln1b".split():
        sbuf(nc, ctx, u, name, [P, NC])
    sbuf(nc, ctx, u, "one", [P, 1])
    for name in "bk bv bo".split():
        sbuf(nc, ctx, u, name, [P, D])
    sbuf(nc, ctx, u, "rft", [64, P])
    sbuf(nc, ctx, u, "blocks", [P, P])
    sbuf(nc, ctx, u, "bg", [P, P])
    sbuf(nc, ctx, u, "kvm", [P, NC, P])
    sbuf(nc, ctx, u, "mt", [P, NC, P])
    sbuf(nc, ctx, u, "am", [P, NC, D])
    sbuf(nc, ctx, u, "x3", [P, NT, D])
    for name, shape, dtype in (
            ("lg", [P, NT, E_], F32), ("top", [P, NT, 8], F32), ("topi", [P, NT, 8], U32), ("gexp", [P, NT, E_], F32),
            ("expert", [P, TOPK, NT], F32), ("is_it", [P, TOPK, NT, E_], F32), ("pick", [P, TOPK, NT, E_], F32),
            ("place", [P, TOPK, NT], F32), ("keep", [P, TOPK, NT], F32), ("write_at", [P, TOPK, NT], U32),
            ("gsum", [P, NT], F32), ("count", [P, E_], F32), ("chosen", [P, NT, E_], BF16), ("before", [P, E_], BF16),
            ("token", [P, NT], U32), ("next_token", [P, NT], U32), ("iota", [P, E_], F32), ("upto", [P, P], BF16), ("ones16", [P, P], BF16),
            ("no_token", [E_ * CAP // P, P], U32)):
        sbuf(nc, ctx, u, name, shape, dtype)
    def part(i, j):
        return u["probs"][i][:, 2 * j:2 * j + 2, :]

    def tiles(x):
        return x.rearrange("p a (t d) -> p (a t) d", d=D)
    flat = u["probs"][0][:, :, :].rearrange("p h t -> p (h t)")
    u["x1t"] = flat[:, 0:NC * (T + 1)].rearrange("p (c t) -> p c t", c=NC)
    u["xk"], u["xr"] = part(1, 0), part(1, 1)
    u["r"] = u["o"]
    u["dx"] = u["xt"]
    u["z"] = tiles(part(0, 0))
    u["qexp"], u["phq"], u["kx"] = part(0, 0), part(0, 1), tiles(part(1, 0))


LATER_WEIGHTS = "wout wr wk0 wv0 wq1 wk1 wv1 wo1 wproj wqkv1".split()


def set_up(nc, ctx, made, a, slots_dram, later):
    u = named(made)
    loaded = ctx.enter_context(nc.semaphore("weights_in"))
    s = semaphores(nc, ctx, "first", "turned taken")
    zeroed = ctx.enter_context(nc.semaphore("zeroed"))
    fixed = ctx.enter_context(nc.semaphore("fixed"))
    gram = ctx.enter_context(nc.semaphore("gram_ready"))
    names = "wqkv0 cos sin id32 blocks iota next_token mur muk bq ln1g ln1b ln2g ln2b wgate".split()
    count = len(names) + 5 + P // HD
    bf16_tables = (u.id16[:, :], u.mask_q[:, :, :], u.mask_k[:, :, :], u.causal_q[:, :], u.causal_k[:, :], u.upto[:, :])
    width = [P, 2 * WQ, 2 * WQ, P, P, P]
    tables = u.y[:, :, :].rearrange("p t d -> p (t d)")[:, 0:sum(width)]
    with nc.Block() as block:
        @block.sync
        def _(sp):
            sp.dma_start(u.src[:, :, :], a["x"][0:1, :, :].rearrange("o (t p) d -> p (o t) d", p=P)).then_inc(loaded, 16)
            for n in names:
                sp.dma_start(made[n][:], a[n]).then_inc(loaded, 16)
            sp.dma_start(tables, a["tables"]).then_inc(loaded, 16)
            for n in ("bk", "bv", "bo"):
                sp.dma_start(made[n][:, :], a[n].partition_broadcast(P).rearrange("p o d -> p (o d)")).then_inc(loaded, 16)
            for j in range(P // HD):
                sp.dma_start(u.rft[:, HD * j:HD * j + HD], a["rft"]).then_inc(loaded, 16)
            sp.wait_ge(zeroed, 1)
            sp.dma_start(slots_dram.rearrange("(r p) o -> r (p o)", p=P), u.no_token[:, :]).then_inc(loaded, 16)
            sp.wait_ge(loaded, 16 * (count + 1))
            for n in LATER_WEIGHTS:
                sp.dma_start(made[n][:], a[n]).then_inc(later, 16)

        @block.vector
        def _(dve):
            dve.memset(u.no_token[:, :], 0).then_inc(zeroed, 1)
            for i in range(3):
                dve.memset(u.v[i][:, :, :, HD:32], 1.0)
            dve.memset(u.before[:, :], 0.0)
            dve.memset(u.one[:, :], 1.0)
            dve.memset(u.ones16[:, :], 1.0)
            dve.wait_ge(loaded, 16 * (count + 1))
            for i, t in enumerate(bf16_tables):
                part = tables[:, sum(width[:i]):sum(width[:i + 1])]
                dve.tensor_copy(t, part if width[i] == P else part.rearrange("p (h w) -> p h w", h=2))
            dve.tensor_copy(u.token[:, :], u.next_token[:, :])
            for k in range(TOPK):
                dve.tensor_scalar(u.write_at[:, k, :], u.next_token[:, :], float(T * k), None, ALU.add)
            dve.tensor_scalar(u.bq_plus[:, :], u.bq[:, :], 1.0, None, ALU.add).then_inc(fixed, 1)
            dve.wait_ge(gram, 1)
            dve.tensor_tensor(u.bg[:, :], u.psum[:, 4, 0:P], u.blocks[:, :], ALU.mult).then_inc(fixed, 1)

        @block.gpsimd
        def _(pool):
            for i in range(3):
                pool.memset(u.qk[i][KS:KS + 32, HG:2 * HG, :], 1.0)

        @block.tensor
        def _(pe):
            pe.wait_ge(loaded, 16 * (count + 1))
            pe.matmul(u.psum[:, 4, 0:P], u.rft[:, :], u.rft[:, :], start=True, stop=True).then_inc(gram, 1)
            turn_tiles(pe, u.src, u, s)

        @block.scalar
        def _(act):
            take_turned(act, u.xt, u, s, 0)


def table_of_slots(nc, ctx, u, slots_dram):
    s = semaphores(nc, ctx, "table", "read floats turned taken")
    with nc.Block() as block:
        @block.sync
        def _(sp):
            sp.dma_start(u.slot_rows[:, :], slots_dram.rearrange("(r p) o -> r (p o)", p=P)).then_inc(s.read, 16)

        @block.vector
        def _(dve):
            dve.wait_ge(s.read, 16)
            dve.tensor_copy(u.slot_floats[:, :], u.slot_rows[:, :]).then_inc(s.floats, 1)
            dve.wait_ge(s.turned, 1)
            dve.tensor_copy(u.slots[:, 0:E_ * CT], u.psum[:, 0, 0:E_ * CT])
            dve.tensor_copy(u.slots[:, E_ * CT:], u.psum[:, 0, 0:CT]).then_inc(s.taken, 1)

        @block.tensor
        def _(pe):
            pe.wait_ge(s.floats, 1)
            pe.transpose(u.psum[:, 0, 0:E_ * CT], u.slot_floats[:, :], u.id32[0:E_ * CT, 0:E_ * CT]).then_inc(s.turned, 1)


def two_layers(nc, a, out):
    slots_dram = nc.dram_tensor("slots", (E_ * CAP, 1), U32, kind="Internal").ap()
    z_dram = nc.dram_tensor("normed", (N, D), F32, kind="Internal").ap()
    x4_dram = nc.dram_tensor("before_last_norm", (N, D), F32, kind="Internal").ap()
    y_dram = nc.dram_tensor("expert_rows", (E_ * CAP, D), F32, kind="Internal").ap()
    with ExitStack() as ctx:
        lasting = {}
        lasting_buffers(nc, ctx, lasting)
        att = semaphores(nc, ctx, "att", ATT_SEMS)
        mix = semaphores(nc, ctx, "mix", POST0_SEMS)
        lin = semaphores(nc, ctx, "lin", LIN_SEMS)
        rt = semaphores(nc, ctx, "route", ROUTE_SEMS)
        moe = semaphores(nc, ctx, "moe", MOE_SEMS)
        comb = semaphores(nc, ctx, "comb", COMBINE_SEMS)
        nc.scalar.preload_act_table_set("natural_log_exp_and_others")
        with ExitStack() as layer:
            made = dict(lasting)
            attention_buffers(nc, layer, made)
            layer_buffers(nc, layer, made)
            later = ctx.enter_context(nc.semaphore("later_weights_in"))
            set_up(nc, ctx, made, a, slots_dram, later)
            u = named(made)
            with nc.Fori(0, B) as b:
                attention(nc, u, att, rt, True, later)
                mixing(nc, u, mix, att, slots_dram, rt.slots_gathered)
                linear_attention(nc, u, lin, mix)
                attention(nc, u, att, lin, False, later)
                route(nc, b, u, rt, att, a["x"], z_dram, x4_dram)
            with nc.Block() as block:
                @block.gpsimd
                def _(pool):
                    scatter_slots(pool, u, slots_dram, rt.slots_gathered)
                    pool.wait_ge(rt.slots_gathered, 16 * TOPK * NT * (B + 1))
        with ExitStack() as layer:
            made = dict(lasting)
            for i in range(2):
                sbuf(nc, layer, made, f"w1{i}", [P, NC, F_])
                sbuf(nc, layer, made, f"w2{i}", [P, NF, D])
                sbuf(nc, layer, made, f"xg{i}", [P, CT, D])
                sbuf(nc, layer, made, f"ye{i}", [P, 2, D])
                sbuf(nc, layer, made, f"b2b{i}", [P, D])
            for n in ("w1", "w2", "xg", "ye", "b2b"):
                made[n] = [made[n + "0"], made[n + "1"]]
            sbuf(nc, layer, made, "xgt", [P, NC, CAP])
            sbuf(nc, layer, made, "hid", [P, NF, CAP])
            sbuf(nc, layer, made, "slot_rows", [E_ * CT, P], U32)
            sbuf(nc, layer, made, "slot_floats", [E_ * CT, P])
            sbuf(nc, layer, made, "slots", [P, (E_ + 1) * CT], U32)
            sbuf(nc, layer, made, "ids", [P, 2 * CT], U32)
            sbuf(nc, layer, made, "b1", [P, E_ * NF])
            sbuf(nc, layer, made, "b1s", [P, 2 * NF])
            sbuf(nc, layer, made, "at", [P, TOPK, 2 * NT], U32)
            sbuf(nc, layer, made, "gate_pair", [P, TOPK, 2 * NT])
            made["rows"] = [layer.enter_context(nc.sbuf_tensor(f"b_rows{i}", [P, TOPK * NT, D], F32)) for i in range(2)]
            made["sums"] = [made["y"], layer.enter_context(nc.sbuf_tensor("b_sums1", [P, NT, D], F32))]
            u = named(made)
            first = layer.enter_context(nc.semaphore("first_expert_in"))
            table_of_slots(nc, ctx, u, slots_dram)
            first_expert(nc, u, moe, first, a["b1"], a["W1"], a["W2"], z_dram)
            with nc.Fori(0, E_ // 2) as i:
                experts(nc, i, u, moe, z_dram, a["W1"], a["W2"], a["b2"], y_dram)
            with nc.Fori(0, B // 2) as i:
                combine(nc, i, u, comb, x4_dram, y_dram, out)



def kernel(**inputs):
    import concourse.bacc as bacc
    from concourse.bass_utils import run_bass_kernel_spmd as run

    x = {k: np.asarray(v) for k, v in inputs.items()}

    def rows(w):
        return np.ascontiguousarray(w.reshape(NC, P, -1).transpose(1, 0, 2))

    def cols(v):
        return np.ascontiguousarray(v.reshape(-1, P).T)

    def grouped(w):
        return np.ascontiguousarray(w.reshape(NC, P, 3, NG, HG * HD).transpose(1, 0, 3, 2, 4).reshape(P, NC, NG, 192))

    by_head = x["L1_ffn_Wqkv"].reshape(D, H, 3, HD).transpose(0, 2, 1, 3)
    arrays = {
        "x": x["L0_attn_x"],
        "wqkv0": grouped(x["L0_attn_w_qkv"].T.reshape(D, 3, H, HD)),
        "wout": rows(x["L0_attn_w_out"].T), "wr": rows(x["L0_ffn_W_r"].T), "wk0": rows(x["L0_ffn_W_k"].T),
        "wv0": rows(x["L0_ffn_W_v"].T), "mur": cols(x["L0_ffn_mu_r"]), "muk": cols(x["L0_ffn_mu_k"]),
        "wq1": rows(x["L1_attn_Wq"]), "wk1": rows(x["L1_attn_Wk"]), "wv1": rows(x["L1_attn_Wv"]),
        "wo1": rows(x["L1_attn_Wo"]), "bq": cols(x["L1_attn_bq"]), "bk": x["L1_attn_bk"][None],
        "bv": x["L1_attn_bv"][None], "bo": x["L1_attn_bo"][None],
        "rft": np.ascontiguousarray(x["L1_attn_random_features"].T),
        "ln1g": cols(x["L1_ffn_ln1_g"]), "ln1b": cols(x["L1_ffn_ln1_b"]),
        "ln2g": cols(x["L1_ffn_ln2_g"]), "ln2b": cols(x["L1_ffn_ln2_b"]),
        "wqkv1": grouped(by_head), "wproj": rows(x["L1_ffn_Wproj"]), "wgate": rows(x["L1_ffn_Wgate"]),
        "W1": x["L1_ffn_W1"], "b1": cols(x["L1_ffn_b1"]), "W2": x["L1_ffn_W2"], "b2": x["L1_ffn_b2"],
    }
    for name, table in constants().items():
        arrays[name[2:]] = table
    nc = bacc.Bacc("TRN2", target_bir_lowering=False, num_devices=1)
    sent, a = {}, {}
    for name, v in arrays.items():
        sent["in_" + name] = np.ascontiguousarray(v)
        a[name] = nc.dram_tensor("in_" + name, v.shape, mybir.dt.from_np(v.dtype), kind="ExternalInput").ap()
    out = nc.dram_tensor("out", (B, T, D), F32, kind="ExternalOutput").ap()
    two_layers(nc, a, out)
    return run(nc, [sent], core_ids=[0]).results[0]["out"]
```
